# Optimizing a Trainium2 kernel written in Bass

```python
import numpy as np
import jax
import jax.numpy as jnp

def _softmax(x, axis=-1):
    return jax.nn.softmax(x, axis=axis)
def _gelu(x):
    return jax.nn.gelu(x, approximate=True)
def _silu(x):
    return jax.nn.silu(x)
def _sigmoid(x):
    return jax.nn.sigmoid(x)
def _layernorm(x, axis=-1, eps=1e-5):
    m = jnp.mean(x, axis=axis, keepdims=True)
    v = jnp.var(x, axis=axis, keepdims=True)
    return (x - m) / jnp.sqrt(v + eps)
def _scatter_add(tgt, idx, src, axis=0):
    return tgt.at[idx].add(src)
def _segment_sum(src, seg, n):
    return jax.ops.segment_sum(src, seg, n)

kernel_name = 'mk_conv_seq_d2_conv_nchw128_9ff37a'

def setup_inputs(seed: int = 0):
    np.random.seed(seed)
    _w = jnp.asarray
    def _rec_inputs():
        import jax
        import jax.numpy as jnp
        _gk = jax.random.key(seed)
        x = -0.0002023 + 1 * jax.random.normal(jax.random.fold_in(_gk, 1), (16, 128, 56, 56), jnp.float32)
        return x
    x = _rec_inputs()
    def _L0_conv_setup():
        import jax, jax.numpy as jnp
        import numpy as np
        B, C, H, W = (16, 128, 56, 56)
        QK, HEADS, NWIN, TOPK, MLPR = (128, 4, 7, 4, 3)
        HD_Q, HD_V = (QK // HEADS, C // HEADS)
        WH, WW = (H // NWIN, W // NWIN)
        P2, W2 = (NWIN * NWIN, WH * WW)
        SCALE = QK ** (-0.5)

        def _dwconv(x, w, b):
            y = jax.lax.conv_general_dilated(x, w, (1, 1), 'SAME', feature_group_count=x.shape[1], dimension_numbers=('NCHW', 'OIHW', 'NCHW'))
            return y + b[None, :, None, None]

        def _ln(x, g, b):
            m = x.mean(-1, keepdims=True)
            v = ((x - m) ** 2).mean(-1, keepdims=True)
            return (x - m) * jax.lax.rsqrt(v + 1e-06) * g + b

        def _win(t):
            b, _, _, c = t.shape
            return t.reshape(b, NWIN, WH, NWIN, WW, c).transpose(0, 1, 3, 2, 4, 5).reshape(b, P2, WH, WW, c)

        def _unwin(t):
            b, c = (t.shape[0], t.shape[-1])
            return t.reshape(b, NWIN, NWIN, WH, WW, c).transpose(0, 1, 3, 2, 4, 5).reshape(b, H, W, c)
        key = jax.random.key(seed)
        ks = jax.random.split(key, 8)
        p = lambda k, sh: (0.02 * jax.random.normal(k, sh)).astype(jnp.float32)
        return {'x': jax.random.normal(ks[0], (B, C, H, W), dtype=jnp.float32), 'pos_w': p(ks[1], (C, 1, 3, 3)), 'pos_b': jnp.zeros((C,), jnp.float32), 'ln1_g': jnp.ones((C,), jnp.float32), 'ln1_b': jnp.zeros((C,), jnp.float32), 'qkv_w': p(ks[2], (C, 2 * QK + C)), 'qkv_b': jnp.zeros((2 * QK + C,), jnp.float32), 'lepe_w': p(ks[3], (C, 1, 5, 5)), 'lepe_b': jnp.zeros((C,), jnp.float32), 'wo_w': p(ks[4], (C, C)), 'wo_b': jnp.zeros((C,), jnp.float32), 'ln2_g': jnp.ones((C,), jnp.float32), 'ln2_b': jnp.zeros((C,), jnp.float32), 'mlp_w1': p(ks[5], (C, MLPR * C)), 'mlp_b1': jnp.zeros((MLPR * C,), jnp.float32), 'mlp_w2': p(ks[6], (MLPR * C, C)), 'mlp_b2': jnp.zeros((C,), jnp.float32)}
    _L0_conv_all = _L0_conv_setup()
    _L0_conv_in = {k: v for k, v in _L0_conv_all.items() if k in ('pos_w', 'pos_b', 'ln1_g', 'ln1_b', 'qkv_w', 'qkv_b', 'lepe_w', 'lepe_b', 'wo_w', 'wo_b', 'ln2_g', 'ln2_b', 'mlp_w1', 'mlp_b1', 'mlp_w2', 'mlp_b2', )}
    del _L0_conv_all

    def _L1_conv_setup():
        import jax, jax.numpy as jnp
        import numpy as np
        TOKEN_NUM = 8
        GCN = 16
        D_INNER = 32
        D_STATE = 16
        D_CONV = 4
        DT_RANK = 1
        GROUPS = 4
        EPS = 1e-05

        def _mamba(seq, in_proj_w, conv1d_w, conv1d_b, x_proj_w, dt_proj_w, dt_proj_b, A_log, D, out_proj_w):
            xz = jnp.einsum('nld,ed->nle', seq, in_proj_w)
            xi, z = jnp.split(xz, 2, axis=-1)
            xc = jax.lax.conv_general_dilated(xi.transpose(0, 2, 1), conv1d_w, (1,), ((D_CONV - 1, 0),), dimension_numbers=('NCH', 'OIH', 'NCH'), feature_group_count=D_INNER)
            xc = jax.nn.silu((xc + conv1d_b[None, :, None]).transpose(0, 2, 1))
            xdbl = jnp.einsum('nld,ed->nle', xc, x_proj_w)
            dt, Bm, Cm = jnp.split(xdbl, [DT_RANK, DT_RANK + D_STATE], axis=-1)
            dt = jax.nn.softplus(jnp.einsum('nlr,dr->nld', dt, dt_proj_w) + dt_proj_b)
            A = -jnp.exp(A_log)
            dA = jnp.exp(dt[..., None] * A)
            dBx = dt[..., None] * Bm[:, :, None, :] * xc[..., None]

            def step(h, inp):
                a, b, c = inp
                h = a * h + b
                return (h, jnp.sum(h * c[:, None, :], axis=-1))
            h0 = jnp.zeros((seq.shape[0], D_INNER, D_STATE), dA.dtype)
            _, ys = jax.lax.scan(step, h0, (dA.transpose(1, 0, 2, 3), dBx.transpose(1, 0, 2, 3), Cm.transpose(1, 0, 2)))
            ym = ys.transpose(1, 0, 2) + D * xc
            ym = ym * jax.nn.silu(z)
            return jnp.einsum('nld,ed->nle', ym, out_proj_w)
        key = jax.random.key(seed)
        ks = jax.random.split(key, 8)
        g = lambda k, shape, scale: jax.random.normal(k, shape, jnp.float32) * scale
        d = {}
        d['x'] = jax.random.normal(ks[0], (2, 128, 128, 128), jnp.float32)
        d['conv_w'] = g(ks[1], (128, 128, 3, 3), 0.03)
        d['conv_b'] = jnp.zeros((128,), jnp.float32)
        d['gn_w'] = jnp.ones((128,), jnp.float32)
        d['gn_b'] = jnp.zeros((128,), jnp.float32)
        d['in_proj_w'] = g(ks[2], (2 * D_INNER, GCN), 0.25)
        d['conv1d_w'] = g(ks[3], (D_INNER, 1, D_CONV), 0.3)
        d['conv1d_b'] = jnp.zeros((D_INNER,), jnp.float32)
        d['x_proj_w'] = g(ks[4], (DT_RANK + 2 * D_STATE, D_INNER), 0.18)
        d['dt_proj_w'] = g(ks[5], (D_INNER, DT_RANK), 1.0)
        d['dt_proj_b'] = jnp.full((D_INNER,), -2.0, jnp.float32)
        d['A_log'] = jnp.tile(jnp.log(jnp.arange(1, D_STATE + 1, dtype=jnp.float32)), (D_INNER, 1))
        d['D'] = jnp.ones((D_INNER,), jnp.float32)
        d['out_proj_w'] = g(ks[6], (GCN, D_INNER), 0.18)
        return d
    _L1_conv_all = _L1_conv_setup()
    _L1_conv_in = {k: v for k, v in _L1_conv_all.items() if k in ('conv_w', 'conv_b', 'gn_w', 'gn_b', 'in_proj_w', 'conv1d_w', 'conv1d_b', 'x_proj_w', 'dt_proj_w', 'dt_proj_b', 'A_log', 'D', 'out_proj_w', )}
    del _L1_conv_all

    return {
        "x": x,
        "L0_conv_pos_w": _L0_conv_in["pos_w"],
        "L0_conv_pos_b": _L0_conv_in["pos_b"],
        "L0_conv_ln1_g": _L0_conv_in["ln1_g"],
        "L0_conv_ln1_b": _L0_conv_in["ln1_b"],
        "L0_conv_qkv_w": _L0_conv_in["qkv_w"],
        "L0_conv_qkv_b": _L0_conv_in["qkv_b"],
        "L0_conv_lepe_w": _L0_conv_in["lepe_w"],
        "L0_conv_lepe_b": _L0_conv_in["lepe_b"],
        "L0_conv_wo_w": _L0_conv_in["wo_w"],
        "L0_conv_wo_b": _L0_conv_in["wo_b"],
        "L0_conv_ln2_g": _L0_conv_in["ln2_g"],
        "L0_conv_ln2_b": _L0_conv_in["ln2_b"],
        "L0_conv_mlp_w1": _L0_conv_in["mlp_w1"],
        "L0_conv_mlp_b1": _L0_conv_in["mlp_b1"],
        "L0_conv_mlp_w2": _L0_conv_in["mlp_w2"],
        "L0_conv_mlp_b2": _L0_conv_in["mlp_b2"],
        "L1_conv_conv_w": _L1_conv_in["conv_w"],
        "L1_conv_conv_b": _L1_conv_in["conv_b"],
        "L1_conv_gn_w": _L1_conv_in["gn_w"],
        "L1_conv_gn_b": _L1_conv_in["gn_b"],
        "L1_conv_in_proj_w": _L1_conv_in["in_proj_w"],
        "L1_conv_conv1d_w": _L1_conv_in["conv1d_w"],
        "L1_conv_conv1d_b": _L1_conv_in["conv1d_b"],
        "L1_conv_x_proj_w": _L1_conv_in["x_proj_w"],
        "L1_conv_dt_proj_w": _L1_conv_in["dt_proj_w"],
        "L1_conv_dt_proj_b": _L1_conv_in["dt_proj_b"],
        "L1_conv_A_log": _L1_conv_in["A_log"],
        "L1_conv_D": _L1_conv_in["D"],
        "L1_conv_out_proj_w": _L1_conv_in["out_proj_w"],
    }

def reference(x, L0_conv_pos_w, L0_conv_pos_b, L0_conv_ln1_g, L0_conv_ln1_b, L0_conv_qkv_w, L0_conv_qkv_b, L0_conv_lepe_w, L0_conv_lepe_b, L0_conv_wo_w, L0_conv_wo_b, L0_conv_ln2_g, L0_conv_ln2_b, L0_conv_mlp_w1, L0_conv_mlp_b1, L0_conv_mlp_w2, L0_conv_mlp_b2, L1_conv_conv_w, L1_conv_conv_b, L1_conv_gn_w, L1_conv_gn_b, L1_conv_in_proj_w, L1_conv_conv1d_w, L1_conv_conv1d_b, L1_conv_x_proj_w, L1_conv_dt_proj_w, L1_conv_dt_proj_b, L1_conv_A_log, L1_conv_D, L1_conv_out_proj_w):
    import jax
    import jax.numpy as jnp
    def _L0_conv_ref(x, pos_w, pos_b, ln1_g, ln1_b, qkv_w, qkv_b, lepe_w, lepe_b, wo_w, wo_b, ln2_g, ln2_b, mlp_w1, mlp_b1, mlp_w2, mlp_b2):
        import jax, jax.numpy as jnp
        import numpy as np
        B, C, H, W = (16, 128, 56, 56)
        QK, HEADS, NWIN, TOPK, MLPR = (128, 4, 7, 4, 3)
        HD_Q, HD_V = (QK // HEADS, C // HEADS)
        WH, WW = (H // NWIN, W // NWIN)
        P2, W2 = (NWIN * NWIN, WH * WW)
        SCALE = QK ** (-0.5)

        def _dwconv(x, w, b):
            y = jax.lax.conv_general_dilated(x, w, (1, 1), 'SAME', feature_group_count=x.shape[1], dimension_numbers=('NCHW', 'OIHW', 'NCHW'))
            return y + b[None, :, None, None]

        def _ln(x, g, b):
            m = x.mean(-1, keepdims=True)
            v = ((x - m) ** 2).mean(-1, keepdims=True)
            return (x - m) * jax.lax.rsqrt(v + 1e-06) * g + b

        def _win(t):
            b, _, _, c = t.shape
            return t.reshape(b, NWIN, WH, NWIN, WW, c).transpose(0, 1, 3, 2, 4, 5).reshape(b, P2, WH, WW, c)

        def _unwin(t):
            b, c = (t.shape[0], t.shape[-1])
            return t.reshape(b, NWIN, NWIN, WH, WW, c).transpose(0, 1, 3, 2, 4, 5).reshape(b, H, W, c)
        x = x + _dwconv(x, pos_w, pos_b)
        xh = x.transpose(0, 2, 3, 1)
        y = _ln(xh, ln1_g, ln1_b)
        qkv = y @ qkv_w + qkv_b
        q, kv = (qkv[..., :QK], qkv[..., QK:])
        qw, kvw = (_win(q), _win(kv))
        q_win = jax.lax.stop_gradient(qw.mean((2, 3)))
        k_win = jax.lax.stop_gradient(kvw[..., :QK].mean((2, 3)))
        logits = jnp.einsum('bpc,bqc->bpq', q_win * SCALE, k_win)
        _, idx = jax.lax.top_k(logits, TOPK)
        kv_pix = kvw.reshape(B, P2, W2, QK + C)
        kv_sel = jax.vmap(lambda t, i: t[i])(kv_pix, idx)
        k_sel = kv_sel[..., :QK].reshape(B, P2, TOPK * W2, HEADS, HD_Q)
        v_sel = kv_sel[..., QK:].reshape(B, P2, TOPK * W2, HEADS, HD_V)
        q_pix = qw.reshape(B, P2, W2, HEADS, HD_Q)
        att = jnp.einsum('bpqhd,bpkhd->bphqk', q_pix * SCALE, k_sel)
        att = jax.nn.softmax(att, axis=-1)
        o = jnp.einsum('bphqk,bpkhd->bpqhd', att, v_sel).reshape(B, P2, W2, C)
        o = _unwin(o)
        v_img = kv[..., QK:].transpose(0, 3, 1, 2)
        lepe = _dwconv(v_img, lepe_w, lepe_b).transpose(0, 2, 3, 1)
        o = (o + lepe) @ wo_w + wo_b
        xh = xh + o
        z = _ln(xh, ln2_g, ln2_b)
        z = jax.nn.gelu(z @ mlp_w1 + mlp_b1, approximate=False) @ mlp_w2 + mlp_b2
        xh = xh + z
        return xh.transpose(0, 3, 1, 2)

    def _L1_conv_ref(x, conv_w, conv_b, gn_w, gn_b, in_proj_w, conv1d_w, conv1d_b, x_proj_w, dt_proj_w, dt_proj_b, A_log, D, out_proj_w):
        import jax, jax.numpy as jnp
        import numpy as np
        TOKEN_NUM = 8
        GCN = 16
        D_INNER = 32
        D_STATE = 16
        D_CONV = 4
        DT_RANK = 1
        GROUPS = 4
        EPS = 1e-05

        def _mamba(seq, in_proj_w, conv1d_w, conv1d_b, x_proj_w, dt_proj_w, dt_proj_b, A_log, D, out_proj_w):
            xz = jnp.einsum('nld,ed->nle', seq, in_proj_w)
            xi, z = jnp.split(xz, 2, axis=-1)
            xc = jax.lax.conv_general_dilated(xi.transpose(0, 2, 1), conv1d_w, (1,), ((D_CONV - 1, 0),), dimension_numbers=('NCH', 'OIH', 'NCH'), feature_group_count=D_INNER)
            xc = jax.nn.silu((xc + conv1d_b[None, :, None]).transpose(0, 2, 1))
            xdbl = jnp.einsum('nld,ed->nle', xc, x_proj_w)
            dt, Bm, Cm = jnp.split(xdbl, [DT_RANK, DT_RANK + D_STATE], axis=-1)
            dt = jax.nn.softplus(jnp.einsum('nlr,dr->nld', dt, dt_proj_w) + dt_proj_b)
            A = -jnp.exp(A_log)
            dA = jnp.exp(dt[..., None] * A)
            dBx = dt[..., None] * Bm[:, :, None, :] * xc[..., None]

            def step(h, inp):
                a, b, c = inp
                h = a * h + b
                return (h, jnp.sum(h * c[:, None, :], axis=-1))
            h0 = jnp.zeros((seq.shape[0], D_INNER, D_STATE), dA.dtype)
            _, ys = jax.lax.scan(step, h0, (dA.transpose(1, 0, 2, 3), dBx.transpose(1, 0, 2, 3), Cm.transpose(1, 0, 2)))
            ym = ys.transpose(1, 0, 2) + D * xc
            ym = ym * jax.nn.silu(z)
            return jnp.einsum('nld,ed->nle', ym, out_proj_w)
        B, C, H, W = x.shape
        y = jax.lax.conv_general_dilated(x, conv_w, (1, 1), ((1, 1), (1, 1)), dimension_numbers=('NCHW', 'OIHW', 'NCHW'))
        y = y + conv_b[None, :, None, None]
        seq = y.reshape(B * H * W, TOKEN_NUM, GCN)
        out = _mamba(seq, in_proj_w, conv1d_w, conv1d_b, x_proj_w, dt_proj_w, dt_proj_b, A_log, D, out_proj_w)
        xr = out.reshape(B, C, H, W)
        g = xr.reshape(B, GROUPS, C // GROUPS, H, W)
        mu = g.mean((2, 3, 4), keepdims=True)
        var = g.var((2, 3, 4), keepdims=True)
        g = (g - mu) / jnp.sqrt(var + EPS)
        xp = g.reshape(B, C, H, W) * gn_w[None, :, None, None] + gn_b[None, :, None, None]
        xp = jax.nn.silu(xp)
        return x + xp

    def _gn(v, G=32, eps=1e-5):
        B_, C_, H_, W_ = v.shape
        g = v.reshape(B_, G, C_ // G, H_, W_)
        m = jnp.mean(g, axis=(2, 3, 4), keepdims=True)
        s = jnp.var(g, axis=(2, 3, 4), keepdims=True)
        return ((g - m) / jnp.sqrt(s + eps)).reshape(v.shape)

    def _ln_c(v, eps=1e-6):
        m = jnp.mean(v, axis=1, keepdims=True)
        s = jnp.var(v, axis=1, keepdims=True)
        return (v - m) / jnp.sqrt(s + eps)

    def _ln_t(v, eps=1e-5):
        m = jnp.mean(v, axis=-1, keepdims=True)
        s = jnp.var(v, axis=-1, keepdims=True)
        return (v - m) / jnp.sqrt(s + eps)

    def _to_tokens(v):
        B_, C_, H_, W_ = v.shape
        return v.reshape(B_, C_, H_ * W_).transpose(0, 2, 1)
    def _from_tokens(t, like):
        B_, C_, H_, W_ = like.shape
        return t.transpose(0, 2, 1).reshape(B_, C_, H_, W_)

    x = _L0_conv_ref(x, L0_conv_pos_w, L0_conv_pos_b, L0_conv_ln1_g, L0_conv_ln1_b, L0_conv_qkv_w, L0_conv_qkv_b, L0_conv_lepe_w, L0_conv_lepe_b, L0_conv_wo_w, L0_conv_wo_b, L0_conv_ln2_g, L0_conv_ln2_b, L0_conv_mlp_w1, L0_conv_mlp_b1, L0_conv_mlp_w2, L0_conv_mlp_b2)
    x = _L1_conv_ref(x, L1_conv_conv_w, L1_conv_conv_b, L1_conv_gn_w, L1_conv_gn_b, L1_conv_in_proj_w, L1_conv_conv1d_w, L1_conv_conv1d_b, L1_conv_x_proj_w, L1_conv_dt_proj_w, L1_conv_dt_proj_b, L1_conv_A_log, L1_conv_D, L1_conv_out_proj_w)
    return x


_drawn_inputs = setup_inputs


def setup_inputs(seed=0):
    import zlib

    import numpy as np

    out = dict(_drawn_inputs(seed))
    spreads = {'L0_conv_pos_b': (0.0, 0.1),
     'L0_conv_ln1_g': (1.0, 0.6),
     'L0_conv_ln1_b': (0.0, 0.8),
     'L0_conv_qkv_b': (0.0, 0.308),
     'L0_conv_lepe_b': (0.0, 0.281),
     'L0_conv_wo_b': (0.0, 0.1),
     'L0_conv_ln2_g': (1.0, 0.6),
     'L0_conv_ln2_b': (0.0, 0.8),
     'L0_conv_mlp_b1': (0.0, 0.35),
     'L0_conv_mlp_b2': (0.0, 0.1),
     'L1_conv_conv_b': (0.0, 0.1),
     'L1_conv_gn_w': (1.0, 0.2),
     'L1_conv_gn_b': (0.0, 0.1),
     'L1_conv_conv1d_b': (0.0, 0.1),
     'L1_conv_dt_proj_b': (-2.0, 0.6),
     'L1_conv_D': (1.0, 0.2)}
    factors = {'L0_conv_qkv_w': 5.942, 'L0_conv_lepe_w': 8.0, 'L1_conv_A_log': 3.16}
    for name, (base, spread) in spreads.items():
        noise = np.random.default_rng([zlib.crc32(name.encode()), seed]).standard_normal(out[name].shape)
        drawn = base * np.exp(spread * noise) if base else spread * noise
        out[name] = jnp.asarray(drawn.astype(out[name].dtype))
    for name, factor in factors.items():
        out[name] = (out[name] * factor).astype(out[name].dtype)
    return out
```

```python
from contextlib import ExitStack

import concourse.bass as bass
from concourse import mybir

FP32 = mybir.dt.float32
BF16 = mybir.dt.bfloat16
U32 = mybir.dt.uint32
ALU = mybir.AluOpType
ACT = mybir.ActivationFunctionType
AXX = mybir.AxisListType.X

IMGS, C, H, W = 16, 128, 56, 56
PIX = H * W
NWIN, WS = 7, 8
WPIX = WS * WS
P2 = NWIN * NWIN
STRIP = WS * W
HEADS, HD, TOPK = 4, 32, 4
SCALE = float(C) ** -0.5
MLP = 3
POS_TAPS, LEPE_TAPS = 9, 25
T, K, DI, NS, G = 8, 16, 32, 16, 4
CPX = T * K
CHUNKS = (PIX + WPIX) // CPX
SPX = CHUNKS * CPX
ONE = 1
TOK = T * C
HALF = NS // 2
NB = IMGS // G
EPS_LN, EPS_GN = 1e-6, 1e-5

_V = {}


def _columns():
    at = 0
    for name, n in (("pos_w", 9), ("pos_b", 1), ("g1", 1), ("b1", 1), ("qkv_b", 3), ("lepe_w", 25), ("lepe_b", 1),
                    ("wo_b", 1), ("g2", 1), ("b2", 1), ("mb1", 3), ("mb2", 1), ("conv_b", 1), ("gn_w", 1), ("gn_b", 1),
                    ("c1b", 1), ("dtb", 1), ("D", 1), ("alog", NS), ("headmask", 4), ("rowmask", 2)):
        _V[name] = (at, n)
        at += n
    return at


NV = _columns()


def layer0(nc, d, x3_dram, ys_dram):
    ctx = ExitStack()
    with ctx:
        def sb(name, shape, dt=FP32):
            return ctx.enter_context(nc.sbuf_tensor(name, shape, dt))

        sems = []

        def sem(name):
            sems.append(ctx.enter_context(nc.semaphore(name)))
            return sems[-1]

        bank = [ctx.enter_context(nc.psum_tensor(f"bank{i}", [C, 512], FP32)) for i in range(8)]

        vec = sb("vec", [C, NV])
        ident = sb("ident", [C, C])
        centre = sb("centre", [C, C])
        mean = sb("mean", [C, C])
        fold = sb("fold", [C, WPIX])
        wqkv = sb("wqkv", [C, 3 * C])
        wo = sb("wo", [C, C])
        w1 = sb("w1", [C, MLP * C])
        w2 = sb("w2", [C, MLP, C])
        wconv = sb("wconv", [C, 9, C])
        fb = sb("fb", [C, 6])
        obias = sb("obias", [C, 1])
        epsc = sb("epsc", [C, 1])
        wc1 = sb("wc1", [C, 1])

        xpad = sb("xpad", [C, H + 2, W + 2])
        x1 = sb("x1", [C, H, W])
        qs = sb("qs", [C, P2, WPIX])
        ks = sb("ks", [C, P2 * WPIX])
        vt = sb("vt", [WPIX, P2 * C])
        vpad = sb("vpad", [C, H + 4, W + 4])
        oacc = sb("oacc", [C, H, W])
        att = sb("att", [C, P2, WPIX])
        xn2 = att
        x3pad = sb("x3pad", [C, H + 2, W + 2])
        ysb = sb("ysb", [C, SPX])

        sq = sb("sq", [C, 2, STRIP])
        lnv = sb("lnv", [C, STRIP])
        rstd = sb("rstd", [C, 2, STRIP])
        xn = sb("xn", [C, 2, NWIN, WPIX])
        xw = sb("xw", [C, P2])
        qw = sb("qw", [C, 2, P2])
        lg = sb("lg", [P2, P2])
        mx8 = sb("mx8", [P2, 8])
        ix8 = sb("ix8", [P2, 8], U32)
        ixrow = sb("ixrow", [1, P2 * TOPK], U32)
        qbd = sb("qbd", [C, 2, 4, WPIX])
        nmax = sb("nmax", [C, 2, 2])
        prob = sb("prob", [C, 2, 2, 256])
        psums = sb("psums", [C, 2, 2])
        rinv = sb("rinv", [C, 2, 2])
        rmask = sb("rmask", [C, 2, 2, 2])
        ksel = sb("ksel", [C, 2, TOPK * WPIX])
        vsel = sb("vsel", [2 * WPIX, 2, TOPK // 2, C])
        pT = sb("pT", [2 * WPIX, 2, 4, C])
        on = sb("on", [C, 2, C])
        hid = sb("hid", [C, 2, MLP, STRIP])

        s_gate = sem("s_gate")
        s_w = sem("s_w")
        s_prep = sem("s_prep")
        s_fb = sem("s_fb")
        s_oz = sem("s_oz")
        s_fold = sem("s_fold")
        s_x = sem("s_x")
        s_pos = sem("s_pos")
        s_cen = sem("s_cen")
        s_sq = sem("s_sq")
        s_var = sem("s_var")
        s_ln = sem("s_ln")
        s_rs = sem("s_rs")
        s_xn = sem("s_xn")
        s_q = sem("s_q")
        s_vt = sem("s_vt")
        s_qk = sem("s_qk")
        s_v = sem("s_v")
        s_xw = sem("s_xw")
        s_qw = sem("s_qw")
        s_qwe = sem("s_qwe")
        s_lg = sem("s_lg")
        s_top = sem("s_top")
        s_ix = sem("s_ix")
        s_bd = sem("s_bd")
        s_vs = [sem("s_vs0"), sem("s_vs1")]
        s_s = sem("s_s")
        s_m = sem("s_m")
        s_p = sem("s_p")
        s_ri = sem("s_ri")
        s_pt = sem("s_pt")
        s_pte = sem("s_pte")
        s_o = sem("s_o")
        s_on = sem("s_on")
        s_of = sem("s_of")
        s_oa = sem("s_oa")
        s_lepe = sem("s_lepe")
        s_wo = sem("s_wo")
        s_x2 = sem("s_x2")
        s_xn2 = sem("s_xn2")
        s_h = sem("s_h")
        s_g = sem("s_g")
        s_y2 = sem("s_y2")
        s_x3 = sem("s_x3")
        s_pad = sem("s_pad")
        s_cv = sem("s_cv")
        s_ys = sem("s_ys")
        s_zero = sem("s_zero")
        s_x3o = sem("s_x3o")
        s_yso = sem("s_yso")

        def v(name, i=0, n=1, rows=slice(None)):
            at = _V[name][0] + i
            return vec[rows, at:at + n]

        SN = NWIN
        NW = P2
        LQ = 4
        LROWS = H // LQ
        LEPES = LEPE_TAPS * LQ
        LEAD, BODY = 5, 8
        PTAPS = [(k // 3 - 1, k % 3 - 1) for k in range(POS_TAPS)]
        N_W = 10

        def chosen(engine, w):
            return nc.values_load_multi_w_load_instructions(
                ixrow[0:1, bass.ds(w * TOPK, TOPK)], engines=[engine], min_val=0, max_val=P2 - 1)[1]

        block = ctx.enter_context(nc.Block())

        @block.sync
        def _(sp):
            for dst, src in ((vec, "vecs"), (ident, "ident"), (centre, "centre"), (mean, "mean"), (fold, "fold"),
                             (wqkv, "qkv_w"), (wo, "wo_w"), (w1, "mlp_w1")):
                sp.dma_start(dst[:, :], d[src]).then_inc(s_w, 16)
            sp.dma_start(w2[:, :, :], d["mlp_w2"].rearrange("(j p) n -> p j n", p=C)).then_inc(s_w, 16)
            sp.dma_start(wconv[:, :, :], d["conv_w"]).then_inc(s_w, 16)
            sp.wait_ge(s_zero, ONE + 1)
            with sp.Fori(0, NB) as bq:
                with sp.Fori(0, G) as bg:
                    b = bq * G + bg
                    sp.wait_ge(s_pos, ONE + b * POS_TAPS)
                    sp.dma_start(xpad[:, 1:H + 1, 1:W + 1],
                                 d["x"][bass.ds(b, 1)].rearrange("a c h w -> c (a h) w")).then_inc(s_x, 16)
                    sp.wait_ge(s_top, ONE + 3 * (b + 1))
                    sp.dma_start(ixrow[0:1, :].rearrange("a (p k) -> a p k", k=TOPK), ix8[:, 0:TOPK]
                                 ).then_inc(s_ix, 16)
                    sp.wait_ge(s_ix, ONE + 16 * (b + 1))
                    sp.wait_ge(s_v, ONE + 3 * SN * (b + 1))
                    sp.sem_inc(s_gate, 1)

                    def gather(w, u, k, first=False):
                        at = chosen(mybir.EngineType.SP, w)
                        sp.wait_ge(s_o, ONE + b * NW if first else ONE + b * NW + w - 1)
                        for t in range(TOPK):
                            sp.dma_start(vsel[WPIX * (t % 2):WPIX * (t % 2 + 1), u, t // 2, :],
                                         vt[:, bass.ds(at[t] * C, C)]).then_inc(s_vs[u], 16)

                    gather(0, 0, 0, True)
                    with sp.Fori(0, (NW - 1) // 2) as k:
                        for i in range(2):
                            gather(k * 2 + i + 1, (i + 1) % 2, k)
                    sp.wait_ge(s_x3, ONE + SN * (b + 1))
                    sp.dma_start(x3_dram[bass.ds(b, 1)].rearrange("a c p -> c (a p)"),
                                 x1[:, :, :].rearrange("c h w -> c (h w)")).then_inc(s_x3o, 16)
            sp.wait_ge(s_x3o, ONE + 16 * IMGS)

        @block.gpsimd
        def _(pool):
            for x in sems:
                pool.sem_inc(x, ONE)
            nc.gpsimd.memset(vpad[:, :, :], 0.0)
            nc.gpsimd.memset(ysb[:, :], 0.0)
            nc.gpsimd.memset(epsc[:, :], EPS_LN)
            nc.gpsimd.memset(x3pad[:, :, :], 0.0)
            nc.gpsimd.memset(xpad[:, :, :], 0.0).then_inc(s_zero, 1)
            pool.wait_ge(s_w, ONE + 16 * N_W)

            def query_block(b, w, u, first):
                at = chosen(mybir.EngineType.Pool, w)
                if not first:
                    pool.wait_ge(s_s, ONE + b * NW + w - 1)
                nc.gpsimd.tensor_tensor(
                    out=qbd[:, u], in0=qs[:, bass.ds(w, 1), :].broadcast_to([C, 4, WPIX]),
                    in1=v("headmask", 0, 4).unsqueeze(2).broadcast_to([C, 4, WPIX]),
                    op=ALU.mult).then_inc(s_bd, 1)
                for t in range(TOPK):
                    m = nc.gpsimd.tensor_copy(ksel[:, u, WPIX * t:WPIX * (t + 1)], ks[:, bass.ds(at[t] * WPIX, WPIX)])
                m.then_inc(s_bd, 1)

            with pool.Fori(0, NB) as bq:
                with pool.Fori(0, G) as bg:
                    b = bq * G + bg
                    pool.wait_ge(s_lepe, ONE + LQ + b * LEPES)
                    pool.wait_ge(s_wo, ONE + b * SN)
                    pool.sem_inc(s_gate, 1)
                    nc.gpsimd.memset(oacc[:, :, :], 0.0).then_inc(s_oz, 1)
                    pool.wait_ge(s_qk, ONE + 2 * SN * (b + 1))
                    pool.wait_ge(s_ix, ONE + 16 * (b + 1))
                    pool.sem_inc(s_gate, 1)
                    query_block(b, 0, 0, True)
                    with pool.Fori(0, (NW - 1) // 2) as k:
                        for i in range(2):
                            query_block(b, k * 2 + i + 1, (i + 1) % 2, False)
                    pool.wait_ge(s_x3, ONE + SN * (b + 1))
                    pool.sem_inc(s_gate, 1)
                    nc.gpsimd.tensor_copy(x3pad[:, 1:H + 1, 1:W + 1], x1[:, :, :]).then_inc(s_pad, 1)

        @block.scalar
        def _(act):
            act.wait_ge(s_zero, ONE + 1)
            act.wait_ge(s_w, ONE + 16 * N_W)
            act.wait_ge(s_fold, ONE + 1)
            for j in range(3):
                nc.scalar.activation(fb[:, j:j + 1], bank[0][:, j:j + 1], ACT.Identity, bias=v("qkv_b", j))
            for j in range(3):
                m = nc.scalar.activation(fb[:, 3 + j:4 + j], bank[0][:, 3 + j:4 + j], ACT.Identity, bias=v("mb1", j))
            m.then_inc(s_fb, 1)
            act.wait_ge(s_fb, ONE + 1)

            def norm(b, s, second):
                n = b * 2 * SN + s + SN * second + 1
                act.wait_ge(s_cen, ONE + n)
                nc.scalar.activation(sq[:, s % 2], bank[s % 2][:, 0:STRIP], ACT.Square).then_inc(s_sq, 1)
                act.wait_ge(s_var, ONE + n)
                nc.scalar.activation(lnv[:, :], bank[2][:, 0:STRIP], ACT.Ln, bias=epsc[:, 0:1]).then_inc(s_ln, 1)
                act.wait_ge(s_ln, ONE + n)
                if s >= 2:
                    act.wait_ge(s_xn2 if second else s_xn, b * SN + s - 1)
                nc.scalar.activation(rstd[:, s % 2], lnv[:, :], ACT.Exp, scale=-0.5).then_inc(s_rs, 1)

            def window(b, w, par, i=None):
                n = b * NW + w
                u = (par + 1) % 2
                if i is None or 1 <= i <= NW:
                    act.wait_ge(s_pt, ONE + n)
                    if i is None or i >= 3:
                        act.wait_ge(s_o, ONE + n - 2)
                    nc.scalar.activation(pT[:, u].rearrange("k i m -> k (i m)"), bank[2 + u][:, :], ACT.Identity
                                         ).then_inc(s_pte, 1)
                if i is None or i < NW:
                    u = par
                    act.wait_ge(s_m, ONE + n + 1)
                    if i is None or i >= 2:
                        act.wait_ge(s_ri, ONE + 2 * n - 2)
                    for hp in range(2):
                        nc.scalar.activation(prob[:, u, hp], bank[u][:, 256 * hp:256 * hp + 256], ACT.Exp,
                                             bias=nmax[:, u, hp:hp + 1], accum_out=psums[:, u, hp:hp + 1]
                                             ).then_inc(s_p, 1)

            with act.Fori(0, NB) as bq:
                with act.Fori(0, G) as bg:
                    b = bq * G + bg
                    act.preload_act_table_set("natural_log_exp_and_others")
                    norm(b, 0, 0)
                    for s in range(SN):
                        if s + 1 < SN:
                            norm(b, s + 1, 0)
                        act.wait_ge(s_q, ONE + b * 3 * SN + 3 * s + 1)
                        nc.scalar.activation(qs[:, NWIN * s:NWIN * (s + 1), :].rearrange("c w k -> c (w k)"),
                                             bank[3][:, 0:STRIP], ACT.Identity, bias=fb[:, 0:1]).then_inc(s_qk, 1)
                        act.wait_ge(s_q, ONE + b * 3 * SN + 3 * s + 2)
                        nc.scalar.activation(ks[:, STRIP * s:STRIP * (s + 1)], bank[4][:, 0:STRIP],
                                             ACT.Identity, bias=fb[:, 1:2]).then_inc(s_qk, 1)
                    act.wait_ge(s_qw, ONE + 2 * b + 2)
                    for j in range(2):
                        nc.scalar.activation(qw[:, j], bank[0][:, j * 64:j * 64 + P2], ACT.Identity,
                                             bias=fb[:, j:j + 1], scale=1.0 / WPIX).then_inc(s_qwe, 1)
                    for w in range(LEAD):
                        window(b, w, w % 2, w)
                    with act.Fori(0, (NW - LEAD) // 2) as k:
                        for i in range(2):
                            window(b, k * 2 + i + LEAD, (LEAD + i) % 2)
                    window(b, NW, NW % 2, NW)
                    for s in range(SN):
                        norm(b, s, 1)
                    for s in range(SN):
                        for j in range(MLP):
                            act.wait_ge(s_h, ONE + b * MLP * SN + s * MLP + j + 1)
                            if s >= 2:
                                act.wait_ge(s_y2, ONE + b * SN + s - 1)
                            nc.scalar.activation(hid[:, s % 2, j], bank[3 + j][:, 0:STRIP], ACT.Gelu,
                                                 bias=fb[:, 3 + j:4 + j]).then_inc(s_g, 1)
                    act.wait_ge(s_yso, ONE + 16 * b)
                    for s in range(SN):
                        act.wait_ge(s_cv, ONE + b * SN + s + 1)
                        p = bank[s % 2]
                        at = s * STRIP
                        lo, up = slice(0, 64), slice(64, 128)
                        n = STRIP if s < SN - 1 else STRIP - WPIX
                        nc.scalar.activation(ysb[lo, at:at + n], p[lo, 0:n], ACT.Identity, bias=v("conv_b", rows=lo))
                        if n < STRIP:
                            nc.scalar.activation(ysb[up, 0:WPIX], p[lo, n:STRIP], ACT.Identity,
                                                 bias=v("conv_b", rows=lo))
                        nc.scalar.activation(ysb[up, WPIX + at:WPIX + at + STRIP], p[up, 0:STRIP], ACT.Identity,
                                             bias=v("conv_b", rows=up)).then_inc(s_ys, 1)
                    act.wait_ge(s_ys, ONE + SN * (b + 1))
                    act.dma_start(ys_dram[bass.ds(bq, 1), :, :, bass.ds(bg, 1), :].rearrange("q j c g p -> c (q j g) p"),
                                  ysb[:, :].rearrange("c (j p) -> c j p", p=CPX)).then_inc(s_yso, 16)
            act.wait_ge(s_yso, ONE + 16 * IMGS)

        @block.vector
        def _(dve):
            dve.wait_ge(s_w, ONE + 16 * N_W)
            dve.wait_ge(s_fold, ONE + 1)
            nc.vector.tensor_scalar(out=wqkv[:, :], in0=wqkv[:, :], scalar1=v("g1"), scalar2=None, op0=ALU.mult)
            nc.vector.tensor_scalar(out=w1[:, :], in0=w1[:, :], scalar1=v("g2"), scalar2=None, op0=ALU.mult)
            nc.vector.tensor_scalar(out=wc1[:, :], in0=v("pos_w", 4), scalar1=1.0, scalar2=None, op0=ALU.add
                                    ).then_inc(s_prep, 1)
            dve.wait_ge(s_fb, ONE + 1)
            nc.vector.tensor_tensor(out=obias[:, :], in0=fb[:, 2:3], in1=v("lepe_b"), op=ALU.add).then_inc(s_prep, 1)
            dve.wait_ge(s_prep, ONE + 2)

            dve.sem_inc(s_lepe, LQ)

            def lepe(b, dy, dx, part):
                src = vpad[:, bass.ds(dy + part * LROWS, LROWS), dx:dx + W]
                dst = oacc[:, part * LROWS:(part + 1) * LROWS, :]
                dve.wait_ge(s_lepe, ONE + b * LEPES + (dy * 5 + dx) * LQ + part + 1)
                nc.vector.scalar_tensor_tensor(out=dst, in0=src, scalar=vec[:, bass.ds(dy * 5 + dx + _V["lepe_w"][0], 1)],
                                               in1=dst, op0=ALU.mult, op1=ALU.add).then_inc(s_lepe, 1)

            def window(b, w, par, i=None, extra=()):
                n = b * NW + w
                if i is None or i < NW:
                    u = par
                    dve.wait_ge(s_s, ONE + n + 1)
                    if i is None or i >= 2:
                        dve.wait_ge(s_p, ONE + 2 * n - 2)
                    nc.vector.tensor_reduce(out=nmax[:, u], in_=bank[u][:, :].rearrange("c (h k) -> c h k", h=2),
                                            axis=AXX, op=ALU.max, negate=True).then_inc(s_m, 1)
                for f in extra:
                    f()
                if i is None or 1 <= i <= NW:
                    u = (par + 1) % 2
                    dve.wait_ge(s_p, ONE + 2 * n)
                    nc.vector.reciprocal(rinv[:, u], psums[:, u]).then_inc(s_ri, 1)
                    dve.wait_ge(s_ri, ONE + 2 * n - 1)
                    nc.vector.tensor_tensor(out=rmask[:, u], in0=rinv[:, u].unsqueeze(2).broadcast_to([C, 2, 2]),
                                            in1=v("rowmask", 0, 2).unsqueeze(1).broadcast_to([C, 2, 2]),
                                            op=ALU.mult).then_inc(s_ri, 1)
                if i is None or 2 <= i <= NW + 1:
                    u = par
                    dve.wait_ge(s_ri, ONE + 2 * n - 2)
                    dve.wait_ge(s_o, ONE + n - 1)
                    if i is None or i >= 4:
                        dve.wait_ge(s_of, ONE + n - 3)
                    nc.vector.tensor_tensor(
                        out=on[:, u].rearrange("c (a k) -> c a k", k=HD),
                        in0=bank[4 + u][:, 0:C].rearrange("c (a k) -> c a k", k=HD),
                        in1=rmask[:, u].rearrange("c a k -> c (a k)").unsqueeze(2).broadcast_to([C, 4, HD]),
                        op=ALU.mult).then_inc(s_on, 1)
                if i is None or 3 <= i <= NW + 2:
                    u = (par + 1) % 2
                    dve.wait_ge(s_of, ONE + n - 2)
                    nc.vector.tensor_scalar(out=att[:, bass.ds(w - 3, 1), :].rearrange("c a k -> c (a k)"),
                                            in0=bank[6 + u][:, 0:WPIX], scalar1=obias[:, 0:1], scalar2=None,
                                            op0=ALU.add).then_inc(s_oa, 1)

            with dve.Fori(0, NB) as bq:
                with dve.Fori(0, G) as bg:
                    b = bq * G + bg
                    dve.wait_ge(s_x, ONE + 16 * (b + 1))
                    dve.wait_ge(s_x3o, ONE + 16 * b)
                    dve.wait_ge(s_pad, ONE + b)
                    nc.vector.tensor_scalar(out=x1[:, :, :], in0=xpad[:, 1:H + 1, 1:W + 1], scalar1=wc1[:, 0:1],
                                            scalar2=v("pos_b"), op0=ALU.mult, op1=ALU.add).then_inc(s_pos, 1)
                    n = 1
                    for k, (dy, dx) in enumerate(PTAPS):
                        if (dy, dx) == (0, 0):
                            continue
                        dve.wait_ge(s_pos, ONE + b * POS_TAPS + n)
                        nc.vector.scalar_tensor_tensor(
                            out=x1[:, :, :], in0=xpad[:, 1 + dy:1 + dy + H, 1 + dx:1 + dx + W],
                            scalar=v("pos_w", k), in1=x1[:, :, :], op0=ALU.mult, op1=ALU.add).then_inc(s_pos, 1)
                        n += 1

                    def by_window(ap):
                        return ap.rearrange("c (y w x) -> c w y x", y=WS, w=NWIN)

                    def normalise(s):
                        dve.wait_ge(s_rs, ONE + b * 2 * SN + s + 1)
                        if s >= 2:
                            dve.wait_ge(s_vt, ONE + b * 2 * SN + 2 * (s - 1))
                        nc.vector.tensor_tensor(out=xn[:, s % 2].rearrange("c w (y x) -> c w y x", y=WS),
                                                in0=by_window(bank[s % 2][:, 0:STRIP]), in1=by_window(rstd[:, s % 2]),
                                                op=ALU.mult).then_inc(s_xn, 1)

                    normalise(0)
                    for s in range(SN):
                        if s + 1 < SN:
                            normalise(s + 1)
                        dve.wait_ge(s_xn, ONE + b * SN + s + 1)
                        nc.vector.tensor_reduce(out=xw[:, NWIN * s:NWIN * (s + 1)], in_=xn[:, s % 2], axis=AXX,
                                                op=ALU.add).then_inc(s_xw, 1)
                        dve.wait_ge(s_q, ONE + b * 3 * SN + 3 * s + 3)
                        nc.vector.tensor_scalar(
                            out=vpad[:, 2 + WS * s:2 + WS * (s + 1), 2:2 + W].rearrange("c y (w x) -> c w y x", x=WS),
                            in0=bank[5][:, 0:STRIP].rearrange("c (w y x) -> c w y x", w=NWIN, y=WS),
                            scalar1=fb[:, 2:3], scalar2=None, op0=ALU.add).then_inc(s_v, 1)
                        for j, (w0, w1_) in enumerate(((0, 4), (4, 7))):
                            dve.wait_ge(s_vt, ONE + b * 2 * SN + 2 * s + j + 1)
                            nc.vector.tensor_copy(vt[:, (NWIN * s + w0) * C:(NWIN * s + w1_) * C],
                                                  bank[6 + j][0:WPIX, 0:(w1_ - w0) * C]).then_inc(s_v, 1)
                    dve.wait_ge(s_lg, ONE + b + 1)
                    nc.vector.tensor_copy(lg[:, :], bank[0][0:P2, 128:128 + P2]).then_inc(s_top, 1)
                    dve.wait_ge(s_top, ONE + 3 * b + 1)
                    dve.sem_inc(s_gate, 1)
                    nc.vector.max(out=mx8[:, :], in_=lg[:, :]).then_inc(s_top, 1)
                    dve.wait_ge(s_top, ONE + 3 * b + 2)
                    dve.wait_ge(s_ix, ONE + 16 * b)
                    dve.sem_inc(s_gate, 1)
                    nc.vector.max_index(out=ix8[:, :], in_max=mx8[:, :], in_values=lg[:, :]).then_inc(s_top, 1)
                    dve.wait_ge(s_v, ONE + 3 * SN * (b + 1))
                    dve.wait_ge(s_oz, ONE + b + 1)
                    for w in range(LEAD):
                        window(b, w, w % 2, w)
                    with dve.Fori(0, 5) as dy:
                        taps = [(lambda dx=dx, part=part: lepe(b, dy, dx, part)) for dx in range(5)
                                for part in range(LQ)]
                        per = len(taps) / BODY
                        for i in range(BODY):
                            window(b, dy * BODY + i + LEAD, (LEAD + i) % 2,
                                   extra=taps[round(i * per):round((i + 1) * per)])
                    with dve.Fori(0, (NW - LEAD - 5 * BODY) // 2) as k:
                        for i in range(2):
                            window(b, k * 2 + i + LEAD + 5 * BODY, (LEAD + i) % 2)
                    for w in range(NW, NW + 3):
                        window(b, w, w % 2, w)

                    def residual(s):
                        dve.wait_ge(s_wo, ONE + b * SN + s + 1)
                        xs = x1[:, WS * s:WS * (s + 1), :].rearrange("c y x -> c (y x)")
                        nc.vector.scalar_tensor_tensor(out=xs, in0=bank[6 + s % 2][:, 0:STRIP], scalar=v("wo_b"),
                                                       in1=xs, op0=ALU.add, op1=ALU.add).then_inc(s_x2, 1)

                    residual(0)
                    residual(1)
                    for s in range(SN):
                        if s + 2 < SN:
                            residual(s + 2)
                        dve.wait_ge(s_rs, ONE + b * 2 * SN + SN + s + 1)
                        nc.vector.tensor_tensor(out=xn2[:, NWIN * s:NWIN * (s + 1), :].rearrange("c w k -> c (w k)"),
                                                in0=bank[s % 2][:, 0:STRIP], in1=rstd[:, s % 2], op=ALU.mult
                                                ).then_inc(s_xn2, 1)
                    for s in range(SN):
                        dve.wait_ge(s_y2, ONE + b * SN + s + 1)
                        dve.wait_ge(s_x2, ONE + b * SN + s + 1)
                        xs = x1[:, WS * s:WS * (s + 1), :].rearrange("c y x -> c (y x)")
                        nc.vector.scalar_tensor_tensor(out=xs, in0=bank[6 + s % 2][:, 0:STRIP], scalar=v("mb2"),
                                                       in1=xs, op0=ALU.add, op1=ALU.add).then_inc(s_x3, 1)

        @block.tensor
        def _(pe):
            pe.wait_ge(s_w, ONE + 16 * N_W)
            for j in range(3):
                nc.tensor.matmul(bank[0][:, j:j + 1], wqkv[:, j * C:(j + 1) * C], v("b1"), start=True, stop=True)
            for j in range(3):
                m = nc.tensor.matmul(bank[0][:, 3 + j:4 + j], w1[:, j * C:(j + 1) * C], v("b2"), start=True, stop=True)
            m.then_inc(s_fold, 1)
            pe.wait_ge(s_fb, ONE + 1)
            pe.wait_ge(s_prep, ONE + 2)

            def strip_of(t, s):
                return t[:, WS * s:WS * (s + 1), :].rearrange("c y x -> c (y x)")

            with pe.Fori(0, NB) as bq:
                with pe.Fori(0, G) as bg:
                    b = bq * G + bg

                    def cen(s, second):
                        if second:
                            pe.wait_ge(s_x2, ONE + b * SN + s + 1)
                            if s >= 2:
                                pe.wait_ge(s_xn2, ONE + b * SN + s - 1)
                        elif s >= 2:
                            pe.wait_ge(s_xn, ONE + b * SN + s - 1)
                        nc.tensor.matmul(bank[s % 2][:, 0:STRIP], centre[:, :], strip_of(x1, s), start=True, stop=True
                                         ).then_inc(s_cen, 1)

                    def var(s, second):
                        n = b * 2 * SN + SN * second + s
                        pe.wait_ge(s_sq, ONE + n + 1)
                        pe.wait_ge(s_ln, ONE + n)
                        nc.tensor.matmul(bank[2][:, 0:STRIP], mean[:, :], sq[:, s % 2], start=True, stop=True
                                         ).then_inc(s_var, 1)

                    pe.wait_ge(s_pos, ONE + POS_TAPS * (b + 1))
                    pe.wait_ge(s_ys, ONE + SN * b)
                    cen(0, 0)
                    var(0, 0)
                    for s in range(SN):
                        if s + 1 < SN:
                            cen(s + 1, 0)
                        pe.wait_ge(s_xn, ONE + b * SN + s + 1)
                        x_s = xn[:, s % 2].rearrange("c w k -> c (w k)")
                        for j in range(3):
                            if s == 0:
                                pe.wait_ge(s_g, ONE + b * MLP * SN)
                            elif j < 2:
                                pe.wait_ge(s_qk, ONE + b * 2 * SN + 2 * (s - 1) + j + 1)
                            else:
                                pe.wait_ge(s_v, ONE + b * 3 * SN + 3 * (s - 1) + 1)
                            nc.tensor.matmul(bank[3 + j][:, 0:STRIP], wqkv[:, j * C:(j + 1) * C], x_s,
                                             start=True, stop=True).then_inc(s_q, 1)
                        if s + 1 < SN:
                            var(s + 1, 0)
                        for j, (w0, w1_) in enumerate(((0, 4), (4, 7))):
                            if s == 0:
                                pe.wait_ge(s_x3, ONE + b * SN)
                            else:
                                pe.wait_ge(s_v, ONE + b * 3 * SN + 3 * (s - 1) + 2 + j)
                            for w in range(w0, w1_):
                                m = nc.tensor.matmul(bank[6 + j][0:WPIX, (w - w0) * C:(w - w0 + 1) * C],
                                                     xn[:, s % 2, w, :], wqkv[:, 2 * C:3 * C], start=True, stop=True)
                            m.then_inc(s_vt, 1)
                    pe.wait_ge(s_xw, ONE + SN * (b + 1))
                    for j in range(2):
                        nc.tensor.matmul(bank[0][:, 64 * j:64 * j + P2], wqkv[:, j * C:(j + 1) * C], xw[:, :],
                                         start=True, stop=True).then_inc(s_qw, 1)
                    pe.wait_ge(s_qwe, ONE + 2 * b + 2)
                    nc.tensor.matmul(bank[0][0:P2, 128:128 + P2], qw[:, 0], qw[:, 1], start=True, stop=True
                                     ).then_inc(s_lg, 1)

                    def window(w, par, half, i=None):
                        n = b * NW + w
                        if i is None or 3 <= i <= NW + 2:
                            u = (par + 1) % 2
                            pe.wait_ge(s_on, ONE + n - 2)
                            if i is None or i >= 5:
                                pe.wait_ge(s_oa, ONE + n - 4)
                            nc.tensor.matmul(bank[6 + u][:, 0:WPIX], on[:, u], fold[:, :], start=True, stop=True
                                             ).then_inc(s_of, 1)
                        if i is None or i < NW:
                            u = par
                            pe.wait_ge(s_bd, ONE + 2 * n + 2)
                            if i is None or i >= 2:
                                pe.wait_ge(s_p, ONE + 2 * n - 2)
                            for hp in range(2):
                                m = nc.tensor.matmul(bank[u][:, 256 * hp:256 * hp + 256],
                                                     qbd[:, u, 2 * hp:2 * hp + 2].rearrange("c h k -> c (h k)"),
                                                     ksel[:, u, :], start=True, stop=True)
                            m.then_inc(s_s, 1)
                        if i is None or 2 <= i <= NW + 1:
                            u = par
                            pe.wait_ge(s_pte, ONE + n - 1)
                            pe.wait_ge(s_vs[u], ONE + 16 * TOPK * (b * ((NW + 1 - u) // 2) + half))
                            if i is None or i >= 4:
                                pe.wait_ge(s_on, ONE + n - 3)
                            for hp in range(2):
                                for c in range(2):
                                    m = nc.tensor.matmul(bank[4 + u][:, 64 * hp:64 * hp + 64], pT[:, u, 2 * hp + c],
                                                         vsel[:, u, c, 64 * hp:64 * hp + 64],
                                                         start=(c == 0), stop=(c == 1))
                            m.then_inc(s_o, 1)
                        if i is None or 1 <= i <= NW:
                            u = (par + 1) % 2
                            pe.wait_ge(s_p, ONE + 2 * n)
                            if i is None or i >= 3:
                                pe.wait_ge(s_pte, ONE + n - 2)
                            for hp in range(2):
                                for c in range(2):
                                    m = nc.tensor.transpose(bank[2 + u][:, C * (2 * hp + c):C * (2 * hp + c + 1)],
                                                            prob[:, u, hp, C * c:C * (c + 1)], ident[:, :])
                            m.then_inc(s_pt, 1)

                    pe.wait_ge(s_qk, ONE + 2 * SN * (b + 1))
                    pe.wait_ge(s_v, ONE + 3 * SN * (b + 1))
                    pe.sem_inc(s_gate, 1)
                    for w in range(LEAD):
                        window(w, w % 2, w // 2, w)
                    with pe.Fori(0, (NW - LEAD) // 2) as k:
                        for i in range(2):
                            window(k * 2 + i + LEAD, (LEAD + i) % 2, k + (LEAD + i) // 2)
                    for w in range(NW, NW + 3):
                        window(w, w % 2, w // 2, w)

                    def project(s):
                        if s >= 2:
                            pe.wait_ge(s_x2, ONE + b * SN + s - 1)
                        nc.tensor.matmul(bank[6 + s % 2][:, 0:STRIP], wo[:, :], strip_of(oacc, s),
                                         start=True, stop=False)
                        nc.tensor.matmul(bank[6 + s % 2][:, 0:STRIP], wo[:, :],
                                         att[:, NWIN * s:NWIN * (s + 1), :].rearrange("c w (y x) -> c y w x", y=WS),
                                         start=False, stop=True).then_inc(s_wo, 1)

                    pe.wait_ge(s_oa, ONE + NW * (b + 1))
                    pe.wait_ge(s_lepe, ONE + LQ + LEPES * (b + 1))
                    project(0)
                    project(1)
                    cen(0, 1)
                    for s in range(SN):
                        if s + 2 < SN:
                            project(s + 2)
                        if s + 1 < SN:
                            cen(s + 1, 1)
                        var(s, 1)

                    def hidden(s):
                        pe.wait_ge(s_xn2, ONE + b * SN + s + 1)
                        for j in range(MLP):
                            if s >= 1:
                                pe.wait_ge(s_g, ONE + b * MLP * SN + (s - 1) * MLP + j + 1)
                            nc.tensor.matmul(bank[3 + j][:, 0:STRIP], w1[:, j * C:(j + 1) * C],
                                             xn2[:, NWIN * s:NWIN * (s + 1), :].rearrange("c w k -> c (w k)"),
                                             start=True, stop=True).then_inc(s_h, 1)

                    hidden(0)
                    for s in range(SN):
                        if s + 1 < SN:
                            hidden(s + 1)
                        pe.wait_ge(s_g, ONE + b * MLP * SN + (s + 1) * MLP)
                        if s >= 2:
                            pe.wait_ge(s_x3, ONE + b * SN + s - 1)
                        for j in range(MLP):
                            m = nc.tensor.matmul(bank[6 + s % 2][:, 0:STRIP], w2[:, j], hid[:, s % 2, j],
                                                 start=(j == 0), stop=(j == MLP - 1))
                        m.then_inc(s_y2, 1)
                    pe.wait_ge(s_pad, ONE + b + 1)
                    for s in range(SN):
                        if s >= 2:
                            pe.wait_ge(s_ys, ONE + b * SN + s - 1)
                        for k, (dy, dx) in enumerate(PTAPS):
                            m = nc.tensor.matmul(bank[s % 2][:, 0:STRIP], wconv[:, k],
                                                 x3pad[:, 1 + WS * s + dy:1 + WS * (s + 1) + dy, 1 + dx:1 + dx + W],
                                                 start=(k == 0), stop=(k == 8))
                        m.then_inc(s_cv, 1)


def sequences(nc, d, ys_dram, xr_dram):
    ctx = ExitStack()
    with ctx:
        def sb(name, shape, dt=FP32):
            return ctx.enter_context(nc.sbuf_tensor("b_" + name, shape, dt))

        sems = []

        def sem(name):
            sems.append(ctx.enter_context(nc.semaphore("b_" + name)))
            return sems[-1]

        acc = ctx.enter_context(nc.psum_tensor("b_acc", [C, TOK], FP32))
        rep = [ctx.enter_context(nc.psum_tensor(f"b_rep{i}", [C, TOK], FP32)) for i in range(2)]
        misc = [ctx.enter_context(nc.psum_tensor(f"b_misc{i}", [C, 512], FP32)) for i in range(2)]

        NCH = NB * CHUNKS
        HT = TOK // 2

        vec = sb("vec", [C, NV])
        ident = sb("ident", [C, C])
        diag_d = sb("diag_d", [C, C])
        negA = sb("negA", [C, NS])
        wx = sb("wx", [C, C])
        wz = sb("wz", [C, C])
        wtap = sb("wtap", [C, 5, C])
        wze = sb("wze", [C, 2, C])
        wdt = sb("wdt", [C, C])
        dtw = sb("dtw", [C, C])
        wbc = sb("wbc", [C, C])
        wout = sb("wout", [C, G * K])
        pickf = sb("pickf", [3 * G * HALF, HALF * C])
        pick = sb("pick", [3 * G * HALF, HALF, C], BF16)

        yc = sb("yc", [C, G, CPX])
        yr = sb("yr", [C, T, G, K])
        yT = sb("yT", [C, 4, C])
        xc = sb("xc", [C, T, C])
        zs = sb("zs", [C, 2, T, C])
        pre = sb("pre", [C, TOK])
        sp_ = sb("sp", [C, TOK])
        dt = sb("dt", [C, TOK])
        uu = sb("uu", [C, TOK])
        bcf = sb("bcf", [C, TOK])
        hi = sb("hi", [C, TOK], BF16)
        mid = sb("mid", [C, TOK], BF16)
        lo = sb("lo", [C, TOK], BF16)
        bcs = sb("bcs", [3 * G * HALF, 2, 4, TOK], BF16)
        dA = sb("dA", [C, 2, HALF, TOK - C])
        hh = sb("hh", [C, 2, HALF, TOK])
        tmp = sb("tmp", [C, HALF, C])
        ym = sb("ym", [C, TOK])
        xo = sb("xo", [C, G, CPX])

        s_gate = sem("gate")
        s_w = sem("w")
        s_p1 = sem("p1")
        s_p2 = sem("p2")
        s_yc = sem("yc")
        s_yr = sem("yr")
        s_t = sem("t")
        s_te = sem("te")
        s_x = sem("x")
        s_xe = sem("xe")
        s_z = sem("z")
        s_ze = sem("ze")
        s_d = sem("d")
        s_pre = sem("pre")
        s_min = sem("min")
        s_el = sem("el")
        s_dt = sem("dt")
        s_u = sem("u")
        s_bc = sem("bc")
        s_bce = sem("bce")
        s_sp = sem("spl")
        s_bcs = sem("bcs")
        s_rep = sem("rep")
        s_use = sem("use")
        s_a = sem("a")
        s_st = sem("st")
        s_yd = sem("yd")
        s_y = sem("y")
        s_ym = sem("ym")
        s_o = sem("o")
        s_oe = sem("oe")
        s_os = sem("os")

        def v(name, i=0, n=1):
            at = _V[name][0] + i
            return vec[:, at:at + n]

        N_W = 10
        STEPS = 2 * (T - 1)

        block = ctx.enter_context(nc.Block())

        def chunks(eng, body):
            body(0, 0, first=True)
            with eng.Fori(0, (NCH - 2) // 2) as k:
                for i in range(2):
                    body(k * 2 + i + 1, (i + 1) % 2)
            body(NCH - 1, (NCH - 1) % 2, last=True)

        @block.sync
        def _(sp):
            for dst, src in ((vec, "vecs"), (ident, "ident"), (wx, "wx"), (wz, "wz"), (wdt, "xp_dt"), (dtw, "dt_w"),
                             (wbc, "xp_bc"), (wout, "w_out"), (pickf, "pick")):
                sp.dma_start(dst[:, :], d[src]).then_inc(s_w, 16)
            sp.dma_start(wtap[:, :, :], d["taps"]).then_inc(s_w, 16)

            def load(n):
                sp.dma_start(yc[:, :, :], ys_dram[bass.ds(n, 1)].rearrange("a c g p -> c (a g) p")).then_inc(s_yc, 16)

            def split(n, par):
                sp.wait_ge(s_sp, ONE + 4 * n + 4)
                for part, src in enumerate((hi, mid, lo)):
                    for m in range(4):
                        sp.dma_start(bcs[32 * part:32 * part + 32, par, m, :], src[32 * m:32 * m + 32, :]
                                     ).then_inc(s_bcs, 16)

            def store(n):
                sp.wait_ge(s_oe, ONE + n + 1)
                sp.dma_start(xr_dram[bass.ds(n, 1)].rearrange("a c g p -> c (a g) p"), xo[:, :, :]).then_inc(s_os, 16)

            load(0)
            split(0, 0)

            def body(n, par, first=False, last=False):
                if not last:
                    sp.wait_ge(s_yr, ONE + n + 1)
                    load(n + 1)
                if not first:
                    store(n - 1)
                if not last:
                    if not first:
                        sp.wait_ge(s_rep, ONE + 32 * n)
                    split(n + 1, 1 - par)

            chunks(sp, body)
            store(NCH - 1)
            sp.wait_ge(s_os, ONE + 16 * NCH)

        @block.gpsimd
        def _(pool):
            for x in sems:
                pool.sem_inc(x, ONE)

            def front(n, before=False):
                pool.wait_ge(s_yc, ONE + 16 * n + 16)
                pool.wait_ge(s_t, ONE + n)
                pool.sem_inc(s_gate, 1)
                nc.gpsimd.tensor_copy(yr[:, :, :, :], yc[:, :, :].rearrange("c g (t k) -> c t g k", k=K)
                                      ).then_inc(s_yr, 1)
                pool.wait_ge(s_pre, ONE + 2 * n + 2)
                pool.sem_inc(s_gate, 1)
                nc.gpsimd.tensor_scalar(out=sp_[:, :], in0=pre[:, :], scalar1=40.0, scalar2=None, op0=ALU.min
                                        ).then_inc(s_min, 1)
                pool.wait_ge(s_bce, ONE + 2 * n + 2)
                pool.wait_ge(s_bcs, ONE + 16 * 12 * n)
                pool.sem_inc(s_gate, 1)
                nc.gpsimd.tensor_copy(hi[:, :], bcf[:, :]).then_inc(s_sp, 1)
                pool.wait_ge(s_sp, ONE + 4 * n + 1)
                nc.gpsimd.tensor_tensor(out=bcf[:, :], in0=bcf[:, :], in1=hi[:, :], op=ALU.subtract).then_inc(s_sp, 1)
                pool.wait_ge(s_sp, ONE + 4 * n + 2)
                pool.sem_inc(s_gate, 1)
                nc.gpsimd.tensor_copy(mid[:, :], bcf[:, :]).then_inc(s_sp, 1)
                pool.wait_ge(s_sp, ONE + 4 * n + 3)
                nc.gpsimd.tensor_tensor(out=lo[:, :], in0=bcf[:, :], in1=mid[:, :], op=ALU.subtract).then_inc(s_sp, 1)
                pool.wait_ge(s_dt, ONE + n + 1)
                pool.wait_ge(s_xe, ONE + 2 * n + 2)
                if before:
                    pool.wait_ge(s_use, ONE + 32 * n - 8)
                nc.gpsimd.tensor_tensor(out=uu[:, :], in0=dt[:, :], in1=xc[:, :, :].rearrange("c t m -> c (t m)"),
                                        op=ALU.mult).then_inc(s_u, 1)

            front(0)

            def body(n, par, first=False, last=False):
                if not last:
                    front(n + 1, True)

            chunks(pool, body)

        @block.scalar
        def _(act):
            act.wait_ge(s_w, ONE + 16 * N_W)
            act.preload_act_table_set("natural_log_exp_and_others")
            nc.scalar.activation(negA[:, :], v("alog", 0, NS), ACT.Exp).then_inc(s_p2, 1)
            act.wait_ge(s_p2, ONE + 1)
            nc.scalar.activation(negA[:, :], negA[:, :], ACT.Copy, scale=-1.0)
            nc.scalar.activation(pick[:, :, :].rearrange("k n c -> k (n c)"), pickf[:, :], ACT.Copy).then_inc(s_p2, 1)
            act.wait_ge(s_p2, ONE + 2)

            def front(n, par):
                act.wait_ge(s_t, ONE + n + 1)
                nc.scalar.activation(yT[:, :, :].rearrange("c q m -> c (q m)"), misc[0][:, :], ACT.Copy).then_inc(s_te, 1)
                for h in range(2):
                    act.wait_ge(s_x, ONE + 2 * n + h + 1)
                    if h == 0:
                        act.wait_ge(s_yd, ONE + n)
                    nc.scalar.activation(xc[:, h:T:2, :], misc[1 - h][:, :].rearrange("c (q m) -> c q m", m=C),
                                         ACT.Silu, bias=v("c1b")).then_inc(s_xe, 1)
                for h in range(2):
                    act.wait_ge(s_z, ONE + 2 * n + h + 1)
                    nc.scalar.activation(zs[:, par, h:T:2, :], misc[1 - h][:, :].rearrange("c (q m) -> c q m", m=C),
                                         ACT.Silu).then_inc(s_ze, 1)
                for h in range(2):
                    act.wait_ge(s_d, ONE + 2 * n + h + 1)
                    nc.scalar.activation(pre[:, HT * h:HT * (h + 1)], misc[1 - h][:, :], ACT.Identity, bias=v("dtb")
                                         ).then_inc(s_pre, 1)
                for h in range(2):
                    act.wait_ge(s_bc, ONE + 2 * n + h + 1)
                    if h == 0:
                        act.wait_ge(s_sp, ONE + 4 * n)
                    nc.scalar.activation(bcf[:, HT * h:HT * (h + 1)], misc[1 - h][:, :], ACT.Copy).then_inc(s_bce, 1)
                act.preload_act_table_set("natural_log_exp_and_others")
                act.wait_ge(s_min, ONE + n + 1)
                nc.scalar.activation(sp_[:, :], sp_[:, :], ACT.Exp).then_inc(s_el, 1)
                act.wait_ge(s_el, ONE + 2 * n + 1)
                nc.scalar.activation(sp_[:, :], sp_[:, :], ACT.Ln, bias=1.0).then_inc(s_el, 1)

            def decay(n, h, first=False):
                act.wait_ge(s_dt, ONE + n + 1)
                if not first:
                    act.wait_ge(s_st, ONE + 2 * STEPS * n - 2 * STEPS + STEPS * (h + 1))
                for i in range(HALF):
                    nc.scalar.activation(dA[:, h, i, :], dt[:, C:TOK], ACT.Exp,
                                         scale=negA[:, HALF * h + i:HALF * h + i + 1]).then_inc(s_a, 1)

            def evac(n):
                act.wait_ge(s_o, ONE + n + 1)
                act.wait_ge(s_os, ONE + 16 * n)
                nc.scalar.activation(xo[:, :, :].rearrange("c g (t k) -> c t g k", t=T),
                                     misc[1][:, :].rearrange("c (t g k) -> c t g k", t=T, g=G), ACT.Copy
                                     ).then_inc(s_oe, 1)

            front(0, 0)
            decay(0, 0, first=True)

            def body(n, par, first=False, last=False):
                decay(n, 1, first=first)
                if not first:
                    evac(n - 1)
                if not last:
                    front(n + 1, 1 - par)
                    decay(n + 1, 0)

            chunks(act, body)
            evac(NCH - 1)

        @block.vector
        def _(dve):
            dve.wait_ge(s_w, ONE + 16 * N_W)
            nc.vector.memset(wze[:, :, :], 0.0).then_inc(s_p1, 1)
            dve.wait_ge(s_p1, ONE + 1)
            for i in range(5):
                nc.vector.tensor_tensor(out=wtap[:, i], in0=wtap[:, i], in1=wx[:, :], op=ALU.mult)
            nc.vector.tensor_copy(wze[0:64, 0], wz[0:64, :])
            nc.vector.tensor_copy(wze[64:128, 1], wz[64:128, :])
            nc.vector.tensor_scalar(out=diag_d[:, :], in0=ident[:, :], scalar1=v("D"), scalar2=None, op0=ALU.mult)
            nc.vector.tensor_tensor(out=wdt[:, :], in0=wdt[:, :], in1=dtw[:, :], op=ALU.mult).then_inc(s_p1, 1)

            def front(n):
                dve.wait_ge(s_el, ONE + 2 * n + 2)
                nc.vector.tensor_tensor(out=dt[:, :], in0=pre[:, :], in1=sp_[:, :], op=ALU.max).then_inc(s_dt, 1)

            def gate(n, par):
                dve.wait_ge(s_y, ONE + 2 * n + 2)
                dve.wait_ge(s_ze, ONE + 2 * n + 2)
                nc.vector.tensor_tensor(out=ym[:, :], in0=acc[:, :], in1=zs[:, par].rearrange("c t m -> c (t m)"),
                                        op=ALU.mult).then_inc(s_ym, 1)

            front(0)

            def body(n, par, first=False, last=False):
                for h in range(2):
                    if h == 0:
                        dve.wait_ge(s_u, ONE + n + 1)
                    if not first:
                        dve.wait_ge(s_y, ONE + 2 * n - 2 + h + 1)
                    for i in range(HALF):
                        use = 32 * n + 16 * h + i
                        dve.wait_ge(s_rep, ONE + use + 1)
                        nc.vector.tensor_tensor(out=hh[:, h, i, :], in0=rep[i % 2][:, :], in1=uu[:, :], op=ALU.mult
                                                ).then_inc(s_use, 1)
                    dve.wait_ge(s_a, ONE + NS * n + HALF * (h + 1))
                    dve.wait_ge(s_use, ONE + 32 * n + 16 * h + HALF)
                    for t in range(1, T):
                        st = 2 * STEPS * n + STEPS * h + 2 * (t - 1)
                        if t > 1:
                            dve.wait_ge(s_st, ONE + st)
                        nc.vector.tensor_tensor(out=tmp[:, :, :], in0=dA[:, h, :, C * (t - 1):C * t],
                                                in1=hh[:, h, :, C * (t - 1):C * t], op=ALU.mult).then_inc(s_st, 1)
                        dve.wait_ge(s_st, ONE + st + 1)
                        nc.vector.tensor_tensor(out=hh[:, h, :, C * t:C * (t + 1)], in0=tmp[:, :, :],
                                                in1=hh[:, h, :, C * t:C * (t + 1)], op=ALU.add).then_inc(s_st, 1)
                        if h == 0 and t == 6 and not first:
                            gate(n - 1, 1 - par)
                        if h == 1 and t == 7 and not last:
                            front(n + 1)
                    dve.wait_ge(s_st, ONE + 2 * STEPS * n + STEPS * (h + 1))
                    for i in range(HALF):
                        use = 32 * n + 16 * h + HALF + i
                        dve.wait_ge(s_rep, ONE + use + 1)
                        nc.vector.tensor_tensor(out=hh[:, h, i, :], in0=rep[i % 2][:, :], in1=hh[:, h, i, :],
                                                op=ALU.mult).then_inc(s_use, 1)

            chunks(dve, body)
            gate(NCH - 1, (NCH - 1) % 2)

        @block.tensor
        def _(pe):
            pe.wait_ge(s_w, ONE + 16 * N_W)
            pe.wait_ge(s_p1, ONE + 2)
            pe.wait_ge(s_p2, ONE + 2)

            def turn(n):
                pe.wait_ge(s_yr, ONE + n + 1)
                pe.wait_ge(s_bce, ONE + 2 * n)
                pe.sem_inc(s_gate, 1)
                for q in range(4):
                    m = nc.tensor.transpose(misc[0][:, C * q:C * (q + 1)],
                                            yr[:, 2 * q:2 * q + 2].rearrange("c b g k -> c (b g k)"),
                                            ident[:, :])
                m.then_inc(s_t, 1)

            def pairs(out, w, shift, start, stop):
                m = 4 - shift
                return nc.tensor.matmul(out[:, C * shift:], w, yT[:, 0:m, :].rearrange("c q m -> c (q m)"),
                                        start=start, stop=stop)

            def conv_even(n):
                pe.wait_ge(s_te, ONE + n + 1)
                pe.wait_ge(s_oe, ONE + n - 1 if not isinstance(n, int) else ONE + max(n - 1, 0))
                pairs(misc[1], wtap[:, 4], 0, True, False)
                pairs(misc[1], wtap[:, 3], 1, False, False)
                pairs(misc[1], wtap[:, 2], 2, False, True).then_inc(s_x, 1)

            def conv_odd(n):
                pairs(misc[0], wtap[:, 1], 0, True, False)
                pairs(misc[0], wtap[:, 0], 1, False, True).then_inc(s_x, 1)

            def gates(n, h):
                pe.wait_ge(s_xe, ONE + 2 * n + h + 1)
                pairs(misc[1 - h], wze[:, h], 0, True, True).then_inc(s_z, 1)

            def steps(n, h):
                pe.wait_ge(s_xe, ONE + 2 * n + 2)
                pe.wait_ge(s_ze, ONE + 2 * n + h + 1)
                nc.tensor.matmul(misc[1 - h][:, :], wdt[:, :], xc[:, 4 * h:4 * h + 4, :].rearrange("c t m -> c (t m)"),
                                 start=True, stop=True).then_inc(s_d, 1)

            def bc(n, h):
                pe.wait_ge(s_pre, ONE + 2 * n + h + 1)
                nc.tensor.matmul(misc[1 - h][:, :], wbc[:, :], xc[:, 4 * h:4 * h + 4, :].rearrange("c t m -> c (t m)"),
                                 start=True, stop=True).then_inc(s_bc, 1)

            def front(n):
                return [lambda: turn(n), lambda: conv_even(n), lambda: conv_odd(n), lambda: gates(n, 0),
                        lambda: gates(n, 1), lambda: steps(n, 0), lambda: steps(n, 1), lambda: bc(n, 0),
                        lambda: bc(n, 1)]

            def repeat(n, par, i, first=False):
                h, c, s = i // 16, i // 8 % 2, i % 8
                if i == 0:
                    pe.wait_ge(s_bcs, ONE + 192 * n + 192)
                if not (first and i < 2):
                    pe.wait_ge(s_use, ONE + 32 * n + i - 1)
                for j in range(2):
                    m = nc.tensor.matmul(rep[i % 2][:, HT * j:HT * (j + 1)], pick[:, s],
                                         bcs[:, par, 2 * c + h, HT * j:HT * (j + 1)], start=True, stop=True)
                m.then_inc(s_rep, 1)

            def skip(n):
                pe.wait_ge(s_ym, ONE + n)
                for j in range(2):
                    m = nc.tensor.matmul(acc[:, HT * j:HT * (j + 1)], diag_d[:, :],
                                         xc[:, 4 * j:4 * j + 4, :].rearrange("c t m -> c (t m)"),
                                         start=True, stop=False)
                m.then_inc(s_yd, 1)

            def add(n, h, k):
                i, j = k // 2, k % 2
                if j == 0:
                    pe.wait_ge(s_use, ONE + 32 * n + 16 * h + HALF + i + 1)
                m = nc.tensor.matmul(acc[:, HT * j:HT * (j + 1)], ident[:, :], hh[:, h, i, HT * j:HT * (j + 1)],
                                     start=False, stop=(h == 1 and i == HALF - 1))
                if k == 2 * HALF - 1:
                    m.then_inc(s_y, 1)

            def project(n, fronts):
                pe.wait_ge(s_ym, ONE + n + 1)
                pe.wait_ge(s_bce, ONE + 2 * fronts)
                for t in range(T):
                    m = nc.tensor.matmul(misc[1][:, G * K * t:G * K * (t + 1)], ym[:, C * t:C * (t + 1)], wout[:, :],
                                         start=True, stop=True)
                m.then_inc(s_o, 1)

            for f in front(0):
                f()

            def body(n, par, first=False, last=False):
                rp = lambda i: repeat(n, par, i, first)
                for i in range(HALF):
                    rp(i)
                    if not first:
                        add(n - 1, 1, i)
                rp(8)
                rp(9)
                if not first:
                    for k in range(HALF, 2 * HALF):
                        add(n - 1, 1, k)
                    project(n - 1, n + 1)
                for i in range(10, 16):
                    rp(i)
                skip(n)
                for i in range(HALF):
                    rp(16 + i)
                    add(n, 0, i)
                rp(24)
                rp(25)
                rest = [lambda k=k: add(n, 0, k) for k in range(HALF, 2 * HALF)]
                parts = [] if last else front(n + 1)
                for k in range(max(len(rest), len(parts))):
                    if k < len(parts):
                        parts[k]()
                    if k < len(rest):
                        rest[k]()
                for i in range(26, 32):
                    rp(i)

            chunks(pe, body)
            for k in range(2 * HALF):
                add(NCH - 1, 1, k)
            pe.wait_ge(s_oe, ONE + NCH - 1)
            project(NCH - 1, NCH)


def normalise(nc, d, x3_dram, xr_dram, out):
    ctx = ExitStack()
    with ctx:
        def sb(name, shape, dt=FP32):
            return ctx.enter_context(nc.sbuf_tensor("c_" + name, shape, dt))

        sems = []

        def sem(name):
            sems.append(ctx.enter_context(nc.semaphore("c_" + name)))
            return sems[-1]

        red = [ctx.enter_context(nc.psum_tensor(f"c_red{i}", [C, 2], FP32)) for i in range(2)]
        S = 2
        vec = sb("vec", [C, NV])
        group = sb("group", [C, C])
        xr = sb("xr", [C, S, PIX])
        x3 = sb("x3", [C, S, PIX])
        res = sb("res", [C, S, PIX])
        stats = sb("stats", [C, S, 7, 6])
        mv = sb("mv", [C, S, 2])
        msq = sb("msq", [C, S, 2])
        var = sb("var", [C, S, 1])
        sc = sb("sc", [C, S, 1])
        rs = sb("rs", [C, S, 1])
        shift = sb("shift", [C, S, 1])
        eps = sb("eps", [C, 1])

        s_gate = sem("gate")
        s_w = sem("w")
        s_x = [sem("x0"), sem("x1")]
        s_st = sem("st")
        s_red = sem("red")
        s_m = sem("m")
        s_ln = sem("ln")
        s_sc = sem("sc")
        s_act = sem("act")
        s_res = sem("res")
        s_out = [sem("out0"), sem("out1")]

        def v(name):
            return vec[:, _V[name][0]:_V[name][0] + 1]

        N_W, LOADS, STATS = 2, 6, 9
        FREE = S
        block = ctx.enter_context(nc.Block())

        def images(eng, body):
            with eng.Fori(0, NB) as q:
                for g in range(G):
                    body(q * G + g, q, g, g % 2)

        @block.sync
        def _(sp):
            sp.dma_start(vec[:, :], d["vecs"]).then_inc(s_w, 16)
            sp.dma_start(group[:, :], d["group"]).then_inc(s_w, 16)

            def body(b, q, g, u):
                sp.wait_ge(s_res, ONE + FREE + b - 1)
                chunk = xr_dram[bass.ds(q * CHUNKS, CHUNKS), :, g, :].rearrange("j c p -> c j p")
                sp.dma_start(xr[0:64, u, 0:PIX - WPIX].rearrange("c (j p) -> c j p", p=CPX),
                             chunk[0:64, 0:CHUNKS - 1, :]).then_inc(s_x[u], 16)
                sp.dma_start(xr[0:64, u, PIX - WPIX:PIX], chunk[64:128, 0, 0:WPIX]).then_inc(s_x[u], 16)
                sp.dma_start(xr[64:128, u, 0:WPIX], chunk[64:128, 0, WPIX:CPX]).then_inc(s_x[u], 16)
                sp.dma_start(xr[64:128, u, WPIX:PIX].rearrange("c (j p) -> c j p", p=CPX), chunk[64:128, 1:CHUNKS, :]
                             ).then_inc(s_x[u], 16)
                for two in range(2):
                    sp.dma_start(x3[64 * two:64 * two + 64, u, :],
                                 x3_dram[bass.ds(b, 1)].rearrange("a (r two) p -> two r (a p)", two=2)[two]
                                 ).then_inc(s_x[u], 16)

            images(sp, body)

        @block.gpsimd
        def _(pool):
            for x in sems:
                pool.sem_inc(x, ONE)
            pool.sem_inc(s_res, FREE)
            for x in s_out:
                pool.sem_inc(x, 32)

        @block.tensor
        def _(pe):
            pe.wait_ge(s_w, ONE + 16 * N_W)

            def body(b, q, g, u):
                pe.wait_ge(s_st, ONE + STATS * (b + 1))
                nc.tensor.matmul(red[u][:, :], group[:, :], mv[:, u], start=True, stop=True).then_inc(s_red, 1)

            images(pe, body)

        @block.scalar
        def _(act):
            act.wait_ge(s_w, ONE + 16 * N_W)

            def store(b, u):
                act.wait_ge(s_res, ONE + FREE + b + 1)
                for two in range(2):
                    act.dma_start(out[bass.ds(b, 1)].rearrange("a (r two) p -> two r (a p)", two=2)[two],
                                  res[64 * two:64 * two + 64, u, :]).then_inc(s_out[u], 16)

            def body(b, q, g, u):
                act.preload_act_table_set("natural_log_exp_and_others")
                act.wait_ge(s_m, ONE + 2 * b + 2)
                nc.scalar.activation(rs[:, u], var[:, u], ACT.Ln, bias=eps[:, 0:1], scale=-1.0).then_inc(s_ln, 1)
                act.wait_ge(s_ln, ONE + 2 * b + 1)
                nc.scalar.activation(rs[:, u], rs[:, u], ACT.Exp, scale=-0.5).then_inc(s_ln, 1)
                act.wait_ge(s_sc, ONE + 3 * b + 3)
                act.wait_ge(s_out[u], ONE + 32 * (2 * q + g // 2 + 1))
                nc.scalar.activation(res[:, u, :], xr[:, u, :], ACT.Silu, bias=shift[:, u], scale=sc[:, u]
                                     ).then_inc(s_act, 1)
                store(b, u)

            images(act, body)
            for x in s_out:
                act.wait_ge(x, ONE + 32 + 32 * IMGS // 2)

        @block.vector
        def _(dve):
            dve.wait_ge(s_w, ONE + 16 * N_W)
            nc.vector.memset(eps[:, :], EPS_GN)

            def body(b, q, g, u):
                dve.wait_ge(s_x[u], ONE + 16 * LOADS * (2 * q + g // 2 + 1))
                for j in range(7):
                    nc.vector.bn_stats(out=stats[:, u, j, :], in_=xr[:, u, STRIP * j:STRIP * (j + 1)]
                                       ).then_inc(s_st, 1)
                dve.wait_ge(s_st, ONE + STATS * b + 7)
                dve.sem_inc(s_gate, 1)
                nc.vector.bn_aggr(out=mv[:, u], in_=stats[:, u].rearrange("c j k -> c (j k)")).then_inc(s_st, 1)
                dve.wait_ge(s_st, ONE + STATS * b + 8)
                nc.vector.scalar_tensor_tensor(out=mv[:, u, 1:2], in0=mv[:, u, 0:1], scalar=mv[:, u, 0:1],
                                               in1=mv[:, u, 1:2], op0=ALU.mult, op1=ALU.add).then_inc(s_st, 1)
                dve.wait_ge(s_red, ONE + b + 1)
                nc.vector.tensor_copy(msq[:, u], red[u][:, :]).then_inc(s_m, 1)
                dve.wait_ge(s_m, ONE + 2 * b + 1)
                nc.vector.scalar_tensor_tensor(out=var[:, u], in0=msq[:, u, 0:1], scalar=msq[:, u, 0:1],
                                               in1=msq[:, u, 1:2], op0=ALU.mult, op1=ALU.subtract,
                                               ).then_inc(s_m, 1)
                dve.wait_ge(s_ln, ONE + 2 * b + 2)
                nc.vector.tensor_tensor(out=sc[:, u], in0=rs[:, u], in1=v("gn_w"), op=ALU.mult).then_inc(s_sc, 1)
                dve.wait_ge(s_sc, ONE + 3 * b + 1)
                nc.vector.tensor_tensor(out=shift[:, u], in0=msq[:, u, 0:1], in1=sc[:, u], op=ALU.mult
                                        ).then_inc(s_sc, 1)
                dve.wait_ge(s_sc, ONE + 3 * b + 2)
                nc.vector.tensor_tensor(out=shift[:, u], in0=v("gn_b"), in1=shift[:, u], op=ALU.subtract
                                        ).then_inc(s_sc, 1)
                dve.wait_ge(s_act, ONE + b + 1)
                nc.vector.tensor_tensor(out=res[:, u, :], in0=res[:, u, :], in1=x3[:, u, :], op=ALU.add
                                        ).then_inc(s_res, 1)

            images(dve, body)


TAP_PAIRS = ((0, 1), (2, 3), (None, 0), (1, 2), (3, None))


def program(nc, d, out):
    x3_dram = nc.dram_tensor("x3", (IMGS, C, PIX), FP32).ap()
    ys_dram = nc.dram_tensor("ys", (NB, CHUNKS, C, G, CPX), FP32).ap()
    xr_dram = nc.dram_tensor("xr", (NB * CHUNKS, C, G, CPX), FP32).ap()
    layer0(nc, d, x3_dram, ys_dram)
    sequences(nc, d, ys_dram.rearrange("q j c g p -> (q j) c g p"), xr_dram)
    normalise(nc, d, x3_dram, xr_dram, out.rearrange("b c h w -> b c (h w)"))


def kernel(**inputs):
    import numpy as np
    import concourse.bacc as bacc
    from concourse.bass_utils import run_bass_kernel_spmd as run

    a = {n: np.asarray(x) for n, x in inputs.items()}
    f32 = np.float32
    even_odd = np.r_[0:C:2, 1:C:2]
    L0, L1 = "L0_conv_", "L1_conv_"

    cols = {
        "pos_w": a[L0 + "pos_w"].reshape(C, 9), "pos_b": a[L0 + "pos_b"].reshape(C, 1),
        "g1": a[L0 + "ln1_g"].reshape(C, 1), "b1": a[L0 + "ln1_b"].reshape(C, 1),
        "qkv_b": a[L0 + "qkv_b"].reshape(3, C).T,
        "lepe_w": a[L0 + "lepe_w"].reshape(C, 25), "lepe_b": a[L0 + "lepe_b"].reshape(C, 1),
        "wo_b": a[L0 + "wo_b"].reshape(C, 1), "g2": a[L0 + "ln2_g"].reshape(C, 1), "b2": a[L0 + "ln2_b"].reshape(C, 1),
        "mb1": a[L0 + "mlp_b1"].reshape(MLP, C).T, "mb2": a[L0 + "mlp_b2"].reshape(C, 1),
        "conv_b": a[L1 + "conv_b"][even_odd].reshape(C, 1),
        "gn_w": a[L1 + "gn_w"][even_odd].reshape(C, 1), "gn_b": a[L1 + "gn_b"][even_odd].reshape(C, 1),
        "c1b": np.tile(a[L1 + "conv1d_b"], G).reshape(C, 1), "dtb": np.tile(a[L1 + "dt_proj_b"], G).reshape(C, 1),
        "D": np.tile(a[L1 + "D"], G).reshape(C, 1), "alog": np.tile(a[L1 + "A_log"], (G, 1)),
        "headmask": np.where(np.arange(C)[:, None] // HD == np.arange(HEADS)[None, :], SCALE, 0.0).astype(f32),
        "rowmask": (np.arange(C)[:, None] // WPIX == np.arange(2)[None, :]).astype(f32),
    }
    vecs = np.concatenate([cols[n] for n in _V], axis=1)
    w_in = a[L1 + "in_proj_w"]
    wx, wz = np.zeros((2, G, K, G, DI), f32), np.zeros((2, G, K, G, DI), f32)
    taps = np.zeros((5, 2, G, K, G, DI), f32)
    x_proj = a[L1 + "x_proj_w"]
    xp_dt, dt_w = np.zeros((G, DI, G, DI), f32), np.zeros((G, DI, G, DI), f32)
    xp_bc = np.zeros((G, DI, 4, G, HALF), f32)
    w_out = np.zeros((G, DI, G, K), f32)
    pick = np.zeros((3, G, HALF, HALF, G, DI), f32)
    cw = a[L1 + "conv1d_w"][:, 0, :]
    for g in range(G):
        for blk in range(2):
            wx[blk, g, :, g, :] = w_in[0:DI].T
            wz[blk, g, :, g, :] = w_in[DI:2 * DI].T
        for m, pair in enumerate(TAP_PAIRS):
            for blk in range(2):
                if pair[blk] is not None:
                    taps[m, blk, g, :, g, :] = cw[:, pair[blk]][None, :]
        xp_dt[g, :, g, :] = x_proj[0][:, None]
        dt_w[g, :, g, :] = a[L1 + "dt_proj_w"][:, 0][None, :]
        for m in range(4):
            at = 1 + NS * (m // 2) + HALF * (m % 2)
            xp_bc[g, :, m, g, :] = x_proj[at:at + HALF].T
        w_out[g, :, g, :] = a[L1 + "out_proj_w"].T
        for n in range(HALF):
            pick[:, g, n, n, g, :] = 1.0
    eye = np.eye(C, dtype=f32)
    rows = np.arange(C) % 64 // 16
    data = {
        "x": a["x"], "vecs": vecs, "ident": eye,
        "centre": (eye - f32(1.0 / C)).astype(f32), "mean": np.full((C, C), 1.0 / C, f32),
        "fold": np.concatenate([np.eye(WPIX, dtype=f32)] * 2, axis=0),
        "qkv_w": a[L0 + "qkv_w"], "wo_w": a[L0 + "wo_w"], "mlp_w1": a[L0 + "mlp_w1"], "mlp_w2": a[L0 + "mlp_w2"],
        "conv_w": np.transpose(a[L1 + "conv_w"], (1, 2, 3, 0)).reshape(C, 9, C)[:, :, even_odd],
        "wx": wx.reshape(C, C), "wz": wz.reshape(C, C), "taps": np.transpose(taps.reshape(5, C, C), (1, 0, 2)),
        "xp_dt": xp_dt.reshape(C, C), "dt_w": dt_w.reshape(C, C), "xp_bc": xp_bc.reshape(C, C),
        "w_out": w_out.reshape(C, G * K), "pick": pick.reshape(3 * G * HALF, HALF * C),
        "group": ((rows[:, None] == rows[None, :]) / 32.0).astype(f32),
    }
    nc = bacc.Bacc("TRN2", target_bir_lowering=False, num_devices=1)
    d, arrays = {}, {}
    for name, x in data.items():
        x = np.ascontiguousarray(x)
        arrays[f"in_{name}"] = x
        d[name] = nc.dram_tensor(f"in_{name}", x.shape, mybir.dt.from_np(x.dtype), kind="ExternalInput").ap()
    out = nc.dram_tensor("out", (IMGS, C, H, W), FP32, kind="ExternalOutput").ap()
    program(nc, d, out)
    return run(nc, [arrays], core_ids=[0]).results[0]["out"]
```

```python
from contextlib import ExitStack

import concourse.bass as bass
from concourse import mybir

FP32 = mybir.dt.float32
BF16 = mybir.dt.bfloat16
U32 = mybir.dt.uint32
ALU = mybir.AluOpType
ACT = mybir.ActivationFunctionType
AXX = mybir.AxisListType.X

IMGS, C, H, W = 16, 128, 56, 56
PIX = H * W
NWIN, WS = 7, 8
WPIX = WS * WS
P2 = NWIN * NWIN
STRIP = WS * W
HEADS, HD, TOPK = 4, 32, 4
SCALE = float(C) ** -0.5
MLP = 3
POS_TAPS, LEPE_TAPS = 9, 25
T, K, DI, NS, G = 8, 16, 32, 16, 4
CPX = T * K
CHUNKS = (PIX + WPIX) // CPX
SPX = CHUNKS * CPX
ONE = 1
TOK = T * C
HALF = NS // 2
NB = IMGS // G
EPS_LN, EPS_GN = 1e-6, 1e-5

_V = {}


def _columns():
    at = 0
    for name, n in (("pos_w", 9), ("pos_b", 1), ("g1", 1), ("b1", 1), ("qkv_b", 3), ("lepe_w", 25), ("lepe_b", 1),
                    ("wo_b", 1), ("g2", 1), ("b2", 1), ("mb1", 3), ("mb2", 1), ("conv_b", 1), ("gn_w", 1), ("gn_b", 1),
                    ("c1b", 1), ("dtb", 1), ("D", 1), ("alog", NS), ("headmask", 4), ("rowmask", 2)):
        _V[name] = (at, n)
        at += n
    return at


NV = _columns()


def layer0(nc, d, x3_dram, ys_dram):
    ctx = ExitStack()
    with ctx:
        def sb(name, shape, dt=FP32):
            return ctx.enter_context(nc.sbuf_tensor(name, shape, dt))

        sems = []

        def sem(name):
            sems.append(ctx.enter_context(nc.semaphore(name)))
            return sems[-1]

        bank = [ctx.enter_context(nc.psum_tensor(f"bank{i}", [C, 512], FP32)) for i in range(8)]

        vec = sb("vec", [C, NV])
        ident = sb("ident", [C, C])
        centre = sb("centre", [C, C])
        mean = sb("mean", [C, C])
        fold = sb("fold", [C, WPIX])
        wqkv = sb("wqkv", [C, 3 * C])
        wo = sb("wo", [C, C])
        w1 = sb("w1", [C, MLP * C])
        w2 = sb("w2", [C, MLP, C])
        wconv = sb("wconv", [C, 9, C])
        fb = sb("fb", [C, 6])
        obias = sb("obias", [C, 1])
        epsc = sb("epsc", [C, 1])
        wc1 = sb("wc1", [C, 1])

        xpad = sb("xpad", [C, H + 2, W + 2])
        x1 = sb("x1", [C, H, W])
        qs = sb("qs", [C, P2, WPIX])
        ks = sb("ks", [C, P2 * WPIX])
        vt = sb("vt", [WPIX, P2 * C])
        vpad = sb("vpad", [C, H + 4, W + 4])
        oacc = sb("oacc", [C, H, W])
        att = sb("att", [C, P2, WPIX])
        xn2 = att
        x3pad = sb("x3pad", [C, H + 2, W + 2])
        ysb = sb("ysb", [C, SPX])

        sq = sb("sq", [C, 2, STRIP])
        lnv = sb("lnv", [C, STRIP])
        rstd = sb("rstd", [C, 2, STRIP])
        xn = sb("xn", [C, 2, NWIN, WPIX])
        xw = sb("xw", [C, P2])
        qw = sb("qw", [C, 2, P2])
        lg = sb("lg", [P2, P2])
        mx8 = sb("mx8", [P2, 8])
        ix8 = sb("ix8", [P2, 8], U32)
        ixrow = sb("ixrow", [1, P2 * TOPK], U32)
        qbd = sb("qbd", [C, 2, 4, WPIX])
        nmax = sb("nmax", [C, 2, 2])
        prob = sb("prob", [C, 2, 2, 256])
        psums = sb("psums", [C, 2, 2])
        rinv = sb("rinv", [C, 2, 2])
        rmask = sb("rmask", [C, 2, 2, 2])
        ksel = sb("ksel", [C, 2, TOPK * WPIX])
        vsel = sb("vsel", [2 * WPIX, 2, TOPK // 2, C])
        pT = sb("pT", [2 * WPIX, 2, 4, C])
        on = sb("on", [C, 2, C])
        hid = sb("hid", [C, 2, MLP, STRIP])

        s_gate = sem("s_gate")
        s_w = sem("s_w")
        s_prep = sem("s_prep")
        s_fb = sem("s_fb")
        s_oz = sem("s_oz")
        s_fold = sem("s_fold")
        s_x = sem("s_x")
        s_pos = sem("s_pos")
        s_cen = sem("s_cen")
        s_sq = sem("s_sq")
        s_var = sem("s_var")
        s_ln = sem("s_ln")
        s_rs = sem("s_rs")
        s_xn = sem("s_xn")
        s_q = sem("s_q")
        s_vt = sem("s_vt")
        s_qk = sem("s_qk")
        s_v = sem("s_v")
        s_xw = sem("s_xw")
        s_qw = sem("s_qw")
        s_qwe = sem("s_qwe")
        s_lg = sem("s_lg")
        s_top = sem("s_top")
        s_ix = sem("s_ix")
        s_bd = sem("s_bd")
        s_vs = [sem("s_vs0"), sem("s_vs1")]
        s_s = sem("s_s")
        s_m = sem("s_m")
        s_p = sem("s_p")
        s_ri = sem("s_ri")
        s_pt = sem("s_pt")
        s_pte = sem("s_pte")
        s_o = sem("s_o")
        s_on = sem("s_on")
        s_of = sem("s_of")
        s_oa = sem("s_oa")
        s_lepe = sem("s_lepe")
        s_wo = sem("s_wo")
        s_x2 = sem("s_x2")
        s_xn2 = sem("s_xn2")
        s_h = sem("s_h")
        s_g = sem("s_g")
        s_y2 = sem("s_y2")
        s_x3 = sem("s_x3")
        s_pad = sem("s_pad")
        s_cv = sem("s_cv")
        s_ys = sem("s_ys")
        s_zero = sem("s_zero")
        s_x3o = sem("s_x3o")
        s_yso = sem("s_yso")

        def v(name, i=0, n=1, rows=slice(None)):
            at = _V[name][0] + i
            return vec[rows, at:at + n]

        SN = NWIN
        NW = P2
        LQ = 4
        LROWS = H // LQ
        LEPES = LEPE_TAPS * LQ
        LEAD, BODY = 5, 8
        PTAPS = [(k // 3 - 1, k % 3 - 1) for k in range(POS_TAPS)]
        N_W = 10

        def chosen(engine, w):
            return nc.values_load_multi_w_load_instructions(
                ixrow[0:1, bass.ds(w * TOPK, TOPK)], engines=[engine], min_val=0, max_val=P2 - 1)[1]

        block = ctx.enter_context(nc.Block())

        @block.sync
        def _(sp):
            for dst, src in ((vec, "vecs"), (ident, "ident"), (centre, "centre"), (mean, "mean"), (fold, "fold"),
                             (wqkv, "qkv_w"), (wo, "wo_w"), (w1, "mlp_w1")):
                sp.dma_start(dst[:, :], d[src]).then_inc(s_w, 16)
            sp.dma_start(w2[:, :, :], d["mlp_w2"].rearrange("(j p) n -> p j n", p=C)).then_inc(s_w, 16)
            sp.dma_start(wconv[:, :, :], d["conv_w"]).then_inc(s_w, 16)
            sp.wait_ge(s_zero, ONE + 1)
            with sp.Fori(0, NB) as bq:
                with sp.Fori(0, G) as bg:
                    b = bq * G + bg
                    sp.wait_ge(s_pos, ONE + b * POS_TAPS)
                    sp.dma_start(xpad[:, 1:H + 1, 1:W + 1],
                                 d["x"][bass.ds(b, 1)].rearrange("a c h w -> c (a h) w")).then_inc(s_x, 16)
                    sp.wait_ge(s_top, ONE + 3 * (b + 1))
                    sp.dma_start(ixrow[0:1, :].rearrange("a (p k) -> a p k", k=TOPK), ix8[:, 0:TOPK]
                                 ).then_inc(s_ix, 16)
                    sp.wait_ge(s_ix, ONE + 16 * (b + 1))
                    sp.wait_ge(s_v, ONE + 3 * SN * (b + 1))
                    sp.sem_inc(s_gate, 1)

                    def gather(w, u, k, first=False):
                        at = chosen(mybir.EngineType.SP, w)
                        sp.wait_ge(s_o, ONE + b * NW if first else ONE + b * NW + w - 1)
                        for t in range(TOPK):
                            sp.dma_start(vsel[WPIX * (t % 2):WPIX * (t % 2 + 1), u, t // 2, :],
                                         vt[:, bass.ds(at[t] * C, C)]).then_inc(s_vs[u], 16)

                    gather(0, 0, 0, True)
                    with sp.Fori(0, (NW - 1) // 2) as k:
                        for i in range(2):
                            gather(k * 2 + i + 1, (i + 1) % 2, k)
                    sp.wait_ge(s_x3, ONE + SN * (b + 1))
                    sp.dma_start(x3_dram[bass.ds(b, 1)].rearrange("a c p -> c (a p)"),
                                 x1[:, :, :].rearrange("c h w -> c (h w)")).then_inc(s_x3o, 16)
            sp.wait_ge(s_x3o, ONE + 16 * IMGS)

        @block.gpsimd
        def _(pool):
            for x in sems:
                pool.sem_inc(x, ONE)
            nc.gpsimd.memset(vpad[:, :, :], 0.0)
            nc.gpsimd.memset(ysb[:, :], 0.0)
            nc.gpsimd.memset(epsc[:, :], EPS_LN)
            nc.gpsimd.memset(x3pad[:, :, :], 0.0)
            nc.gpsimd.memset(xpad[:, :, :], 0.0).then_inc(s_zero, 1)
            pool.wait_ge(s_w, ONE + 16 * N_W)

            def query_block(b, w, u, first):
                at = chosen(mybir.EngineType.Pool, w)
                if not first:
                    pool.wait_ge(s_s, ONE + b * NW + w - 1)
                nc.gpsimd.tensor_tensor(
                    out=qbd[:, u], in0=qs[:, bass.ds(w, 1), :].broadcast_to([C, 4, WPIX]),
                    in1=v("headmask", 0, 4).unsqueeze(2).broadcast_to([C, 4, WPIX]),
                    op=ALU.mult).then_inc(s_bd, 1)
                for t in range(TOPK):
                    m = nc.gpsimd.tensor_copy(ksel[:, u, WPIX * t:WPIX * (t + 1)], ks[:, bass.ds(at[t] * WPIX, WPIX)])
                m.then_inc(s_bd, 1)

            with pool.Fori(0, NB) as bq:
                with pool.Fori(0, G) as bg:
                    b = bq * G + bg
                    pool.wait_ge(s_lepe, ONE + LQ + b * LEPES)
                    pool.wait_ge(s_wo, ONE + b * SN)
                    pool.sem_inc(s_gate, 1)
                    nc.gpsimd.memset(oacc[:, :, :], 0.0).then_inc(s_oz, 1)
                    pool.wait_ge(s_qk, ONE + 2 * SN * (b + 1))
                    pool.wait_ge(s_ix, ONE + 16 * (b + 1))
                    pool.sem_inc(s_gate, 1)
                    query_block(b, 0, 0, True)
                    with pool.Fori(0, (NW - 1) // 2) as k:
                        for i in range(2):
                            query_block(b, k * 2 + i + 1, (i + 1) % 2, False)
                    pool.wait_ge(s_x3, ONE + SN * (b + 1))
                    pool.sem_inc(s_gate, 1)
                    nc.gpsimd.tensor_copy(x3pad[:, 1:H + 1, 1:W + 1], x1[:, :, :]).then_inc(s_pad, 1)

        @block.scalar
        def _(act):
            act.wait_ge(s_zero, ONE + 1)
            act.wait_ge(s_w, ONE + 16 * N_W)
            act.wait_ge(s_fold, ONE + 1)
            for j in range(3):
                nc.scalar.activation(fb[:, j:j + 1], bank[0][:, j:j + 1], ACT.Identity, bias=v("qkv_b", j))
            for j in range(3):
                m = nc.scalar.activation(fb[:, 3 + j:4 + j], bank[0][:, 3 + j:4 + j], ACT.Identity, bias=v("mb1", j))
            m.then_inc(s_fb, 1)
            act.wait_ge(s_fb, ONE + 1)

            def norm(b, s, second):
                n = b * 2 * SN + s + SN * second + 1
                act.wait_ge(s_cen, ONE + n)
                nc.scalar.activation(sq[:, s % 2], bank[s % 2][:, 0:STRIP], ACT.Square).then_inc(s_sq, 1)
                act.wait_ge(s_var, ONE + n)
                nc.scalar.activation(lnv[:, :], bank[2][:, 0:STRIP], ACT.Ln, bias=epsc[:, 0:1]).then_inc(s_ln, 1)
                act.wait_ge(s_ln, ONE + n)
                if s >= 2:
                    act.wait_ge(s_xn2 if second else s_xn, b * SN + s - 1)
                nc.scalar.activation(rstd[:, s % 2], lnv[:, :], ACT.Exp, scale=-0.5).then_inc(s_rs, 1)

            def window(b, w, par, i=None):
                n = b * NW + w
                u = (par + 1) % 2
                if i is None or 1 <= i <= NW:
                    act.wait_ge(s_pt, ONE + n)
                    if i is None or i >= 3:
                        act.wait_ge(s_o, ONE + n - 2)
                    nc.scalar.activation(pT[:, u].rearrange("k i m -> k (i m)"), bank[2 + u][:, :], ACT.Identity
                                         ).then_inc(s_pte, 1)
                if i is None or i < NW:
                    u = par
                    act.wait_ge(s_m, ONE + n + 1)
                    if i is None or i >= 2:
                        act.wait_ge(s_ri, ONE + 2 * n - 2)
                    for hp in range(2):
                        nc.scalar.activation(prob[:, u, hp], bank[u][:, 256 * hp:256 * hp + 256], ACT.Exp,
                                             bias=nmax[:, u, hp:hp + 1], accum_out=psums[:, u, hp:hp + 1]
                                             ).then_inc(s_p, 1)

            with act.Fori(0, NB) as bq:
                with act.Fori(0, G) as bg:
                    b = bq * G + bg
                    act.preload_act_table_set("natural_log_exp_and_others")
                    norm(b, 0, 0)
                    for s in range(SN):
                        if s + 1 < SN:
                            norm(b, s + 1, 0)
                        act.wait_ge(s_q, ONE + b * 3 * SN + 3 * s + 1)
                        nc.scalar.activation(qs[:, NWIN * s:NWIN * (s + 1), :].rearrange("c w k -> c (w k)"),
                                             bank[3][:, 0:STRIP], ACT.Identity, bias=fb[:, 0:1]).then_inc(s_qk, 1)
                        act.wait_ge(s_q, ONE + b * 3 * SN + 3 * s + 2)
                        nc.scalar.activation(ks[:, STRIP * s:STRIP * (s + 1)], bank[4][:, 0:STRIP],
                                             ACT.Identity, bias=fb[:, 1:2]).then_inc(s_qk, 1)
                    act.wait_ge(s_qw, ONE + 2 * b + 2)
                    for j in range(2):
                        nc.scalar.activation(qw[:, j], bank[0][:, j * 64:j * 64 + P2], ACT.Identity,
                                             bias=fb[:, j:j + 1], scale=1.0 / WPIX).then_inc(s_qwe, 1)
                    for w in range(LEAD):
                        window(b, w, w % 2, w)
                    with act.Fori(0, (NW - LEAD) // 2) as k:
                        for i in range(2):
                            window(b, k * 2 + i + LEAD, (LEAD + i) % 2)
                    window(b, NW, NW % 2, NW)
                    for s in range(SN):
                        norm(b, s, 1)
                    for s in range(SN):
                        for j in range(MLP):
                            act.wait_ge(s_h, ONE + b * MLP * SN + s * MLP + j + 1)
                            if s >= 2:
                                act.wait_ge(s_y2, ONE + b * SN + s - 1)
                            nc.scalar.activation(hid[:, s % 2, j], bank[3 + j][:, 0:STRIP], ACT.Gelu,
                                                 bias=fb[:, 3 + j:4 + j]).then_inc(s_g, 1)
                    act.wait_ge(s_yso, ONE + 16 * b)
                    for s in range(SN):
                        act.wait_ge(s_cv, ONE + b * SN + s + 1)
                        p = bank[s % 2]
                        at = s * STRIP
                        lo, up = slice(0, 64), slice(64, 128)
                        n = STRIP if s < SN - 1 else STRIP - WPIX
                        nc.scalar.activation(ysb[lo, at:at + n], p[lo, 0:n], ACT.Identity, bias=v("conv_b", rows=lo))
                        if n < STRIP:
                            nc.scalar.activation(ysb[up, 0:WPIX], p[lo, n:STRIP], ACT.Identity,
                                                 bias=v("conv_b", rows=lo))
                        nc.scalar.activation(ysb[up, WPIX + at:WPIX + at + STRIP], p[up, 0:STRIP], ACT.Identity,
                                             bias=v("conv_b", rows=up)).then_inc(s_ys, 1)
                    act.wait_ge(s_ys, ONE + SN * (b + 1))
                    act.dma_start(ys_dram[bass.ds(bq, 1), :, :, bass.ds(bg, 1), :].rearrange("q j c g p -> c (q j g) p"),
                                  ysb[:, :].rearrange("c (j p) -> c j p", p=CPX)).then_inc(s_yso, 16)
            act.wait_ge(s_yso, ONE + 16 * IMGS)

        @block.vector
        def _(dve):
            dve.wait_ge(s_w, ONE + 16 * N_W)
            dve.wait_ge(s_fold, ONE + 1)
            nc.vector.tensor_scalar(out=wqkv[:, :], in0=wqkv[:, :], scalar1=v("g1"), scalar2=None, op0=ALU.mult)
            nc.vector.tensor_scalar(out=w1[:, :], in0=w1[:, :], scalar1=v("g2"), scalar2=None, op0=ALU.mult)
            nc.vector.tensor_scalar(out=wc1[:, :], in0=v("pos_w", 4), scalar1=1.0, scalar2=None, op0=ALU.add
                                    ).then_inc(s_prep, 1)
            dve.wait_ge(s_fb, ONE + 1)
            nc.vector.tensor_tensor(out=obias[:, :], in0=fb[:, 2:3], in1=v("lepe_b"), op=ALU.add).then_inc(s_prep, 1)
            dve.wait_ge(s_prep, ONE + 2)

            dve.sem_inc(s_lepe, LQ)

            def lepe(b, dy, dx, part):
                src = vpad[:, bass.ds(dy + part * LROWS, LROWS), dx:dx + W]
                dst = oacc[:, part * LROWS:(part + 1) * LROWS, :]
                dve.wait_ge(s_lepe, ONE + b * LEPES + (dy * 5 + dx) * LQ + part + 1)
                nc.vector.scalar_tensor_tensor(out=dst, in0=src, scalar=vec[:, bass.ds(dy * 5 + dx + _V["lepe_w"][0], 1)],
                                               in1=dst, op0=ALU.mult, op1=ALU.add).then_inc(s_lepe, 1)

            def window(b, w, par, i=None, extra=()):
                n = b * NW + w
                if i is None or i < NW:
                    u = par
                    dve.wait_ge(s_s, ONE + n + 1)
                    if i is None or i >= 2:
                        dve.wait_ge(s_p, ONE + 2 * n - 2)
                    nc.vector.tensor_reduce(out=nmax[:, u], in_=bank[u][:, :].rearrange("c (h k) -> c h k", h=2),
                                            axis=AXX, op=ALU.max, negate=True).then_inc(s_m, 1)
                for f in extra:
                    f()
                if i is None or 1 <= i <= NW:
                    u = (par + 1) % 2
                    dve.wait_ge(s_p, ONE + 2 * n)
                    nc.vector.reciprocal(rinv[:, u], psums[:, u]).then_inc(s_ri, 1)
                    dve.wait_ge(s_ri, ONE + 2 * n - 1)
                    nc.vector.tensor_tensor(out=rmask[:, u], in0=rinv[:, u].unsqueeze(2).broadcast_to([C, 2, 2]),
                                            in1=v("rowmask", 0, 2).unsqueeze(1).broadcast_to([C, 2, 2]),
                                            op=ALU.mult).then_inc(s_ri, 1)
                if i is None or 2 <= i <= NW + 1:
                    u = par
                    dve.wait_ge(s_ri, ONE + 2 * n - 2)
                    dve.wait_ge(s_o, ONE + n - 1)
                    if i is None or i >= 4:
                        dve.wait_ge(s_of, ONE + n - 3)
                    nc.vector.tensor_tensor(
                        out=on[:, u].rearrange("c (a k) -> c a k", k=HD),
                        in0=bank[4 + u][:, 0:C].rearrange("c (a k) -> c a k", k=HD),
                        in1=rmask[:, u].rearrange("c a k -> c (a k)").unsqueeze(2).broadcast_to([C, 4, HD]),
                        op=ALU.mult).then_inc(s_on, 1)
                if i is None or 3 <= i <= NW + 2:
                    u = (par + 1) % 2
                    dve.wait_ge(s_of, ONE + n - 2)
                    nc.vector.tensor_scalar(out=att[:, bass.ds(w - 3, 1), :].rearrange("c a k -> c (a k)"),
                                            in0=bank[6 + u][:, 0:WPIX], scalar1=obias[:, 0:1], scalar2=None,
                                            op0=ALU.add).then_inc(s_oa, 1)

            with dve.Fori(0, NB) as bq:
                with dve.Fori(0, G) as bg:
                    b = bq * G + bg
                    dve.wait_ge(s_x, ONE + 16 * (b + 1))
                    dve.wait_ge(s_x3o, ONE + 16 * b)
                    dve.wait_ge(s_pad, ONE + b)
                    nc.vector.tensor_scalar(out=x1[:, :, :], in0=xpad[:, 1:H + 1, 1:W + 1], scalar1=wc1[:, 0:1],
                                            scalar2=v("pos_b"), op0=ALU.mult, op1=ALU.add).then_inc(s_pos, 1)
                    n = 1
                    for k, (dy, dx) in enumerate(PTAPS):
                        if (dy, dx) == (0, 0):
                            continue
                        dve.wait_ge(s_pos, ONE + b * POS_TAPS + n)
                        nc.vector.scalar_tensor_tensor(
                            out=x1[:, :, :], in0=xpad[:, 1 + dy:1 + dy + H, 1 + dx:1 + dx + W],
                            scalar=v("pos_w", k), in1=x1[:, :, :], op0=ALU.mult, op1=ALU.add).then_inc(s_pos, 1)
                        n += 1

                    def by_window(ap):
                        return ap.rearrange("c (y w x) -> c w y x", y=WS, w=NWIN)

                    def normalise(s):
                        dve.wait_ge(s_rs, ONE + b * 2 * SN + s + 1)
                        if s >= 2:
                            dve.wait_ge(s_vt, ONE + b * 2 * SN + 2 * (s - 1))
                        nc.vector.tensor_tensor(out=xn[:, s % 2].rearrange("c w (y x) -> c w y x", y=WS),
                                                in0=by_window(bank[s % 2][:, 0:STRIP]), in1=by_window(rstd[:, s % 2]),
                                                op=ALU.mult).then_inc(s_xn, 1)

                    normalise(0)
                    for s in range(SN):
                        if s + 1 < SN:
                            normalise(s + 1)
                        dve.wait_ge(s_xn, ONE + b * SN + s + 1)
                        nc.vector.tensor_reduce(out=xw[:, NWIN * s:NWIN * (s + 1)], in_=xn[:, s % 2], axis=AXX,
                                                op=ALU.add).then_inc(s_xw, 1)
                        dve.wait_ge(s_q, ONE + b * 3 * SN + 3 * s + 3)
                        nc.vector.tensor_scalar(
                            out=vpad[:, 2 + WS * s:2 + WS * (s + 1), 2:2 + W].rearrange("c y (w x) -> c w y x", x=WS),
                            in0=bank[5][:, 0:STRIP].rearrange("c (w y x) -> c w y x", w=NWIN, y=WS),
                            scalar1=fb[:, 2:3], scalar2=None, op0=ALU.add).then_inc(s_v, 1)
                        for j, (w0, w1_) in enumerate(((0, 4), (4, 7))):
                            dve.wait_ge(s_vt, ONE + b * 2 * SN + 2 * s + j + 1)
                            nc.vector.tensor_copy(vt[:, (NWIN * s + w0) * C:(NWIN * s + w1_) * C],
                                                  bank[6 + j][0:WPIX, 0:(w1_ - w0) * C]).then_inc(s_v, 1)
                    dve.wait_ge(s_lg, ONE + b + 1)
                    nc.vector.tensor_copy(lg[:, :], bank[0][0:P2, 128:128 + P2]).then_inc(s_top, 1)
                    dve.wait_ge(s_top, ONE + 3 * b + 1)
                    dve.sem_inc(s_gate, 1)
                    nc.vector.max(out=mx8[:, :], in_=lg[:, :]).then_inc(s_top, 1)
                    dve.wait_ge(s_top, ONE + 3 * b + 2)
                    dve.wait_ge(s_ix, ONE + 16 * b)
                    dve.sem_inc(s_gate, 1)
                    nc.vector.max_index(out=ix8[:, :], in_max=mx8[:, :], in_values=lg[:, :]).then_inc(s_top, 1)
                    dve.wait_ge(s_v, ONE + 3 * SN * (b + 1))
                    dve.wait_ge(s_oz, ONE + b + 1)
                    for w in range(LEAD):
                        window(b, w, w % 2, w)
                    with dve.Fori(0, 5) as dy:
                        taps = [(lambda dx=dx, part=part: lepe(b, dy, dx, part)) for dx in range(5)
                                for part in range(LQ)]
                        per = len(taps) / BODY
                        for i in range(BODY):
                            window(b, dy * BODY + i + LEAD, (LEAD + i) % 2,
                                   extra=taps[round(i * per):round((i + 1) * per)])
                    with dve.Fori(0, (NW - LEAD - 5 * BODY) // 2) as k:
                        for i in range(2):
                            window(b, k * 2 + i + LEAD + 5 * BODY, (LEAD + i) % 2)
                    for w in range(NW, NW + 3):
                        window(b, w, w % 2, w)

                    def residual(s):
                        dve.wait_ge(s_wo, ONE + b * SN + s + 1)
                        xs = x1[:, WS * s:WS * (s + 1), :].rearrange("c y x -> c (y x)")
                        nc.vector.scalar_tensor_tensor(out=xs, in0=bank[6 + s % 2][:, 0:STRIP], scalar=v("wo_b"),
                                                       in1=xs, op0=ALU.add, op1=ALU.add).then_inc(s_x2, 1)

                    residual(0)
                    residual(1)
                    for s in range(SN):
                        if s + 2 < SN:
                            residual(s + 2)
                        dve.wait_ge(s_rs, ONE + b * 2 * SN + SN + s + 1)
                        nc.vector.tensor_tensor(out=xn2[:, NWIN * s:NWIN * (s + 1), :].rearrange("c w k -> c (w k)"),
                                                in0=bank[s % 2][:, 0:STRIP], in1=rstd[:, s % 2], op=ALU.mult
                                                ).then_inc(s_xn2, 1)
                    for s in range(SN):
                        dve.wait_ge(s_y2, ONE + b * SN + s + 1)
                        dve.wait_ge(s_x2, ONE + b * SN + s + 1)
                        xs = x1[:, WS * s:WS * (s + 1), :].rearrange("c y x -> c (y x)")
                        nc.vector.scalar_tensor_tensor(out=xs, in0=bank[6 + s % 2][:, 0:STRIP], scalar=v("mb2"),
                                                       in1=xs, op0=ALU.add, op1=ALU.add).then_inc(s_x3, 1)

        @block.tensor
        def _(pe):
            pe.wait_ge(s_w, ONE + 16 * N_W)
            for j in range(3):
                nc.tensor.matmul(bank[0][:, j:j + 1], wqkv[:, j * C:(j + 1) * C], v("b1"), start=True, stop=True)
            for j in range(3):
                m = nc.tensor.matmul(bank[0][:, 3 + j:4 + j], w1[:, j * C:(j + 1) * C], v("b2"), start=True, stop=True)
            m.then_inc(s_fold, 1)
            pe.wait_ge(s_fb, ONE + 1)
            pe.wait_ge(s_prep, ONE + 2)

            def strip_of(t, s):
                return t[:, WS * s:WS * (s + 1), :].rearrange("c y x -> c (y x)")

            with pe.Fori(0, NB) as bq:
                with pe.Fori(0, G) as bg:
                    b = bq * G + bg

                    def cen(s, second):
                        if second:
                            pe.wait_ge(s_x2, ONE + b * SN + s + 1)
                            if s >= 2:
                                pe.wait_ge(s_xn2, ONE + b * SN + s - 1)
                        elif s >= 2:
                            pe.wait_ge(s_xn, ONE + b * SN + s - 1)
                        nc.tensor.matmul(bank[s % 2][:, 0:STRIP], centre[:, :], strip_of(x1, s), start=True, stop=True
                                         ).then_inc(s_cen, 1)

                    def var(s, second):
                        n = b * 2 * SN + SN * second + s
                        pe.wait_ge(s_sq, ONE + n + 1)
                        pe.wait_ge(s_ln, ONE + n)
                        nc.tensor.matmul(bank[2][:, 0:STRIP], mean[:, :], sq[:, s % 2], start=True, stop=True
                                         ).then_inc(s_var, 1)

                    pe.wait_ge(s_pos, ONE + POS_TAPS * (b + 1))
                    pe.wait_ge(s_ys, ONE + SN * b)
                    cen(0, 0)
                    var(0, 0)
                    for s in range(SN):
                        if s + 1 < SN:
                            cen(s + 1, 0)
                        pe.wait_ge(s_xn, ONE + b * SN + s + 1)
                        x_s = xn[:, s % 2].rearrange("c w k -> c (w k)")
                        for j in range(3):
                            if s == 0:
                                pe.wait_ge(s_g, ONE + b * MLP * SN)
                            elif j < 2:
                                pe.wait_ge(s_qk, ONE + b * 2 * SN + 2 * (s - 1) + j + 1)
                            else:
                                pe.wait_ge(s_v, ONE + b * 3 * SN + 3 * (s - 1) + 1)
                            nc.tensor.matmul(bank[3 + j][:, 0:STRIP], wqkv[:, j * C:(j + 1) * C], x_s,
                                             start=True, stop=True).then_inc(s_q, 1)
                        if s + 1 < SN:
                            var(s + 1, 0)
                        for j, (w0, w1_) in enumerate(((0, 4), (4, 7))):
                            if s == 0:
                                pe.wait_ge(s_x3, ONE + b * SN)
                            else:
                                pe.wait_ge(s_v, ONE + b * 3 * SN + 3 * (s - 1) + 2 + j)
                            for w in range(w0, w1_):
                                m = nc.tensor.matmul(bank[6 + j][0:WPIX, (w - w0) * C:(w - w0 + 1) * C],
                                                     xn[:, s % 2, w, :], wqkv[:, 2 * C:3 * C], start=True, stop=True)
                            m.then_inc(s_vt, 1)
                    pe.wait_ge(s_xw, ONE + SN * (b + 1))
                    for j in range(2):
                        nc.tensor.matmul(bank[0][:, 64 * j:64 * j + P2], wqkv[:, j * C:(j + 1) * C], xw[:, :],
                                         start=True, stop=True).then_inc(s_qw, 1)
                    pe.wait_ge(s_qwe, ONE + 2 * b + 2)
                    nc.tensor.matmul(bank[0][0:P2, 128:128 + P2], qw[:, 0], qw[:, 1], start=True, stop=True
                                     ).then_inc(s_lg, 1)

                    def window(w, par, half, i=None):
                        n = b * NW + w
                        if i is None or 3 <= i <= NW + 2:
                            u = (par + 1) % 2
                            pe.wait_ge(s_on, ONE + n - 2)
                            if i is None or i >= 5:
                                pe.wait_ge(s_oa, ONE + n - 4)
                            nc.tensor.matmul(bank[6 + u][:, 0:WPIX], on[:, u], fold[:, :], start=True, stop=True
                                             ).then_inc(s_of, 1)
                        if i is None or i < NW:
                            u = par
                            pe.wait_ge(s_bd, ONE + 2 * n + 2)
                            if i is None or i >= 2:
                                pe.wait_ge(s_p, ONE + 2 * n - 2)
                            for hp in range(2):
                                m = nc.tensor.matmul(bank[u][:, 256 * hp:256 * hp + 256],
                                                     qbd[:, u, 2 * hp:2 * hp + 2].rearrange("c h k -> c (h k)"),
                                                     ksel[:, u, :], start=True, stop=True)
                            m.then_inc(s_s, 1)
                        if i is None or 2 <= i <= NW + 1:
                            u = par
                            pe.wait_ge(s_pte, ONE + n - 1)
                            pe.wait_ge(s_vs[u], ONE + 16 * TOPK * (b * ((NW + 1 - u) // 2) + half))
                            if i is None or i >= 4:
                                pe.wait_ge(s_on, ONE + n - 3)
                            for hp in range(2):
                                for c in range(2):
                                    m = nc.tensor.matmul(bank[4 + u][:, 64 * hp:64 * hp + 64], pT[:, u, 2 * hp + c],
                                                         vsel[:, u, c, 64 * hp:64 * hp + 64],
                                                         start=(c == 0), stop=(c == 1))
                            m.then_inc(s_o, 1)
                        if i is None or 1 <= i <= NW:
                            u = (par + 1) % 2
                            pe.wait_ge(s_p, ONE + 2 * n)
                            if i is None or i >= 3:
                                pe.wait_ge(s_pte, ONE + n - 2)
                            for hp in range(2):
                                for c in range(2):
                                    m = nc.tensor.transpose(bank[2 + u][:, C * (2 * hp + c):C * (2 * hp + c + 1)],
                                                            prob[:, u, hp, C * c:C * (c + 1)], ident[:, :])
                            m.then_inc(s_pt, 1)

                    pe.wait_ge(s_qk, ONE + 2 * SN * (b + 1))
                    pe.wait_ge(s_v, ONE + 3 * SN * (b + 1))
                    pe.sem_inc(s_gate, 1)
                    for w in range(LEAD):
                        window(w, w % 2, w // 2, w)
                    with pe.Fori(0, (NW - LEAD) // 2) as k:
                        for i in range(2):
                            window(k * 2 + i + LEAD, (LEAD + i) % 2, k + (LEAD + i) // 2)
                    for w in range(NW, NW + 3):
                        window(w, w % 2, w // 2, w)

                    def project(s):
                        if s >= 2:
                            pe.wait_ge(s_x2, ONE + b * SN + s - 1)
                        nc.tensor.matmul(bank[6 + s % 2][:, 0:STRIP], wo[:, :], strip_of(oacc, s),
                                         start=True, stop=False)
                        nc.tensor.matmul(bank[6 + s % 2][:, 0:STRIP], wo[:, :],
                                         att[:, NWIN * s:NWIN * (s + 1), :].rearrange("c w (y x) -> c y w x", y=WS),
                                         start=False, stop=True).then_inc(s_wo, 1)

                    pe.wait_ge(s_oa, ONE + NW * (b + 1))
                    pe.wait_ge(s_lepe, ONE + LQ + LEPES * (b + 1))
                    project(0)
                    project(1)
                    cen(0, 1)
                    for s in range(SN):
                        if s + 2 < SN:
                            project(s + 2)
                        if s + 1 < SN:
                            cen(s + 1, 1)
                        var(s, 1)

                    def hidden(s):
                        pe.wait_ge(s_xn2, ONE + b * SN + s + 1)
                        for j in range(MLP):
                            if s >= 1:
                                pe.wait_ge(s_g, ONE + b * MLP * SN + (s - 1) * MLP + j + 1)
                            nc.tensor.matmul(bank[3 + j][:, 0:STRIP], w1[:, j * C:(j + 1) * C],
                                             xn2[:, NWIN * s:NWIN * (s + 1), :].rearrange("c w k -> c (w k)"),
                                             start=True, stop=True).then_inc(s_h, 1)

                    hidden(0)
                    for s in range(SN):
                        if s + 1 < SN:
                            hidden(s + 1)
                        pe.wait_ge(s_g, ONE + b * MLP * SN + (s + 1) * MLP)
                        if s >= 2:
                            pe.wait_ge(s_x3, ONE + b * SN + s - 1)
                        for j in range(MLP):
                            m = nc.tensor.matmul(bank[6 + s % 2][:, 0:STRIP], w2[:, j], hid[:, s % 2, j],
                                                 start=(j == 0), stop=(j == MLP - 1))
                        m.then_inc(s_y2, 1)
                    pe.wait_ge(s_pad, ONE + b + 1)
                    for s in range(SN):
                        if s >= 2:
                            pe.wait_ge(s_ys, ONE + b * SN + s - 1)
                        for k, (dy, dx) in enumerate(PTAPS):
                            m = nc.tensor.matmul(bank[s % 2][:, 0:STRIP], wconv[:, k],
                                                 x3pad[:, 1 + WS * s + dy:1 + WS * (s + 1) + dy, 1 + dx:1 + dx + W],
                                                 start=(k == 0), stop=(k == 8))
                        m.then_inc(s_cv, 1)


def sequences(nc, d, ys_dram, xr_dram):
    ctx = ExitStack()
    with ctx:
        def sb(name, shape, dt=FP32):
            return ctx.enter_context(nc.sbuf_tensor("b_" + name, shape, dt))

        sems = []

        def sem(name):
            sems.append(ctx.enter_context(nc.semaphore("b_" + name)))
            return sems[-1]

        acc = ctx.enter_context(nc.psum_tensor("b_acc", [C, TOK], FP32))
        rep = [ctx.enter_context(nc.psum_tensor(f"b_rep{i}", [C, TOK], FP32)) for i in range(2)]
        misc = [ctx.enter_context(nc.psum_tensor(f"b_misc{i}", [C, 512], FP32)) for i in range(2)]

        NCH = NB * CHUNKS
        HT = TOK // 2

        vec = sb("vec", [C, NV])
        ident = sb("ident", [C, C])
        diag_d = sb("diag_d", [C, C])
        negA = sb("negA", [C, NS])
        wx = sb("wx", [C, C])
        wz = sb("wz", [C, C])
        wtap = sb("wtap", [C, 5, C])
        wze = sb("wze", [C, 2, C])
        wdt = sb("wdt", [C, C])
        dtw = sb("dtw", [C, C])
        wbc = sb("wbc", [C, C])
        wout = sb("wout", [C, G * K])
        pickf = sb("pickf", [3 * G * HALF, HALF * C])
        pick = sb("pick", [3 * G * HALF, HALF, C], BF16)

        yc = sb("yc", [C, G, CPX])
        yr = sb("yr", [C, T, G, K])
        yT = sb("yT", [C, 4, C])
        xc = sb("xc", [C, 2, T, C])
        zs = sb("zs", [C, 2, T, C])
        pre = sb("pre", [C, TOK])
        sp_ = sb("sp", [C, TOK])
        dt = sb("dt", [C, TOK])
        uu = sb("uu", [C, TOK])
        bcf = sb("bcf", [C, TOK])
        hi = sb("hi", [C, TOK], BF16)
        mid = sb("mid", [C, TOK], BF16)
        lo = sb("lo", [C, TOK], BF16)
        bcs = sb("bcs", [3 * G * HALF, 2, 4, TOK], BF16)
        dA = sb("dA", [C, 2, HALF, TOK - C])
        hh = sb("hh", [C, 2, HALF, TOK])
        tmp = sb("tmp", [C, HALF, C])
        ym = sb("ym", [C, TOK])
        xo = sb("xo", [C, G, CPX])

        s_gate = sem("gate")
        s_w = sem("w")
        s_p1 = sem("p1")
        s_p2 = sem("p2")
        s_yc = sem("yc")
        s_yr = sem("yr")
        s_t = sem("t")
        s_te = sem("te")
        s_x = sem("x")
        s_xe = sem("xe")
        s_z = sem("z")
        s_ze = sem("ze")
        s_d = sem("d")
        s_pre = sem("pre")
        s_el = sem("el")
        s_dt = sem("dt")
        s_u = sem("u")
        s_bc = sem("bc")
        s_bce = sem("bce")
        s_sp = sem("spl")
        s_bcs = sem("bcs")
        s_rep = sem("rep")
        s_use = sem("use")
        s_a = sem("a")
        s_st = sem("st")
        s_yd = sem("yd")
        s_y = sem("y")
        s_ym = sem("ym")
        s_o = sem("o")
        s_oe = sem("oe")
        s_os = sem("os")

        def v(name, i=0, n=1):
            at = _V[name][0] + i
            return vec[:, at:at + n]

        N_W = 10
        STEPS = 2 * (T - 1)

        block = ctx.enter_context(nc.Block())

        def early(n):
            return isinstance(n, int) and n < 2

        def use_b(n, h, i):
            return i if h == 0 and isinstance(n, int) and n == 0 else 32 * n - 8 + 16 * h + i

        def use_c(n, h, i):
            if h == 1 and isinstance(n, int) and n == NCH - 1:
                return 32 * NCH - 8 + i
            return 32 * n + 16 * (1 + h) + i

        def chunks(eng, body):
            body(0, 0)
            with eng.Fori(0, (NCH - 4) // 2) as k:
                for i in range(2):
                    body(k * 2 + i + 1, (i + 1) % 2)
            for n in range(NCH - 3, NCH):
                body(n, n % 2)

        def is_first(n):
            return isinstance(n, int) and n == 0

        def before_end(n, left):
            return not isinstance(n, int) or n + left < NCH

        @block.sync
        def _(sp):
            for dst, src in ((vec, "vecs"), (ident, "ident"), (wx, "wx"), (wz, "wz"), (wdt, "xp_dt"), (dtw, "dt_w"),
                             (wbc, "xp_bc"), (wout, "w_out"), (pickf, "pick")):
                sp.dma_start(dst[:, :], d[src]).then_inc(s_w, 16)
            sp.dma_start(wtap[:, :, :], d["taps"]).then_inc(s_w, 16)

            def load(n):
                sp.dma_start(yc[:, :, :], ys_dram[bass.ds(n, 1)].rearrange("a c g p -> c (a g) p")).then_inc(s_yc, 16)

            def split(n, par):
                sp.wait_ge(s_sp, ONE + 4 * n + 4)
                for part, src in enumerate((hi, mid, lo)):
                    for m in range(4):
                        sp.dma_start(bcs[32 * part:32 * part + 32, par, m, :], src[32 * m:32 * m + 32, :]
                                     ).then_inc(s_bcs, 16)

            def store(n):
                sp.wait_ge(s_oe, ONE + n + 1)
                sp.dma_start(xr_dram[bass.ds(n, 1)].rearrange("a c g p -> c (a g) p"), xo[:, :, :]).then_inc(s_os, 16)

            load(0)
            sp.wait_ge(s_yr, ONE + 1)
            load(1)
            split(0, 0)

            def body(n, par):
                if before_end(n, 2):
                    sp.wait_ge(s_yr, ONE + n + 2)
                    load(n + 2)
                if before_end(n, 1):
                    if not is_first(n):
                        sp.wait_ge(s_rep, ONE + use_c(n - 1, 1, HALF))
                    split(n + 1, 1 - par)
                if not is_first(n):
                    store(n - 1)

            chunks(sp, body)
            store(NCH - 1)
            sp.wait_ge(s_os, ONE + 16 * NCH)

        @block.gpsimd
        def _(pool):
            for x in sems:
                pool.sem_inc(x, ONE)

            def reorder(n):
                pool.wait_ge(s_yc, ONE + 16 * n + 16)
                pool.wait_ge(s_t, ONE + n)
                pool.sem_inc(s_gate, 1)
                nc.gpsimd.tensor_copy(yr[:, :, :, :], yc[:, :, :].rearrange("c g (t k) -> c t g k", k=K)
                                      ).then_inc(s_yr, 1)

            def front(n, par):
                pool.wait_ge(s_sp, ONE + 4 * n + 1)
                nc.gpsimd.tensor_tensor(out=bcf[:, :], in0=bcf[:, :], in1=hi[:, :], op=ALU.subtract).then_inc(s_sp, 1)
                pool.wait_ge(s_sp, ONE + 4 * n + 3)
                nc.gpsimd.tensor_tensor(out=lo[:, :], in0=bcf[:, :], in1=mid[:, :], op=ALU.subtract).then_inc(s_sp, 1)
                pool.wait_ge(s_dt, ONE + n + 1)
                if not is_first(n):
                    pool.wait_ge(s_use, ONE + use_b(n - 1, 1, HALF))
                nc.gpsimd.tensor_tensor(out=uu[:, :], in0=dt[:, :], in1=xc[:, par].rearrange("c t m -> c (t m)"),
                                        op=ALU.mult).then_inc(s_u, 1)

            reorder(0)
            front(0, 0)
            reorder(1)

            def body(n, par):
                if before_end(n, 1):
                    front(n + 1, 1 - par)
                if before_end(n, 2):
                    reorder(n + 2)

            chunks(pool, body)

        @block.scalar
        def _(act):
            act.wait_ge(s_w, ONE + 16 * N_W)
            act.preload_act_table_set("natural_log_exp_and_others")
            nc.scalar.activation(negA[:, :], v("alog", 0, NS), ACT.Exp).then_inc(s_p2, 1)
            act.wait_ge(s_p2, ONE + 1)
            nc.scalar.activation(negA[:, :], negA[:, :], ACT.Copy, scale=-1.0)
            nc.scalar.activation(pick[:, :, :].rearrange("k n c -> k (n c)"), pickf[:, :], ACT.Copy).then_inc(s_p2, 1)
            act.wait_ge(s_p2, ONE + 2)

            def turned(n):
                act.wait_ge(s_t, ONE + n + 1)
                nc.scalar.activation(yT[:, :, :].rearrange("c q m -> c (q m)"), misc[0][:, :], ACT.Copy).then_inc(s_te, 1)

            def front(n, par):
                for h in range(2):
                    act.wait_ge(s_x, ONE + 2 * n + h + 1)
                    if h == 0 and not early(n):
                        act.wait_ge(s_yd, ONE + n - 1)
                    nc.scalar.activation(xc[:, par, h:T:2, :], misc[1 - h][:, :].rearrange("c (q m) -> c q m", m=C),
                                         ACT.Silu, bias=v("c1b")).then_inc(s_xe, 1)
                for h in range(2):
                    act.wait_ge(s_d, ONE + 2 * n + h + 1)
                    nc.scalar.activation(pre[:, HT * h:HT * (h + 1)], misc[1 - h][:, :], ACT.Identity, bias=v("dtb")
                                         ).then_inc(s_pre, 1)
                for h in range(2):
                    act.wait_ge(s_bc, ONE + 2 * n + h + 1)
                    if h == 0:
                        act.wait_ge(s_sp, ONE + 4 * n)
                    nc.scalar.activation(bcf[:, HT * h:HT * (h + 1)], misc[1 - h][:, :], ACT.Copy).then_inc(s_bce, 1)
                act.wait_ge(s_bce, ONE + 2 * n + 2)
                act.wait_ge(s_bcs, ONE + 16 * 12 * n)
                nc.scalar.activation(hi[:, :], bcf[:, :], ACT.Copy).then_inc(s_sp, 1)
                act.wait_ge(s_pre, ONE + 2 * n + 2)
                nc.scalar.activation(sp_[:, :], pre[:, :], ACT.Abs).then_inc(s_el, 1)
                act.wait_ge(s_sp, ONE + 4 * n + 2)
                nc.scalar.activation(mid[:, :], bcf[:, :], ACT.Copy).then_inc(s_sp, 1)
                act.preload_act_table_set("natural_log_exp_and_others")
                act.wait_ge(s_el, ONE + 3 * n + 1)
                nc.scalar.activation(sp_[:, :], sp_[:, :], ACT.Exp, scale=-1.0).then_inc(s_el, 1)
                act.wait_ge(s_el, ONE + 3 * n + 2)
                nc.scalar.activation(sp_[:, :], sp_[:, :], ACT.Ln, bias=1.0).then_inc(s_el, 1)

            def gates(n, par):
                for h in range(2):
                    act.wait_ge(s_z, ONE + 2 * n + h + 1)
                    if h == 0 and not early(n):
                        act.wait_ge(s_ym, ONE + n - 1)
                    nc.scalar.activation(zs[:, par, h:T:2, :], misc[h][:, :].rearrange("c (q m) -> c q m", m=C),
                                         ACT.Silu).then_inc(s_ze, 1)

            def decay(n, h):
                act.wait_ge(s_dt, ONE + n + 1)
                if not is_first(n):
                    act.wait_ge(s_st, ONE + 2 * STEPS * n - 2 * STEPS + STEPS * (h + 1))
                for i in range(HALF):
                    nc.scalar.activation(dA[:, h, i, :], dt[:, C:TOK], ACT.Exp,
                                         scale=negA[:, HALF * h + i:HALF * h + i + 1]).then_inc(s_a, 1)

            def evac(n):
                act.wait_ge(s_o, ONE + n + 1)
                act.wait_ge(s_os, ONE + 16 * n)
                nc.scalar.activation(xo[:, :, :].rearrange("c g (t k) -> c t g k", t=T),
                                     misc[1][:, :].rearrange("c (t g k) -> c t g k", t=T, g=G), ACT.Copy
                                     ).then_inc(s_oe, 1)

            turned(0)
            front(0, 0)
            decay(0, 0)
            gates(0, 0)

            def body(n, par):
                if before_end(n, 1):
                    turned(n + 1)
                act.preload_act_table_set("natural_log_exp_and_others")
                decay(n, 1)
                if before_end(n, 1):
                    front(n + 1, 1 - par)
                if not is_first(n):
                    evac(n - 1)
                if before_end(n, 1):
                    decay(n + 1, 0)
                    gates(n + 1, 1 - par)

            chunks(act, body)
            evac(NCH - 1)

        @block.vector
        def _(dve):
            dve.wait_ge(s_w, ONE + 16 * N_W)
            nc.vector.memset(wze[:, :, :], 0.0).then_inc(s_p1, 1)
            dve.wait_ge(s_p1, ONE + 1)
            for i in range(5):
                nc.vector.tensor_tensor(out=wtap[:, i], in0=wtap[:, i], in1=wx[:, :], op=ALU.mult)
            nc.vector.tensor_copy(wze[0:64, 0], wz[0:64, :])
            nc.vector.tensor_copy(wze[64:128, 1], wz[64:128, :])
            nc.vector.tensor_scalar(out=diag_d[:, :], in0=ident[:, :], scalar1=v("D"), scalar2=None, op0=ALU.mult)
            nc.vector.tensor_tensor(out=wdt[:, :], in0=wdt[:, :], in1=dtw[:, :], op=ALU.mult).then_inc(s_p1, 1)

            def front(n):
                dve.wait_ge(s_el, ONE + 3 * n + 3)
                nc.vector.scalar_tensor_tensor(out=dt[:, :], in0=pre[:, :], scalar=0.0, in1=sp_[:, :], op0=ALU.max,
                                               op1=ALU.add).then_inc(s_dt, 1)

            def gate(n, par):
                dve.wait_ge(s_y, ONE + NS * n + NS)
                dve.wait_ge(s_ze, ONE + 2 * n + 2)
                nc.vector.tensor_tensor(out=ym[:, :], in0=acc[:, :], in1=zs[:, par].rearrange("c t m -> c (t m)"),
                                        op=ALU.mult).then_inc(s_ym, 1)

            def states_in(n, h, i):
                dve.wait_ge(s_rep, ONE + use_b(n, h, i + 1))
                if not is_first(n):
                    dve.wait_ge(s_y, ONE + NS * n - NS + HALF * h + i + 1)
                nc.vector.tensor_tensor(out=hh[:, h, i, :], in0=rep[i % 2][:, :], in1=uu[:, :], op=ALU.mult
                                        ).then_inc(s_use, 1)

            def states_out(n, h, i):
                dve.wait_ge(s_rep, ONE + use_c(n, h, i + 1))
                nc.vector.tensor_tensor(out=hh[:, h, i, :], in0=rep[i % 2][:, :], in1=hh[:, h, i, :], op=ALU.mult
                                        ).then_inc(s_use, 1)

            BETWEEN = (0, 1, 3, 4, 6, 7, 9, 10)

            def recur(n, h, between):
                dve.wait_ge(s_a, ONE + NS * n + HALF * (h + 1))
                dve.wait_ge(s_use, ONE + use_b(n, h, HALF))
                for j in range(STEPS):
                    t = j // 2 + 1
                    if j > 0:
                        dve.wait_ge(s_st, ONE + 2 * STEPS * n + STEPS * h + j)
                    now = hh[:, h, :, C * t:C * (t + 1)]
                    if j % 2 == 0:
                        nc.vector.tensor_tensor(out=tmp[:, :, :], in0=dA[:, h, :, C * (t - 1):C * t],
                                                in1=hh[:, h, :, C * (t - 1):C * t], op=ALU.mult).then_inc(s_st, 1)
                    else:
                        nc.vector.tensor_tensor(out=now, in0=tmp[:, :, :], in1=now, op=ALU.add).then_inc(s_st, 1)
                    for f in between.get(j, ()):
                        f()
                dve.wait_ge(s_st, ONE + 2 * STEPS * n + STEPS * (h + 1))

            front(0)

            def body(n, par):
                dve.wait_ge(s_u, ONE + n + 1)
                for i in range(HALF):
                    states_in(n, 0, i)
                recur(n, 0, {} if is_first(n) else
                      {j: [lambda i=i: states_out(n - 1, 1, i)] for i, j in enumerate(BETWEEN)})
                for i in range(HALF):
                    states_in(n, 1, i)
                    if i == 3 and not is_first(n):
                        gate(n - 1, 1 - par)
                between = {j: [lambda i=i: states_out(n, 0, i)] for i, j in enumerate(BETWEEN)}
                if before_end(n, 1):
                    between[2] = [lambda: front(n + 1)]
                recur(n, 1, between)

            chunks(dve, body)
            for i in range(HALF):
                states_out(NCH - 1, 1, i)
            gate(NCH - 1, (NCH - 1) % 2)

        @block.tensor
        def _(pe):
            pe.wait_ge(s_w, ONE + 16 * N_W)
            pe.wait_ge(s_p1, ONE + 2)
            pe.wait_ge(s_p2, ONE + 2)

            def turn(n):
                pe.wait_ge(s_yr, ONE + n + 1)
                if not is_first(n):
                    pe.wait_ge(s_ze, ONE + 2 * n - 1)
                pe.sem_inc(s_gate, 1)
                for q in range(4):
                    m = nc.tensor.transpose(misc[0][:, C * q:C * (q + 1)],
                                            yr[:, 2 * q:2 * q + 2].rearrange("c b g k -> c (b g k)"),
                                            ident[:, :])
                m.then_inc(s_t, 1)

            def pairs(out, w, shift, start, stop):
                m = 4 - shift
                return nc.tensor.matmul(out[:, C * shift:], w, yT[:, 0:m, :].rearrange("c q m -> c (q m)"),
                                        start=start, stop=stop)

            def conv_even(n, k):
                if k == 0:
                    pe.wait_ge(s_te, ONE + n + 1)
                    pe.wait_ge(s_ze, ONE + 2 * n)
                m = pairs(misc[1], wtap[:, 4 - k], k, k == 0, k == 2)
                if k == 2:
                    m.then_inc(s_x, 1)

            def conv_odd(n, k):
                m = pairs(misc[0], wtap[:, 1 - k], k, k == 0, k == 1)
                if k == 1:
                    m.then_inc(s_x, 1)

            def steps(n, par, h):
                pe.wait_ge(s_xe, ONE + 2 * n + 2)
                nc.tensor.matmul(misc[1 - h][:, :], wdt[:, :],
                                 xc[:, par, 4 * h:4 * h + 4, :].rearrange("c t m -> c (t m)"),
                                 start=True, stop=True).then_inc(s_d, 1)

            def bc(n, par, h):
                pe.wait_ge(s_pre, ONE + 2 * n + h + 1)
                nc.tensor.matmul(misc[1 - h][:, :], wbc[:, :],
                                 xc[:, par, 4 * h:4 * h + 4, :].rearrange("c t m -> c (t m)"),
                                 start=True, stop=True).then_inc(s_bc, 1)

            def gates(n, h, projected):
                if h == 1 and projected:
                    pe.wait_ge(s_oe, ONE + n - 1)
                else:
                    pe.wait_ge(s_bce, ONE + 2 * n + 2)
                pairs(misc[h], wze[:, h], 0, True, True).then_inc(s_z, 1)

            def repeat(n, par, c, h, i):
                use = (use_c if c else use_b)(n, h, i)
                if not c and h == 0 and i == 0:
                    pe.wait_ge(s_bcs, ONE + 192 * n + 192)
                if not (isinstance(use, int) and use < 2):
                    pe.wait_ge(s_use, ONE + use - 1)
                for j in range(2):
                    m = nc.tensor.matmul(rep[i % 2][:, HT * j:HT * (j + 1)], pick[:, i],
                                         bcs[:, par, 2 * c + h, HT * j:HT * (j + 1)], start=True, stop=True)
                m.then_inc(s_rep, 1)

            def skip(n, par, j):
                if j == 0:
                    pe.wait_ge(s_ym, ONE + n)
                m = nc.tensor.matmul(acc[:, HT * j:HT * (j + 1)], diag_d[:, :],
                                     xc[:, par, 4 * j:4 * j + 4, :].rearrange("c t m -> c (t m)"),
                                     start=True, stop=False)
                if j == 1:
                    m.then_inc(s_yd, 1)

            def add(n, h, i, j):
                if j == 0:
                    pe.wait_ge(s_use, ONE + use_c(n, h, i + 1))
                m = nc.tensor.matmul(acc[:, HT * j:HT * (j + 1)], ident[:, :], hh[:, h, i, HT * j:HT * (j + 1)],
                                     start=False, stop=(h == 1 and i == HALF - 1))
                if j == 1:
                    m.then_inc(s_y, 1)

            def project(n, tokens):
                pe.wait_ge(s_ym, ONE + n + 1)
                for t in tokens:
                    m = nc.tensor.matmul(misc[1][:, G * K * t:G * K * (t + 1)], ym[:, C * t:C * (t + 1)], wout[:, :],
                                         start=True, stop=True)
                    if t == T - 1:
                        m.then_inc(s_o, 1)

            turn(0)
            for k in range(3):
                conv_even(0, k)
            for k in range(2):
                conv_odd(0, k)
            for h in range(2):
                steps(0, 0, h)
            for h in range(2):
                bc(0, 0, h)
            for h in range(2):
                gates(0, h, False)

            def body(n, par):
                first, more = is_first(n), before_end(n, 1)
                other = 1 - par
                for i in range(HALF):
                    repeat(n, par, 0, 0, i)
                    if i < 2 and not first:
                        for j in range(2):
                            add(n - 1, 0, 6 + i, j)
                    if more:
                        if i == 2:
                            turn(n + 1)
                        if 3 <= i < 6:
                            conv_even(n + 1, i - 3)
                        if i >= 6:
                            conv_odd(n + 1, i - 6)
                for i in range(HALF):
                    if not first:
                        repeat(n - 1, other, 1, 1, i)
                        if i >= 2:
                            for j in range(2):
                                add(n - 1, 1, i - 2, j)
                    if more and 2 <= i < 4:
                        steps(n + 1, other, i - 2)
                    if more and 4 <= i < 6:
                        bc(n + 1, other, i - 4)
                for i in range(HALF):
                    repeat(n, par, 0, 1, i)
                    if not first:
                        if i < 2:
                            for j in range(2):
                                add(n - 1, 1, 6 + i, j)
                        if i >= 6:
                            if i == 6:
                                pe.wait_ge(s_bce if more else s_ze, ONE + 2 * n + (3 if more else 2))
                            project(n - 1, range(4 * (i - 6), 4 * (i - 5)))
                for i in range(HALF):
                    repeat(n, par, 1, 0, i)
                    if i < 2:
                        skip(n, par, i)
                    else:
                        for j in range(2):
                            add(n, 0, i - 2, j)
                    if more and i == 3:
                        gates(n + 1, 0, False)
                    if more and i == 5:
                        gates(n + 1, 1, not first)

            chunks(pe, body)
            last = NCH - 1
            for i in range(2):
                for j in range(2):
                    add(last, 0, 6 + i, j)
            for i in range(HALF):
                repeat(last, last % 2, 1, 1, i)
                if i >= 2:
                    for j in range(2):
                        add(last, 1, i - 2, j)
            for i in range(2):
                for j in range(2):
                    add(last, 1, 6 + i, j)
            pe.wait_ge(s_oe, ONE + last)
            project(last, range(T))


def normalise(nc, d, x3_dram, xr_dram, out):
    ctx = ExitStack()
    with ctx:
        def sb(name, shape, dt=FP32):
            return ctx.enter_context(nc.sbuf_tensor("c_" + name, shape, dt))

        sems = []

        def sem(name):
            sems.append(ctx.enter_context(nc.semaphore("c_" + name)))
            return sems[-1]

        red = [ctx.enter_context(nc.psum_tensor(f"c_red{i}", [C, 2], FP32)) for i in range(2)]
        S = 2
        vec = sb("vec", [C, NV])
        group = sb("group", [C, C])
        xr = sb("xr", [C, S, PIX])
        x3 = sb("x3", [C, S, PIX])
        res = sb("res", [C, S, PIX])
        stats = sb("stats", [C, S, 7, 6])
        mv = sb("mv", [C, S, 2])
        msq = sb("msq", [C, S, 2])
        var = sb("var", [C, S, 1])
        sc = sb("sc", [C, S, 1])
        rs = sb("rs", [C, S, 1])
        shift = sb("shift", [C, S, 1])
        eps = sb("eps", [C, 1])

        s_gate = sem("gate")
        s_w = sem("w")
        s_x = [sem("x0"), sem("x1")]
        s_st = sem("st")
        s_red = sem("red")
        s_m = sem("m")
        s_ln = sem("ln")
        s_sc = sem("sc")
        s_act = sem("act")
        s_res = sem("res")
        s_out = [sem("out0"), sem("out1")]

        def v(name):
            return vec[:, _V[name][0]:_V[name][0] + 1]

        N_W, LOADS, STATS = 2, 6, 9
        FREE = S
        block = ctx.enter_context(nc.Block())

        def images(eng, body):
            with eng.Fori(0, NB) as q:
                for g in range(G):
                    body(q * G + g, q, g, g % 2)

        @block.sync
        def _(sp):
            sp.dma_start(vec[:, :], d["vecs"]).then_inc(s_w, 16)
            sp.dma_start(group[:, :], d["group"]).then_inc(s_w, 16)

            def body(b, q, g, u):
                sp.wait_ge(s_res, ONE + FREE + b - 1)
                chunk = xr_dram[bass.ds(q * CHUNKS, CHUNKS), :, g, :].rearrange("j c p -> c j p")
                sp.dma_start(xr[0:64, u, 0:PIX - WPIX].rearrange("c (j p) -> c j p", p=CPX),
                             chunk[0:64, 0:CHUNKS - 1, :]).then_inc(s_x[u], 16)
                sp.dma_start(xr[0:64, u, PIX - WPIX:PIX], chunk[64:128, 0, 0:WPIX]).then_inc(s_x[u], 16)
                sp.dma_start(xr[64:128, u, 0:WPIX], chunk[64:128, 0, WPIX:CPX]).then_inc(s_x[u], 16)
                sp.dma_start(xr[64:128, u, WPIX:PIX].rearrange("c (j p) -> c j p", p=CPX), chunk[64:128, 1:CHUNKS, :]
                             ).then_inc(s_x[u], 16)
                for two in range(2):
                    sp.dma_start(x3[64 * two:64 * two + 64, u, :],
                                 x3_dram[bass.ds(b, 1)].rearrange("a (r two) p -> two r (a p)", two=2)[two]
                                 ).then_inc(s_x[u], 16)

            images(sp, body)

        @block.gpsimd
        def _(pool):
            for x in sems:
                pool.sem_inc(x, ONE)
            pool.sem_inc(s_res, FREE)
            for x in s_out:
                pool.sem_inc(x, 32)

        @block.tensor
        def _(pe):
            pe.wait_ge(s_w, ONE + 16 * N_W)

            def body(b, q, g, u):
                pe.wait_ge(s_st, ONE + STATS * (b + 1))
                nc.tensor.matmul(red[u][:, :], group[:, :], mv[:, u], start=True, stop=True).then_inc(s_red, 1)

            images(pe, body)

        @block.scalar
        def _(act):
            act.wait_ge(s_w, ONE + 16 * N_W)

            def store(b, u):
                act.wait_ge(s_res, ONE + FREE + b + 1)
                for two in range(2):
                    act.dma_start(out[bass.ds(b, 1)].rearrange("a (r two) p -> two r (a p)", two=2)[two],
                                  res[64 * two:64 * two + 64, u, :]).then_inc(s_out[u], 16)

            def body(b, q, g, u):
                act.preload_act_table_set("natural_log_exp_and_others")
                act.wait_ge(s_m, ONE + 2 * b + 2)
                nc.scalar.activation(rs[:, u], var[:, u], ACT.Ln, bias=eps[:, 0:1], scale=-1.0).then_inc(s_ln, 1)
                act.wait_ge(s_ln, ONE + 2 * b + 1)
                nc.scalar.activation(rs[:, u], rs[:, u], ACT.Exp, scale=-0.5).then_inc(s_ln, 1)
                act.wait_ge(s_sc, ONE + 3 * b + 3)
                act.wait_ge(s_out[u], ONE + 32 * (2 * q + g // 2 + 1))
                nc.scalar.activation(res[:, u, :], xr[:, u, :], ACT.Silu, bias=shift[:, u], scale=sc[:, u]
                                     ).then_inc(s_act, 1)
                store(b, u)

            images(act, body)
            for x in s_out:
                act.wait_ge(x, ONE + 32 + 32 * IMGS // 2)

        @block.vector
        def _(dve):
            dve.wait_ge(s_w, ONE + 16 * N_W)
            nc.vector.memset(eps[:, :], EPS_GN)

            def body(b, q, g, u):
                dve.wait_ge(s_x[u], ONE + 16 * LOADS * (2 * q + g // 2 + 1))
                for j in range(7):
                    nc.vector.bn_stats(out=stats[:, u, j, :], in_=xr[:, u, STRIP * j:STRIP * (j + 1)]
                                       ).then_inc(s_st, 1)
                dve.wait_ge(s_st, ONE + STATS * b + 7)
                dve.sem_inc(s_gate, 1)
                nc.vector.bn_aggr(out=mv[:, u], in_=stats[:, u].rearrange("c j k -> c (j k)")).then_inc(s_st, 1)
                dve.wait_ge(s_st, ONE + STATS * b + 8)
                nc.vector.scalar_tensor_tensor(out=mv[:, u, 1:2], in0=mv[:, u, 0:1], scalar=mv[:, u, 0:1],
                                               in1=mv[:, u, 1:2], op0=ALU.mult, op1=ALU.add).then_inc(s_st, 1)
                dve.wait_ge(s_red, ONE + b + 1)
                nc.vector.tensor_copy(msq[:, u], red[u][:, :]).then_inc(s_m, 1)
                dve.wait_ge(s_m, ONE + 2 * b + 1)
                nc.vector.scalar_tensor_tensor(out=var[:, u], in0=msq[:, u, 0:1], scalar=msq[:, u, 0:1],
                                               in1=msq[:, u, 1:2], op0=ALU.mult, op1=ALU.subtract,
                                               ).then_inc(s_m, 1)
                dve.wait_ge(s_ln, ONE + 2 * b + 2)
                nc.vector.tensor_tensor(out=sc[:, u], in0=rs[:, u], in1=v("gn_w"), op=ALU.mult).then_inc(s_sc, 1)
                dve.wait_ge(s_sc, ONE + 3 * b + 1)
                nc.vector.tensor_tensor(out=shift[:, u], in0=msq[:, u, 0:1], in1=sc[:, u], op=ALU.mult
                                        ).then_inc(s_sc, 1)
                dve.wait_ge(s_sc, ONE + 3 * b + 2)
                nc.vector.tensor_tensor(out=shift[:, u], in0=v("gn_b"), in1=shift[:, u], op=ALU.subtract
                                        ).then_inc(s_sc, 1)
                dve.wait_ge(s_act, ONE + b + 1)
                nc.vector.tensor_tensor(out=res[:, u, :], in0=res[:, u, :], in1=x3[:, u, :], op=ALU.add
                                        ).then_inc(s_res, 1)

            images(dve, body)


TAP_PAIRS = ((0, 1), (2, 3), (None, 0), (1, 2), (3, None))


def program(nc, d, out):
    x3_dram = nc.dram_tensor("x3", (IMGS, C, PIX), FP32).ap()
    ys_dram = nc.dram_tensor("ys", (NB, CHUNKS, C, G, CPX), FP32).ap()
    xr_dram = nc.dram_tensor("xr", (NB * CHUNKS, C, G, CPX), FP32).ap()
    layer0(nc, d, x3_dram, ys_dram)
    sequences(nc, d, ys_dram.rearrange("q j c g p -> (q j) c g p"), xr_dram)
    normalise(nc, d, x3_dram, xr_dram, out.rearrange("b c h w -> b c (h w)"))


def kernel(**inputs):
    import numpy as np
    import concourse.bacc as bacc
    from concourse.bass_utils import run_bass_kernel_spmd as run

    a = {n: np.asarray(x) for n, x in inputs.items()}
    f32 = np.float32
    even_odd = np.r_[0:C:2, 1:C:2]
    L0, L1 = "L0_conv_", "L1_conv_"

    cols = {
        "pos_w": a[L0 + "pos_w"].reshape(C, 9), "pos_b": a[L0 + "pos_b"].reshape(C, 1),
        "g1": a[L0 + "ln1_g"].reshape(C, 1), "b1": a[L0 + "ln1_b"].reshape(C, 1),
        "qkv_b": a[L0 + "qkv_b"].reshape(3, C).T,
        "lepe_w": a[L0 + "lepe_w"].reshape(C, 25), "lepe_b": a[L0 + "lepe_b"].reshape(C, 1),
        "wo_b": a[L0 + "wo_b"].reshape(C, 1), "g2": a[L0 + "ln2_g"].reshape(C, 1), "b2": a[L0 + "ln2_b"].reshape(C, 1),
        "mb1": a[L0 + "mlp_b1"].reshape(MLP, C).T, "mb2": a[L0 + "mlp_b2"].reshape(C, 1),
        "conv_b": a[L1 + "conv_b"][even_odd].reshape(C, 1),
        "gn_w": a[L1 + "gn_w"][even_odd].reshape(C, 1), "gn_b": a[L1 + "gn_b"][even_odd].reshape(C, 1),
        "c1b": np.tile(a[L1 + "conv1d_b"], G).reshape(C, 1), "dtb": np.tile(a[L1 + "dt_proj_b"], G).reshape(C, 1),
        "D": np.tile(a[L1 + "D"], G).reshape(C, 1), "alog": np.tile(a[L1 + "A_log"], (G, 1)),
        "headmask": np.where(np.arange(C)[:, None] // HD == np.arange(HEADS)[None, :], SCALE, 0.0).astype(f32),
        "rowmask": (np.arange(C)[:, None] // WPIX == np.arange(2)[None, :]).astype(f32),
    }
    vecs = np.concatenate([cols[n] for n in _V], axis=1)
    w_in = a[L1 + "in_proj_w"]
    wx, wz = np.zeros((2, G, K, G, DI), f32), np.zeros((2, G, K, G, DI), f32)
    taps = np.zeros((5, 2, G, K, G, DI), f32)
    x_proj = a[L1 + "x_proj_w"]
    xp_dt, dt_w = np.zeros((G, DI, G, DI), f32), np.zeros((G, DI, G, DI), f32)
    xp_bc = np.zeros((G, DI, 4, G, HALF), f32)
    w_out = np.zeros((G, DI, G, K), f32)
    pick = np.zeros((3, G, HALF, HALF, G, DI), f32)
    cw = a[L1 + "conv1d_w"][:, 0, :]
    for g in range(G):
        for blk in range(2):
            wx[blk, g, :, g, :] = w_in[0:DI].T
            wz[blk, g, :, g, :] = w_in[DI:2 * DI].T
        for m, pair in enumerate(TAP_PAIRS):
            for blk in range(2):
                if pair[blk] is not None:
                    taps[m, blk, g, :, g, :] = cw[:, pair[blk]][None, :]
        xp_dt[g, :, g, :] = x_proj[0][:, None]
        dt_w[g, :, g, :] = a[L1 + "dt_proj_w"][:, 0][None, :]
        for m in range(4):
            at = 1 + NS * (m // 2) + HALF * (m % 2)
            xp_bc[g, :, m, g, :] = x_proj[at:at + HALF].T
        w_out[g, :, g, :] = a[L1 + "out_proj_w"].T
        for n in range(HALF):
            pick[:, g, n, n, g, :] = 1.0
    eye = np.eye(C, dtype=f32)
    rows = np.arange(C) % 64 // 16
    data = {
        "x": a["x"], "vecs": vecs, "ident": eye,
        "centre": (eye - f32(1.0 / C)).astype(f32), "mean": np.full((C, C), 1.0 / C, f32),
        "fold": np.concatenate([np.eye(WPIX, dtype=f32)] * 2, axis=0),
        "qkv_w": a[L0 + "qkv_w"], "wo_w": a[L0 + "wo_w"], "mlp_w1": a[L0 + "mlp_w1"], "mlp_w2": a[L0 + "mlp_w2"],
        "conv_w": np.transpose(a[L1 + "conv_w"], (1, 2, 3, 0)).reshape(C, 9, C)[:, :, even_odd],
        "wx": wx.reshape(C, C), "wz": wz.reshape(C, C), "taps": np.transpose(taps.reshape(5, C, C), (1, 0, 2)),
        "xp_dt": xp_dt.reshape(C, C), "dt_w": dt_w.reshape(C, C), "xp_bc": xp_bc.reshape(C, C),
        "w_out": w_out.reshape(C, G * K), "pick": pick.reshape(3 * G * HALF, HALF * C),
        "group": ((rows[:, None] == rows[None, :]) / 32.0).astype(f32),
    }
    nc = bacc.Bacc("TRN2", target_bir_lowering=False, num_devices=1)
    d, arrays = {}, {}
    for name, x in data.items():
        x = np.ascontiguousarray(x)
        arrays[f"in_{name}"] = x
        d[name] = nc.dram_tensor(f"in_{name}", x.shape, mybir.dt.from_np(x.dtype), kind="ExternalInput").ap()
    out = nc.dram_tensor("out", (IMGS, C, H, W), FP32, kind="ExternalOutput").ap()
    program(nc, d, out)
    return run(nc, [arrays], core_ids=[0]).results[0]["out"]
```

```python
from contextlib import ExitStack

import concourse.bass as bass
from concourse import mybir

FP32 = mybir.dt.float32
BF16 = mybir.dt.bfloat16
U32 = mybir.dt.uint32
ALU = mybir.AluOpType
ACT = mybir.ActivationFunctionType
AXX = mybir.AxisListType.X

IMGS, C, H, W = 16, 128, 56, 56
PIX = H * W
NWIN, WS = 7, 8
WPIX = WS * WS
P2 = NWIN * NWIN
STRIP = WS * W
HEADS, HD, TOPK = 4, 32, 4
SCALE = float(C) ** -0.5
MLP = 3
POS_TAPS, LEPE_TAPS = 9, 25
T, K, DI, NS, G = 8, 16, 32, 16, 4
CPX = T * K
CHUNKS = (PIX + WPIX) // CPX
SPX = CHUNKS * CPX
ONE = 1
TOK = T * C
HALF = NS // 2
NB = IMGS // G
EPS_LN, EPS_GN = 1e-6, 1e-5

_V = {}


def _columns():
    at = 0
    for name, n in (("pos_w", 9), ("pos_b", 1), ("g1", 1), ("b1", 1), ("qkv_b", 3), ("lepe_w", 25), ("lepe_b", 1),
                    ("wo_b", 1), ("g2", 1), ("b2", 1), ("mb1", 3), ("mb2", 1), ("conv_b", 1), ("gn_w", 1), ("gn_b", 1),
                    ("c1b", 1), ("dtb", 1), ("D", 1), ("alog", NS), ("headmask", 4), ("rowmask", 2)):
        _V[name] = (at, n)
        at += n
    return at


NV = _columns()


def layer0(nc, d, x3_dram, ys_dram):
    ctx = ExitStack()
    with ctx:
        def sb(name, shape, dt=FP32):
            return ctx.enter_context(nc.sbuf_tensor(name, shape, dt))

        sems = []

        def sem(name):
            sems.append(ctx.enter_context(nc.semaphore(name)))
            return sems[-1]

        bank = [ctx.enter_context(nc.psum_tensor(f"bank{i}", [C, 512], FP32)) for i in range(8)]

        vec = sb("vec", [C, NV])
        ident = sb("ident", [C, C])
        centre = sb("centre", [C, C])
        mean = sb("mean", [C, C])
        fold = sb("fold", [C, WPIX])
        wqkv = sb("wqkv", [C, 3 * C])
        wo = sb("wo", [C, C])
        w1 = sb("w1", [C, MLP * C])
        w2 = sb("w2", [C, MLP, C])
        wconv = sb("wconv", [C, 9, C])
        fb = sb("fb", [C, 6])
        obias = sb("obias", [C, 1])
        epsc = sb("epsc", [C, 1])
        wc1 = sb("wc1", [C, 1])

        xpad = sb("xpad", [C, H + 2, W + 2])
        x1 = sb("x1", [C, H, W])
        qs = sb("qs", [C, P2, WPIX])
        ks = sb("ks", [C, P2 * WPIX])
        vt = sb("vt", [WPIX, P2 * C])
        vpad = sb("vpad", [C, H + 4, W + 4])
        oacc = sb("oacc", [C, H, W])
        att = sb("att", [C, P2, WPIX])
        xn2 = att
        x3pad = sb("x3pad", [C, H + 2, W + 2])
        ysb = sb("ysb", [C, SPX])

        sq = sb("sq", [C, 2, STRIP])
        lnv = sb("lnv", [C, STRIP])
        rstd = sb("rstd", [C, 2, STRIP])
        xn = sb("xn", [C, 2, NWIN, WPIX])
        xw = sb("xw", [C, P2])
        qw = sb("qw", [C, 2, P2])
        lg = sb("lg", [P2, P2])
        mx8 = sb("mx8", [P2, 8])
        ix8 = sb("ix8", [P2, 8], U32)
        ixrow = sb("ixrow", [1, P2 * TOPK], U32)
        qbd = sb("qbd", [C, 2, 4, WPIX])
        nmax = sb("nmax", [C, 2, 2])
        prob = sb("prob", [C, 2, 2, 256])
        psums = sb("psums", [C, 2, 2])
        rinv = sb("rinv", [C, 2, 2])
        rmask = sb("rmask", [C, 2, 2, 2])
        VSLOTS = 4
        ksel = sb("ksel", [C, 2, TOPK * WPIX])
        vsel = sb("vsel", [2 * WPIX, VSLOTS, TOPK // 2, C])
        pT = sb("pT", [2 * WPIX, 2, 4, C])
        on = sb("on", [C, 2, C])
        hid = sb("hid", [C, 2, MLP, STRIP])

        s_gate = sem("s_gate")
        s_w = sem("s_w")
        s_prep = sem("s_prep")
        s_fb = sem("s_fb")
        s_oz = sem("s_oz")
        s_fold = sem("s_fold")
        s_x = sem("s_x")
        s_pos = sem("s_pos")
        s_cen = sem("s_cen")
        s_sq = sem("s_sq")
        s_var = sem("s_var")
        s_ln = sem("s_ln")
        s_rs = sem("s_rs")
        s_xn = sem("s_xn")
        s_q = sem("s_q")
        s_vt = sem("s_vt")
        s_qk = sem("s_qk")
        s_v = sem("s_v")
        s_xw = sem("s_xw")
        s_qw = sem("s_qw")
        s_qwe = sem("s_qwe")
        s_lg = sem("s_lg")
        s_top = sem("s_top")
        s_ix = sem("s_ix")
        s_bd = sem("s_bd")
        s_vs = [sem(f"s_vs{i}") for i in range(4)]
        s_s = sem("s_s")
        s_m = sem("s_m")
        s_p = sem("s_p")
        s_ri = sem("s_ri")
        s_pt = sem("s_pt")
        s_pte = sem("s_pte")
        s_o = sem("s_o")
        s_on = sem("s_on")
        s_of = sem("s_of")
        s_oa = sem("s_oa")
        s_lepe = sem("s_lepe")
        s_lm = sem("s_lm")
        s_la = sem("s_la")
        s_wo = sem("s_wo")
        s_x2 = sem("s_x2")
        s_xn2 = sem("s_xn2")
        s_h = sem("s_h")
        s_g = sem("s_g")
        s_y2 = sem("s_y2")
        s_x3 = sem("s_x3")
        s_pad = sem("s_pad")
        s_cv = sem("s_cv")
        s_ys = sem("s_ys")
        s_zero = sem("s_zero")
        s_x3o = sem("s_x3o")
        s_yso = sem("s_yso")

        def v(name, i=0, n=1, rows=slice(None)):
            at = _V[name][0] + i
            return vec[rows, at:at + n]

        SN = NWIN
        NW = P2
        LQ = 3
        LROWS = H // (LQ + 1)
        LEPES = LEPE_TAPS * LQ
        LEAD, BODY = 5, 8
        TAP_MUL, TAP_ADD = (0, 1, 2, 4, 5), (2, 3, 5, 6, 7)
        PTAPS = [(k // 3 - 1, k % 3 - 1) for k in range(POS_TAPS)]
        N_W = 10

        def chosen(engine, w, windows=1):
            return nc.values_load_multi_w_load_instructions(
                ixrow[0:1, bass.ds(w * TOPK, TOPK * windows)], engines=[engine], min_val=0, max_val=P2 - 1,
                skip_runtime_bounds_check_because="max_index gives places among a row's P2 scores")[1]

        def product(dx):
            return hid[:, dx % 2].rearrange("c j p -> c (j p)")[:, 0:LROWS * W].rearrange("c (y x) -> c y x", x=W)

        block = ctx.enter_context(nc.Block())

        @block.sync
        def _(sp):
            for dst, src in ((vec, "vecs"), (ident, "ident"), (centre, "centre"), (mean, "mean"), (fold, "fold"),
                             (wqkv, "qkv_w"), (wo, "wo_w"), (w1, "mlp_w1")):
                sp.dma_start(dst[:, :], d[src]).then_inc(s_w, 16)
            sp.dma_start(w2[:, :, :], d["mlp_w2"].rearrange("(j p) n -> p j n", p=C)).then_inc(s_w, 16)
            sp.dma_start(wconv[:, :, :], d["conv_w"]).then_inc(s_w, 16)
            sp.wait_ge(s_zero, ONE + 1)

            def load(image):
                sp.dma_start(xpad[:, 1:H + 1, 1:W + 1],
                             d["x"][bass.ds(image, 1)].rearrange("a c h w -> c (a h) w")).then_inc(s_x, 16)

            load(0)
            with sp.Fori(0, NB) as bq:
                with sp.Fori(0, G) as bg:
                    b = bq * G + bg
                    sp.wait_ge(s_top, ONE + 3 * (b + 1))
                    sp.dma_start(ixrow[0:1, :].rearrange("a (p k) -> a p k", k=TOPK), ix8[:, 0:TOPK]
                                 ).then_inc(s_ix, 16)
                    sp.wait_ge(s_pos, ONE + (b + 1) * POS_TAPS)
                    load((b + 1) % IMGS)
                    sp.wait_ge(s_ix, ONE + 16 * (b + 1))
                    sp.wait_ge(s_v, ONE + 3 * SN * (b + 1))
                    sp.sem_inc(s_gate, 1)

                    def gather(w, u, at, first=False):
                        sp.wait_ge(s_o, ONE + b * NW if first else ONE + b * NW + w - (VSLOTS - 1))
                        for t in range(TOPK):
                            sp.dma_start(vsel[WPIX * (t % 2):WPIX * (t % 2 + 1), u, t // 2, :],
                                         vt[:, bass.ds(at[t] * C, C)]).then_inc(s_vs[u], 16)

                    at = chosen(mybir.EngineType.SP, 0, LEAD)
                    for w in range(LEAD):
                        gather(w, w % VSLOTS, at[w * TOPK:(w + 1) * TOPK], w < VSLOTS)
                    with sp.Fori(0, (NW - LEAD) // VSLOTS) as k:
                        at = chosen(mybir.EngineType.SP, k * VSLOTS + LEAD, VSLOTS)
                        for i in range(VSLOTS):
                            gather(k * VSLOTS + i + LEAD, (LEAD + i) % VSLOTS, at[i * TOPK:(i + 1) * TOPK])
                    sp.wait_ge(s_x3, ONE + SN * (b + 1))
                    sp.dma_start(x3_dram[bass.ds(b, 1)].rearrange("a c p -> c (a p)"),
                                 x1[:, :, :].rearrange("c h w -> c (h w)")).then_inc(s_x3o, 16)
            sp.wait_ge(s_x3o, ONE + 16 * IMGS)
            sp.wait_ge(s_x, ONE + 16 * (IMGS + 1))

        @block.gpsimd
        def _(pool):
            for x in sems:
                pool.sem_inc(x, ONE)
            nc.gpsimd.memset(vpad[:, :, :], 0.0)
            nc.gpsimd.memset(ysb[:, :], 0.0)
            nc.gpsimd.memset(epsc[:, :], EPS_LN)
            nc.gpsimd.memset(x3pad[:, :, :], 0.0)
            nc.gpsimd.memset(xpad[:, :, :], 0.0).then_inc(s_zero, 1)
            pool.wait_ge(s_w, ONE + 16 * N_W)

            def query_block(b, w, u, first):
                at = chosen(mybir.EngineType.Pool, w)
                if not first:
                    pool.wait_ge(s_s, ONE + b * NW + w - 1)
                nc.gpsimd.tensor_tensor(
                    out=qbd[:, u], in0=qs[:, bass.ds(w, 1), :].broadcast_to([C, 4, WPIX]),
                    in1=v("headmask", 0, 4).unsqueeze(2).broadcast_to([C, 4, WPIX]),
                    op=ALU.mult).then_inc(s_bd, 1)
                for t in range(TOPK):
                    m = nc.gpsimd.tensor_copy(ksel[:, u, WPIX * t:WPIX * (t + 1)], ks[:, bass.ds(at[t] * WPIX, WPIX)])
                m.then_inc(s_bd, 1)

            with pool.Fori(0, NB) as bq:
                with pool.Fori(0, G) as bg:
                    b = bq * G + bg
                    pool.wait_ge(s_lepe, ONE + LQ + b * LEPES)
                    pool.wait_ge(s_wo, ONE + b * SN)
                    pool.wait_ge(s_la, ONE + b * LEPE_TAPS)
                    pool.sem_inc(s_gate, 1)
                    nc.gpsimd.memset(oacc[:, :, :], 0.0).then_inc(s_oz, 1)
                    pool.wait_ge(s_qk, ONE + 2 * SN * (b + 1))
                    pool.wait_ge(s_ix, ONE + 16 * (b + 1))
                    pool.sem_inc(s_gate, 1)

                    def tap_add(dy, dx):
                        tap = b * LEPE_TAPS + dy * 5 + dx
                        pool.wait_ge(s_lm, ONE + tap + 1)
                        pool.wait_ge(s_la, ONE + tap)
                        dst = oacc[:, LQ * LROWS:H, :]
                        nc.gpsimd.tensor_tensor(out=dst, in0=product(dx), in1=dst, op=ALU.add).then_inc(s_la, 1)

                    for w in range(LEAD):
                        query_block(b, w, w % 2, w < 2)
                    pool.wait_ge(s_oz, ONE + b + 1)
                    pool.sem_inc(s_gate, 1)
                    with pool.Fori(0, 5) as dy:
                        for i in range(BODY):
                            query_block(b, dy * BODY + i + LEAD, (LEAD + i) % 2, False)
                            if i in TAP_ADD:
                                tap_add(dy, TAP_ADD.index(i))
                    with pool.Fori(0, (NW - LEAD - 5 * BODY) // 2) as k:
                        for i in range(2):
                            query_block(b, k * 2 + i + LEAD + 5 * BODY, (LEAD + i) % 2, False)

        @block.scalar
        def _(act):
            act.wait_ge(s_zero, ONE + 1)
            act.wait_ge(s_w, ONE + 16 * N_W)
            act.wait_ge(s_fold, ONE + 1)
            for j in range(3):
                nc.scalar.activation(fb[:, j:j + 1], bank[0][:, j:j + 1], ACT.Identity, bias=v("qkv_b", j))
            for j in range(3):
                m = nc.scalar.activation(fb[:, 3 + j:4 + j], bank[0][:, 3 + j:4 + j], ACT.Identity, bias=v("mb1", j))
            m.then_inc(s_fb, 1)
            act.wait_ge(s_fb, ONE + 1)

            def norm(b, s, second):
                n = b * 2 * SN + s + SN * second + 1
                act.wait_ge(s_cen, ONE + n)
                nc.scalar.activation(sq[:, s % 2], bank[s % 2][:, 0:STRIP], ACT.Square).then_inc(s_sq, 1)
                act.wait_ge(s_var, ONE + n)
                nc.scalar.activation(lnv[:, :], bank[2][:, 0:STRIP], ACT.Ln, bias=epsc[:, 0:1]).then_inc(s_ln, 1)
                act.wait_ge(s_ln, ONE + n)
                if s >= 2:
                    act.wait_ge(s_xn2 if second else s_xn, b * SN + s - 1)
                nc.scalar.activation(rstd[:, s % 2], lnv[:, :], ACT.Exp, scale=-0.5).then_inc(s_rs, 1)

            def window(b, w, par, i=None):
                n = b * NW + w
                u = (par + 1) % 2
                if i is None or 1 <= i <= NW:
                    act.wait_ge(s_pt, ONE + n)
                    if i is None or i >= 3:
                        act.wait_ge(s_o, ONE + n - 2)
                    nc.scalar.activation(pT[:, u].rearrange("k i m -> k (i m)"), bank[2 + u][:, :], ACT.Identity
                                         ).then_inc(s_pte, 1)
                if i is None or i < NW:
                    u = par
                    act.wait_ge(s_m, ONE + n + 1)
                    if i is None or i >= 2:
                        act.wait_ge(s_ri, ONE + 2 * n - 2)
                    for hp in range(2):
                        nc.scalar.activation(prob[:, u, hp], bank[u][:, 256 * hp:256 * hp + 256], ACT.Exp,
                                             bias=nmax[:, u, hp:hp + 1], accum_out=psums[:, u, hp:hp + 1]
                                             ).then_inc(s_p, 1)

            with act.Fori(0, NB) as bq:
                with act.Fori(0, G) as bg:
                    b = bq * G + bg
                    act.preload_act_table_set("natural_log_exp_and_others")
                    norm(b, 0, 0)
                    for s in range(SN):
                        if s + 1 < SN:
                            norm(b, s + 1, 0)
                        act.wait_ge(s_q, ONE + b * 3 * SN + 3 * s + 1)
                        nc.scalar.activation(qs[:, NWIN * s:NWIN * (s + 1), :].rearrange("c w k -> c (w k)"),
                                             bank[3][:, 0:STRIP], ACT.Identity, bias=fb[:, 0:1]).then_inc(s_qk, 1)
                        act.wait_ge(s_q, ONE + b * 3 * SN + 3 * s + 2)
                        nc.scalar.activation(ks[:, STRIP * s:STRIP * (s + 1)], bank[4][:, 0:STRIP],
                                             ACT.Identity, bias=fb[:, 1:2]).then_inc(s_qk, 1)
                    act.wait_ge(s_qw, ONE + 2 * b + 2)
                    for j in range(2):
                        nc.scalar.activation(qw[:, j], bank[0][:, j * 64:j * 64 + P2], ACT.Identity,
                                             bias=fb[:, j:j + 1], scale=1.0 / WPIX).then_inc(s_qwe, 1)
                    for w in range(LEAD):
                        window(b, w, w % 2, w)

                    def tap_multiply(dy, dx):
                        tap = b * LEPE_TAPS + dy * 5 + dx
                        act.wait_ge(s_la, ONE + tap if dx == 0 else ONE + tap - 1)
                        act.sem_inc(s_gate, 1)
                        nc.scalar.activation(product(dx), vpad[:, bass.ds(dy + LQ * LROWS, LROWS), dx:dx + W], ACT.Copy,
                                             scale=vec[:, bass.ds(dy * 5 + dx + _V["lepe_w"][0], 1)]).then_inc(s_lm, 1)

                    act.wait_ge(s_v, ONE + 3 * SN * (b + 1))
                    with act.Fori(0, 5) as dy:
                        for i in range(BODY):
                            window(b, dy * BODY + i + LEAD, (LEAD + i) % 2)
                            if i in TAP_MUL:
                                tap_multiply(dy, TAP_MUL.index(i))
                    with act.Fori(0, (NW - LEAD - 5 * BODY) // 2) as k:
                        for i in range(2):
                            window(b, k * 2 + i + LEAD + 5 * BODY, (LEAD + i) % 2)
                    window(b, NW, NW % 2, NW)
                    for s in range(SN):
                        norm(b, s, 1)

                    def pad(s):
                        act.wait_ge(s_x3, ONE + b * SN + s + 1)
                        nc.scalar.activation(x3pad[:, 1 + WS * s:1 + WS * (s + 1), 1:W + 1],
                                             x1[:, WS * s:WS * (s + 1), :], ACT.Copy).then_inc(s_pad, 1)

                    for s in range(SN):
                        for j in range(MLP):
                            act.wait_ge(s_h, ONE + b * MLP * SN + s * MLP + j + 1)
                            if s >= 2:
                                act.wait_ge(s_y2, ONE + b * SN + s - 1)
                            nc.scalar.activation(hid[:, s % 2, j], bank[3 + j][:, 0:STRIP], ACT.Gelu,
                                                 bias=fb[:, 3 + j:4 + j]).then_inc(s_g, 1)
                        if s >= 2:
                            pad(s - 2)
                    pad(SN - 2)
                    pad(SN - 1)
                    act.wait_ge(s_yso, ONE + 16 * b)
                    for s in range(SN):
                        act.wait_ge(s_cv, ONE + b * SN + s + 1)
                        p = bank[s % 2]
                        at = s * STRIP
                        lo, up = slice(0, 64), slice(64, 128)
                        n = STRIP if s < SN - 1 else STRIP - WPIX
                        nc.scalar.activation(ysb[lo, at:at + n], p[lo, 0:n], ACT.Identity, bias=v("conv_b", rows=lo))
                        if n < STRIP:
                            nc.scalar.activation(ysb[up, 0:WPIX], p[lo, n:STRIP], ACT.Identity,
                                                 bias=v("conv_b", rows=lo))
                        nc.scalar.activation(ysb[up, WPIX + at:WPIX + at + STRIP], p[up, 0:STRIP], ACT.Identity,
                                             bias=v("conv_b", rows=up)).then_inc(s_ys, 1)
                    act.wait_ge(s_ys, ONE + SN * (b + 1))
                    act.dma_start(ys_dram[bass.ds(bq, 1), :, :, bass.ds(bg, 1), :].rearrange("q j c g p -> c (q j g) p"),
                                  ysb[:, :].rearrange("c (j p) -> c j p", p=CPX)).then_inc(s_yso, 16)
            act.wait_ge(s_yso, ONE + 16 * IMGS)

        @block.vector
        def _(dve):
            dve.wait_ge(s_w, ONE + 16 * N_W)
            dve.wait_ge(s_fold, ONE + 1)
            nc.vector.tensor_scalar(out=wqkv[:, :], in0=wqkv[:, :], scalar1=v("g1"), scalar2=None, op0=ALU.mult)
            nc.vector.tensor_scalar(out=w1[:, :], in0=w1[:, :], scalar1=v("g2"), scalar2=None, op0=ALU.mult)
            nc.vector.tensor_scalar(out=wc1[:, :], in0=v("pos_w", 4), scalar1=1.0, scalar2=None, op0=ALU.add
                                    ).then_inc(s_prep, 1)
            dve.wait_ge(s_fb, ONE + 1)
            nc.vector.tensor_tensor(out=obias[:, :], in0=fb[:, 2:3], in1=v("lepe_b"), op=ALU.add).then_inc(s_prep, 1)
            dve.wait_ge(s_prep, ONE + 2)

            dve.sem_inc(s_lepe, LQ)

            def lepe(b, dy, dx, part):
                src = vpad[:, bass.ds(dy + part * LROWS, LROWS), dx:dx + W]
                dst = oacc[:, part * LROWS:(part + 1) * LROWS, :]
                dve.wait_ge(s_lepe, ONE + b * LEPES + (dy * 5 + dx) * LQ + part + 1)
                nc.vector.scalar_tensor_tensor(out=dst, in0=src, scalar=vec[:, bass.ds(dy * 5 + dx + _V["lepe_w"][0], 1)],
                                               in1=dst, op0=ALU.mult, op1=ALU.add).then_inc(s_lepe, 1)

            def window(b, w, par, i=None, extra=()):
                n = b * NW + w
                if i is None or i < NW:
                    u = par
                    dve.wait_ge(s_s, ONE + n + 1)
                    if i is None or i >= 2:
                        dve.wait_ge(s_p, ONE + 2 * n - 2)
                    nc.vector.tensor_reduce(out=nmax[:, u], in_=bank[u][:, :].rearrange("c (h k) -> c h k", h=2),
                                            axis=AXX, op=ALU.max, negate=True).then_inc(s_m, 1)
                for f in extra:
                    f()
                if i is None or 1 <= i <= NW:
                    u = (par + 1) % 2
                    dve.wait_ge(s_p, ONE + 2 * n)
                    nc.vector.reciprocal(rinv[:, u], psums[:, u]).then_inc(s_ri, 1)
                    dve.wait_ge(s_ri, ONE + 2 * n - 1)
                    nc.vector.tensor_tensor(out=rmask[:, u], in0=rinv[:, u].unsqueeze(2).broadcast_to([C, 2, 2]),
                                            in1=v("rowmask", 0, 2).unsqueeze(1).broadcast_to([C, 2, 2]),
                                            op=ALU.mult).then_inc(s_ri, 1)
                if i is None or 2 <= i <= NW + 1:
                    u = par
                    dve.wait_ge(s_ri, ONE + 2 * n - 2)
                    dve.wait_ge(s_o, ONE + n - 1)
                    if i is None or i >= 4:
                        dve.wait_ge(s_of, ONE + n - 3)
                    nc.vector.tensor_tensor(
                        out=on[:, u].rearrange("c (a k) -> c a k", k=HD),
                        in0=bank[4 + u][:, 0:C].rearrange("c (a k) -> c a k", k=HD),
                        in1=rmask[:, u].rearrange("c a k -> c (a k)").unsqueeze(2).broadcast_to([C, 4, HD]),
                        op=ALU.mult).then_inc(s_on, 1)
                if i is None or 4 <= i <= NW + 3:
                    u = par
                    dve.wait_ge(s_of, ONE + n - 3)
                    nc.vector.tensor_scalar(out=att[:, bass.ds(w - 4, 1), :].rearrange("c a k -> c (a k)"),
                                            in0=bank[6 + u][:, 0:WPIX], scalar1=obias[:, 0:1], scalar2=None,
                                            op0=ALU.add).then_inc(s_oa, 1)

            with dve.Fori(0, NB) as bq:
                with dve.Fori(0, G) as bg:
                    b = bq * G + bg
                    dve.wait_ge(s_x, ONE + 16 * (b + 1))
                    dve.wait_ge(s_x3o, ONE + 16 * b)
                    dve.wait_ge(s_pad, ONE + SN * b)
                    nc.vector.tensor_scalar(out=x1[:, :, :], in0=xpad[:, 1:H + 1, 1:W + 1], scalar1=wc1[:, 0:1],
                                            scalar2=v("pos_b"), op0=ALU.mult, op1=ALU.add).then_inc(s_pos, 1)
                    n = 1
                    for k, (dy, dx) in enumerate(PTAPS):
                        if (dy, dx) == (0, 0):
                            continue
                        dve.wait_ge(s_pos, ONE + b * POS_TAPS + n)
                        nc.vector.scalar_tensor_tensor(
                            out=x1[:, :, :], in0=xpad[:, 1 + dy:1 + dy + H, 1 + dx:1 + dx + W],
                            scalar=v("pos_w", k), in1=x1[:, :, :], op0=ALU.mult, op1=ALU.add).then_inc(s_pos, 1)
                        n += 1

                    def by_window(ap):
                        return ap.rearrange("c (y w x) -> c w y x", y=WS, w=NWIN)

                    def normalise(s):
                        dve.wait_ge(s_rs, ONE + b * 2 * SN + s + 1)
                        if s >= 2:
                            dve.wait_ge(s_vt, ONE + b * 2 * SN + 2 * (s - 1))
                        nc.vector.tensor_tensor(out=xn[:, s % 2].rearrange("c w (y x) -> c w y x", y=WS),
                                                in0=by_window(bank[s % 2][:, 0:STRIP]), in1=by_window(rstd[:, s % 2]),
                                                op=ALU.mult).then_inc(s_xn, 1)

                    normalise(0)
                    for s in range(SN):
                        if s + 1 < SN:
                            normalise(s + 1)
                        dve.wait_ge(s_xn, ONE + b * SN + s + 1)
                        nc.vector.tensor_reduce(out=xw[:, NWIN * s:NWIN * (s + 1)], in_=xn[:, s % 2], axis=AXX,
                                                op=ALU.add).then_inc(s_xw, 1)
                        dve.wait_ge(s_q, ONE + b * 3 * SN + 3 * s + 3)
                        nc.vector.tensor_scalar(
                            out=vpad[:, 2 + WS * s:2 + WS * (s + 1), 2:2 + W].rearrange("c y (w x) -> c w y x", x=WS),
                            in0=bank[5][:, 0:STRIP].rearrange("c (w y x) -> c w y x", w=NWIN, y=WS),
                            scalar1=fb[:, 2:3], scalar2=None, op0=ALU.add).then_inc(s_v, 1)
                        for j, (w0, w1_) in enumerate(((0, 4), (4, 7))):
                            dve.wait_ge(s_vt, ONE + b * 2 * SN + 2 * s + j + 1)
                            nc.vector.tensor_copy(vt[:, (NWIN * s + w0) * C:(NWIN * s + w1_) * C],
                                                  bank[6 + j][0:WPIX, 0:(w1_ - w0) * C]).then_inc(s_v, 1)
                    dve.wait_ge(s_lg, ONE + b + 1)
                    nc.vector.tensor_copy(lg[:, :], bank[0][0:P2, 128:128 + P2]).then_inc(s_top, 1)
                    dve.wait_ge(s_top, ONE + 3 * b + 1)
                    dve.sem_inc(s_gate, 1)
                    nc.vector.max(out=mx8[:, :], in_=lg[:, :]).then_inc(s_top, 1)
                    dve.wait_ge(s_top, ONE + 3 * b + 2)
                    dve.wait_ge(s_ix, ONE + 16 * b)
                    dve.sem_inc(s_gate, 1)
                    nc.vector.max_index(out=ix8[:, :], in_max=mx8[:, :], in_values=lg[:, :]).then_inc(s_top, 1)
                    dve.wait_ge(s_v, ONE + 3 * SN * (b + 1))
                    dve.wait_ge(s_oz, ONE + b + 1)
                    for w in range(LEAD):
                        window(b, w, w % 2, w)
                    with dve.Fori(0, 5) as dy:
                        taps = [(lambda dx=dx, part=part: lepe(b, dy, dx, part)) for dx in range(5)
                                for part in range(LQ)]
                        per = len(taps) / BODY
                        for i in range(BODY):
                            window(b, dy * BODY + i + LEAD, (LEAD + i) % 2,
                                   extra=taps[round(i * per):round((i + 1) * per)])
                    with dve.Fori(0, (NW - LEAD - 5 * BODY) // 2) as k:
                        for i in range(2):
                            window(b, k * 2 + i + LEAD + 5 * BODY, (LEAD + i) % 2)
                    for w in range(NW, NW + 4):
                        window(b, w, w % 2, w)

                    def residual(s):
                        dve.wait_ge(s_wo, ONE + b * SN + s + 1)
                        xs = x1[:, WS * s:WS * (s + 1), :].rearrange("c y x -> c (y x)")
                        nc.vector.scalar_tensor_tensor(out=xs, in0=bank[6 + s % 2][:, 0:STRIP], scalar=v("wo_b"),
                                                       in1=xs, op0=ALU.add, op1=ALU.add).then_inc(s_x2, 1)

                    residual(0)
                    residual(1)
                    for s in range(SN):
                        if s + 2 < SN:
                            residual(s + 2)
                        dve.wait_ge(s_rs, ONE + b * 2 * SN + SN + s + 1)
                        nc.vector.tensor_tensor(out=xn2[:, NWIN * s:NWIN * (s + 1), :].rearrange("c w k -> c (w k)"),
                                                in0=bank[s % 2][:, 0:STRIP], in1=rstd[:, s % 2], op=ALU.mult
                                                ).then_inc(s_xn2, 1)
                    for s in range(SN):
                        dve.wait_ge(s_y2, ONE + b * SN + s + 1)
                        dve.wait_ge(s_x2, ONE + b * SN + s + 1)
                        xs = x1[:, WS * s:WS * (s + 1), :].rearrange("c y x -> c (y x)")
                        nc.vector.scalar_tensor_tensor(out=xs, in0=bank[6 + s % 2][:, 0:STRIP], scalar=v("mb2"),
                                                       in1=xs, op0=ALU.add, op1=ALU.add).then_inc(s_x3, 1)

        @block.tensor
        def _(pe):
            pe.wait_ge(s_w, ONE + 16 * N_W)
            for j in range(3):
                nc.tensor.matmul(bank[0][:, j:j + 1], wqkv[:, j * C:(j + 1) * C], v("b1"), start=True, stop=True)
            for j in range(3):
                m = nc.tensor.matmul(bank[0][:, 3 + j:4 + j], w1[:, j * C:(j + 1) * C], v("b2"), start=True, stop=True)
            m.then_inc(s_fold, 1)
            pe.wait_ge(s_fb, ONE + 1)
            pe.wait_ge(s_prep, ONE + 2)

            def strip_of(t, s):
                return t[:, WS * s:WS * (s + 1), :].rearrange("c y x -> c (y x)")

            with pe.Fori(0, NB) as bq:
                with pe.Fori(0, G) as bg:
                    b = bq * G + bg

                    def cen(s, second):
                        if second:
                            pe.wait_ge(s_x2, ONE + b * SN + s + 1)
                            if s >= 2:
                                pe.wait_ge(s_xn2, ONE + b * SN + s - 1)
                        elif s >= 2:
                            pe.wait_ge(s_xn, ONE + b * SN + s - 1)
                        nc.tensor.matmul(bank[s % 2][:, 0:STRIP], centre[:, :], strip_of(x1, s), start=True, stop=True
                                         ).then_inc(s_cen, 1)

                    def var(s, second):
                        n = b * 2 * SN + SN * second + s
                        pe.wait_ge(s_sq, ONE + n + 1)
                        pe.wait_ge(s_ln, ONE + n)
                        nc.tensor.matmul(bank[2][:, 0:STRIP], mean[:, :], sq[:, s % 2], start=True, stop=True
                                         ).then_inc(s_var, 1)

                    pe.wait_ge(s_pos, ONE + POS_TAPS * (b + 1))
                    pe.wait_ge(s_ys, ONE + SN * b)
                    cen(0, 0)
                    var(0, 0)
                    for s in range(SN):
                        if s + 1 < SN:
                            cen(s + 1, 0)
                        pe.wait_ge(s_xn, ONE + b * SN + s + 1)
                        x_s = xn[:, s % 2].rearrange("c w k -> c (w k)")
                        for j in range(3):
                            if s == 0:
                                pe.wait_ge(s_g, ONE + b * MLP * SN)
                            elif j < 2:
                                pe.wait_ge(s_qk, ONE + b * 2 * SN + 2 * (s - 1) + j + 1)
                            else:
                                pe.wait_ge(s_v, ONE + b * 3 * SN + 3 * (s - 1) + 1)
                            nc.tensor.matmul(bank[3 + j][:, 0:STRIP], wqkv[:, j * C:(j + 1) * C], x_s,
                                             start=True, stop=True).then_inc(s_q, 1)
                        if s + 1 < SN:
                            var(s + 1, 0)
                        for j, (w0, w1_) in enumerate(((0, 4), (4, 7))):
                            if s == 0:
                                pe.wait_ge(s_x3, ONE + b * SN)
                            else:
                                pe.wait_ge(s_v, ONE + b * 3 * SN + 3 * (s - 1) + 2 + j)
                            for w in range(w0, w1_):
                                m = nc.tensor.matmul(bank[6 + j][0:WPIX, (w - w0) * C:(w - w0 + 1) * C],
                                                     xn[:, s % 2, w, :], wqkv[:, 2 * C:3 * C], start=True, stop=True)
                            m.then_inc(s_vt, 1)
                    pe.wait_ge(s_xw, ONE + SN * (b + 1))
                    for j in range(2):
                        nc.tensor.matmul(bank[0][:, 64 * j:64 * j + P2], wqkv[:, j * C:(j + 1) * C], xw[:, :],
                                         start=True, stop=True).then_inc(s_qw, 1)
                    pe.wait_ge(s_qwe, ONE + 2 * b + 2)
                    nc.tensor.matmul(bank[0][0:P2, 128:128 + P2], qw[:, 0], qw[:, 1], start=True, stop=True
                                     ).then_inc(s_lg, 1)

                    def window(w, par, slot, at, i=None):
                        n = b * NW + w
                        if i is None or 4 <= i <= NW + 3:
                            u = par
                            pe.wait_ge(s_on, ONE + n - 3)
                            if i is None or i >= 6:
                                pe.wait_ge(s_oa, ONE + n - 5)
                            nc.tensor.matmul(bank[6 + u][:, 0:WPIX], on[:, u], fold[:, :], start=True, stop=True
                                             ).then_inc(s_of, 1)
                        if i is None or i < NW:
                            u = par
                            pe.wait_ge(s_bd, ONE + 2 * n + 2)
                            if i is None or i >= 2:
                                pe.wait_ge(s_p, ONE + 2 * n - 2)
                            for hp in range(2):
                                m = nc.tensor.matmul(bank[u][:, 256 * hp:256 * hp + 256],
                                                     qbd[:, u, 2 * hp:2 * hp + 2].rearrange("c h k -> c (h k)"),
                                                     ksel[:, u, :], start=True, stop=True)
                            m.then_inc(s_s, 1)
                        if i is None or 2 <= i <= NW + 1:
                            u = par
                            pe.wait_ge(s_pte, ONE + n - 1)
                            pe.wait_ge(s_vs[slot], ONE + 16 * TOPK * (b * len(range(slot, NW, VSLOTS)) + at))
                            if i is None or i >= 4:
                                pe.wait_ge(s_on, ONE + n - 3)
                            for hp in range(2):
                                for c in range(2):
                                    m = nc.tensor.matmul(bank[4 + u][:, 64 * hp:64 * hp + 64], pT[:, u, 2 * hp + c],
                                                         vsel[:, slot, c, 64 * hp:64 * hp + 64],
                                                         start=(c == 0), stop=(c == 1))
                            m.then_inc(s_o, 1)
                        if i is None or 1 <= i <= NW:
                            u = (par + 1) % 2
                            pe.wait_ge(s_p, ONE + 2 * n)
                            if i is None or i >= 3:
                                pe.wait_ge(s_pte, ONE + n - 2)
                            for hp in range(2):
                                for c in range(2):
                                    m = nc.tensor.transpose(bank[2 + u][:, C * (2 * hp + c):C * (2 * hp + c + 1)],
                                                            prob[:, u, hp, C * c:C * (c + 1)], ident[:, :])
                            m.then_inc(s_pt, 1)

                    pe.wait_ge(s_qk, ONE + 2 * SN * (b + 1))
                    pe.wait_ge(s_v, ONE + 3 * SN * (b + 1))
                    pe.sem_inc(s_gate, 1)
                    for w in range(LEAD):
                        window(w, w % 2, (w - 2) % VSLOTS, (w - 2) // VSLOTS + 1, w)
                    with pe.Fori(0, (NW - LEAD) // VSLOTS) as k:
                        for i in range(VSLOTS):
                            w = LEAD + i - 2
                            window(k * VSLOTS + i + LEAD, (LEAD + i) % 2, w % VSLOTS, k + w // VSLOTS + 1)
                    for w in range(NW, NW + 4):
                        window(w, w % 2, (w - 2) % VSLOTS, (w - 2) // VSLOTS + 1, w)

                    def project(s):
                        if s >= 2:
                            pe.wait_ge(s_x2, ONE + b * SN + s - 1)
                        nc.tensor.matmul(bank[6 + s % 2][:, 0:STRIP], wo[:, :], strip_of(oacc, s),
                                         start=True, stop=False)
                        nc.tensor.matmul(bank[6 + s % 2][:, 0:STRIP], wo[:, :],
                                         att[:, NWIN * s:NWIN * (s + 1), :].rearrange("c w (y x) -> c y w x", y=WS),
                                         start=False, stop=True).then_inc(s_wo, 1)

                    pe.wait_ge(s_oa, ONE + NW * (b + 1))
                    pe.wait_ge(s_lepe, ONE + LQ + LEPES * (b + 1))
                    pe.wait_ge(s_la, ONE + LEPE_TAPS * (b + 1))
                    project(0)
                    project(1)
                    cen(0, 1)
                    for s in range(SN):
                        if s + 2 < SN:
                            project(s + 2)
                        if s + 1 < SN:
                            cen(s + 1, 1)
                        var(s, 1)

                    def hidden(s):
                        pe.wait_ge(s_xn2, ONE + b * SN + s + 1)
                        for j in range(MLP):
                            if s >= 1:
                                pe.wait_ge(s_g, ONE + b * MLP * SN + (s - 1) * MLP + j + 1)
                            nc.tensor.matmul(bank[3 + j][:, 0:STRIP], w1[:, j * C:(j + 1) * C],
                                             xn2[:, NWIN * s:NWIN * (s + 1), :].rearrange("c w k -> c (w k)"),
                                             start=True, stop=True).then_inc(s_h, 1)

                    hidden(0)
                    for s in range(SN):
                        if s + 1 < SN:
                            hidden(s + 1)
                        pe.wait_ge(s_g, ONE + b * MLP * SN + (s + 1) * MLP)
                        if s >= 2:
                            pe.wait_ge(s_x3, ONE + b * SN + s - 1)
                        for j in range(MLP):
                            m = nc.tensor.matmul(bank[6 + s % 2][:, 0:STRIP], w2[:, j], hid[:, s % 2, j],
                                                 start=(j == 0), stop=(j == MLP - 1))
                        m.then_inc(s_y2, 1)
                    for s in range(SN):
                        pe.wait_ge(s_pad, ONE + b * SN + min(s + 2, SN))
                        if s >= 2:
                            pe.wait_ge(s_ys, ONE + b * SN + s - 1)
                        for k, (dy, dx) in enumerate(PTAPS):
                            m = nc.tensor.matmul(bank[s % 2][:, 0:STRIP], wconv[:, k],
                                                 x3pad[:, 1 + WS * s + dy:1 + WS * (s + 1) + dy, 1 + dx:1 + dx + W],
                                                 start=(k == 0), stop=(k == 8))
                        m.then_inc(s_cv, 1)


def sequences(nc, d, ys_dram, xr_dram):
    ctx = ExitStack()
    with ctx:
        def sb(name, shape, dt=FP32):
            return ctx.enter_context(nc.sbuf_tensor("b_" + name, shape, dt))

        sems = []

        def sem(name):
            sems.append(ctx.enter_context(nc.semaphore("b_" + name)))
            return sems[-1]

        acc = ctx.enter_context(nc.psum_tensor("b_acc", [C, TOK], FP32))
        rep = [ctx.enter_context(nc.psum_tensor(f"b_rep{i}", [C, TOK], FP32)) for i in range(2)]
        misc = [ctx.enter_context(nc.psum_tensor(f"b_misc{i}", [C, 512], FP32)) for i in range(2)]

        NCH = NB * CHUNKS
        HT = TOK // 2

        vec = sb("vec", [C, NV])
        ident = sb("ident", [C, C])
        diag_d = sb("diag_d", [C, C])
        negA = sb("negA", [C, NS])
        wx = sb("wx", [C, C])
        wz = sb("wz", [C, C])
        wtap = sb("wtap", [C, 5, C])
        wze = sb("wze", [C, 2, C])
        wdt = sb("wdt", [C, C])
        dtw = sb("dtw", [C, C])
        wbc = sb("wbc", [C, C])
        wout = sb("wout", [C, G * K])
        pick = sb("pick", [3 * G * HALF, HALF, C], BF16)

        yc = sb("yc", [C, G, CPX])
        yr = sb("yr", [C, T, G, K])
        yT = sb("yT", [C, 4, C])
        xc = sb("xc", [C, 2, T, C])
        zs = sb("zs", [C, 2, T, C])
        pre = sb("pre", [C, TOK])
        sp_ = sb("sp", [C, TOK])
        dt = pre
        uu = sb("uu", [C, TOK])
        bcf = sb("bcf", [C, TOK])
        hi = sb("hi", [C, TOK], BF16)
        mid = sb("mid", [C, TOK], BF16)
        lo = sb("lo", [C, TOK], BF16)
        bcs = sb("bcs", [3 * G * HALF, 2, 4, TOK], BF16)
        dA = sb("dA", [C, 2, HALF, TOK - C])
        hh = sb("hh", [C, 2, HALF, TOK])
        tmp = sb("tmp", [C, HALF, C])
        crep = sb("crep", [C, 2, TOK])
        ym = sb("ym", [C, TOK])
        pickf = ym[0:3 * G * HALF, :]
        xo = sb("xo", [C, G, CPX])

        s_gate = sem("gate")
        s_w = sem("w")
        s_p1 = sem("p1")
        s_p2 = sem("p2")
        s_yc = sem("yc")
        s_yr = sem("yr")
        s_t = sem("t")
        s_te = sem("te")
        s_x = sem("x")
        s_xe = sem("xe")
        s_z = sem("z")
        s_ze = sem("ze")
        s_d = sem("d")
        s_pre = sem("pre")
        s_el = sem("el")
        s_dt = sem("dt")
        s_u = sem("u")
        s_bc = sem("bc")
        s_bce = sem("bce")
        s_sp = sem("spl")
        s_bcs = sem("bcs")
        s_rep = sem("rep")
        s_use = [sem("use0"), sem("use1")]
        s_ce = sem("ce")
        s_pm = sem("pm")
        s_a = sem("a")
        s_st = sem("st")
        s_yd = sem("yd")
        s_y = sem("y")
        s_ym = sem("ym")
        s_o = sem("o")
        s_oe = sem("oe")
        s_os = sem("os")

        def v(name, i=0, n=1):
            at = _V[name][0] + i
            return vec[:, at:at + n]

        N_W = 10
        STEPS = 2 * (T - 1)

        block = ctx.enter_context(nc.Block())

        def early(n):
            return isinstance(n, int) and n < 2

        POOLED = (1, 3, 5, 6, 7)

        def base_b(n, h):
            return 0 if h == 0 and isinstance(n, int) and n == 0 else 32 * n - 8 + 16 * h

        def base_c(n, h):
            if h == 1 and isinstance(n, int) and n == NCH - 1:
                return 32 * NCH - 8
            return 32 * n + 16 * (1 + h)

        def half_b(n, h):
            return 0 if h == 0 and isinstance(n, int) and n == 0 else 16 * n - 4 + 8 * h

        def half_c(n, h):
            return 16 * NCH - 4 if h == 1 and isinstance(n, int) and n == NCH - 1 else 16 * n + 8 * (1 + h)

        def products(n, h, q):
            return len(POOLED) * (2 * n + h) + q

        def chunks(eng, body):
            body(0, 0)
            with eng.Fori(0, (NCH - 4) // 2) as k:
                for i in range(2):
                    body(k * 2 + i + 1, (i + 1) % 2)
            for n in range(NCH - 3, NCH):
                body(n, n % 2)

        def is_first(n):
            return isinstance(n, int) and n == 0

        def before_end(n, left):
            return not isinstance(n, int) or n + left < NCH

        @block.sync
        def _(sp):
            for dst, src in ((vec, "vecs"), (ident, "ident"), (wx, "wx"), (wz, "wz"), (wdt, "xp_dt"), (dtw, "dt_w"),
                             (wbc, "xp_bc"), (wout, "w_out"), (pickf, "pick")):
                sp.dma_start(dst[:, :], d[src]).then_inc(s_w, 16)
            sp.dma_start(wtap[:, :, :], d["taps"]).then_inc(s_w, 16)

            def load(n):
                sp.dma_start(yc[:, :, :], ys_dram[bass.ds(n, 1)].rearrange("a c g p -> c (a g) p")).then_inc(s_yc, 16)

            def split(n, par):
                sp.wait_ge(s_sp, ONE + 4 * n + 4)
                for part, src in enumerate((hi, mid, lo)):
                    for m in range(4):
                        sp.dma_start(bcs[32 * part:32 * part + 32, par, m, :], src[32 * m:32 * m + 32, :]
                                     ).then_inc(s_bcs, 16)

            def store(n):
                sp.wait_ge(s_oe, ONE + n + 1)
                sp.dma_start(xr_dram[bass.ds(n, 1)].rearrange("a c g p -> c (a g) p"), xo[:, :, :]).then_inc(s_os, 16)

            load(0)
            sp.wait_ge(s_yr, ONE + 1)
            load(1)
            split(0, 0)

            def body(n, par):
                if before_end(n, 2):
                    sp.wait_ge(s_yr, ONE + n + 2)
                    load(n + 2)
                if before_end(n, 1):
                    if not is_first(n):
                        sp.wait_ge(s_rep, ONE + base_c(n - 1, 1) + HALF)
                    split(n + 1, 1 - par)
                if not is_first(n):
                    store(n - 1)

            chunks(sp, body)
            store(NCH - 1)
            sp.wait_ge(s_os, ONE + 16 * NCH)

        @block.gpsimd
        def _(pool):
            for x in sems:
                pool.sem_inc(x, ONE)

            def reorder(n):
                pool.wait_ge(s_yc, ONE + 16 * n + 16)
                pool.wait_ge(s_t, ONE + n)
                pool.sem_inc(s_gate, 1)
                nc.gpsimd.tensor_copy(yr[:, :, :, :], yc[:, :, :].rearrange("c g (t k) -> c t g k", k=K)
                                      ).then_inc(s_yr, 1)

            def front(n, par):
                pool.wait_ge(s_sp, ONE + 4 * n + 1)
                nc.gpsimd.tensor_tensor(out=bcf[:, :], in0=bcf[:, :], in1=hi[:, :], op=ALU.subtract).then_inc(s_sp, 1)
                pool.wait_ge(s_sp, ONE + 4 * n + 3)
                nc.gpsimd.tensor_tensor(out=lo[:, :], in0=bcf[:, :], in1=mid[:, :], op=ALU.subtract).then_inc(s_sp, 1)
                pool.wait_ge(s_dt, ONE + n + 1)
                if not is_first(n):
                    for x in s_use:
                        pool.wait_ge(x, ONE + half_b(n - 1, 1) + HALF // 2)
                nc.gpsimd.tensor_tensor(out=uu[:, :], in0=dt[:, :], in1=xc[:, par].rearrange("c t m -> c (t m)"),
                                        op=ALU.mult).then_inc(s_u, 1)

            def states_out(n, h):
                pool.wait_ge(s_st, ONE + 2 * STEPS * n + STEPS * (h + 1))
                for q, i in enumerate(POOLED):
                    pool.wait_ge(s_ce, ONE + products(n, h, q) + 1)
                    now = hh[:, h, i, :]
                    nc.gpsimd.tensor_tensor(out=now, in0=crep[:, (h + q) % 2, :], in1=now, op=ALU.mult).then_inc(s_pm, 1)

            reorder(0)
            front(0, 0)
            reorder(1)

            def body(n, par):
                if not is_first(n):
                    states_out(n - 1, 1)
                if before_end(n, 1):
                    front(n + 1, 1 - par)
                states_out(n, 0)
                if before_end(n, 2):
                    reorder(n + 2)

            chunks(pool, body)
            states_out(NCH - 1, 1)

        @block.scalar
        def _(act):
            act.wait_ge(s_w, ONE + 16 * N_W)
            act.preload_act_table_set("natural_log_exp_and_others")
            nc.scalar.activation(negA[:, :], v("alog", 0, NS), ACT.Exp).then_inc(s_p2, 1)
            act.wait_ge(s_p2, ONE + 1)
            nc.scalar.activation(negA[:, :], negA[:, :], ACT.Copy, scale=-1.0)
            nc.scalar.activation(pick[:, :, :].rearrange("k n c -> k (n c)"), pickf[:, :], ACT.Copy).then_inc(s_p2, 1)
            act.wait_ge(s_p2, ONE + 2)

            def turned(n):
                act.wait_ge(s_t, ONE + n + 1)
                nc.scalar.activation(yT[:, :, :].rearrange("c q m -> c (q m)"), misc[0][:, :], ACT.Copy).then_inc(s_te, 1)

            def copy_c(n, h, q):
                i = POOLED[q]
                act.wait_ge(s_rep, ONE + base_c(n, h) + i + 1)
                if not (is_first(n) and h == 0 and q < 2):
                    act.wait_ge(s_pm, ONE + products(n, h, q) - 1)
                nc.scalar.activation(crep[:, (h + q) % 2, :], rep[i % 2][:, :], ACT.Copy).then_inc(s_ce, 1)
                act.wait_ge(s_ce, ONE + products(n, h, q) + 1)
                act.sem_inc(s_use[i % 2], 1)

            def front(n, par, copy=lambda q: None):
                for h in range(2):
                    act.wait_ge(s_x, ONE + 2 * n + h + 1)
                    if h == 0 and not early(n):
                        act.wait_ge(s_yd, ONE + n - 1)
                    nc.scalar.activation(xc[:, par, h:T:2, :], misc[1 - h][:, :].rearrange("c (q m) -> c q m", m=C),
                                         ACT.Silu, bias=v("c1b")).then_inc(s_xe, 1)
                for h in range(2):
                    copy(h)
                    act.wait_ge(s_d, ONE + 2 * n + h + 1)
                    if h == 0:
                        act.wait_ge(s_u, ONE + n)
                    nc.scalar.activation(pre[:, HT * h:HT * (h + 1)], misc[1 - h][:, :], ACT.Identity, bias=v("dtb")
                                         ).then_inc(s_pre, 1)
                for h in range(2):
                    for q in ((2,), (3, 4))[h]:
                        copy(q)
                    act.wait_ge(s_bc, ONE + 2 * n + h + 1)
                    if h == 0:
                        act.wait_ge(s_sp, ONE + 4 * n)
                    nc.scalar.activation(bcf[:, HT * h:HT * (h + 1)], misc[1 - h][:, :], ACT.Copy).then_inc(s_bce, 1)
                act.wait_ge(s_bce, ONE + 2 * n + 2)
                act.wait_ge(s_bcs, ONE + 16 * 12 * n)
                nc.scalar.activation(hi[:, :], bcf[:, :], ACT.Copy).then_inc(s_sp, 1)
                act.wait_ge(s_pre, ONE + 2 * n + 2)
                nc.scalar.activation(sp_[:, :], pre[:, :], ACT.Abs).then_inc(s_el, 1)
                act.preload_act_table_set("natural_log_exp_and_others")
                act.wait_ge(s_el, ONE + 3 * n + 1)
                nc.scalar.activation(sp_[:, :], sp_[:, :], ACT.Exp, scale=-1.0).then_inc(s_el, 1)
                act.wait_ge(s_el, ONE + 3 * n + 2)
                nc.scalar.activation(sp_[:, :], sp_[:, :], ACT.Ln, bias=1.0).then_inc(s_el, 1)
                act.wait_ge(s_sp, ONE + 4 * n + 2)
                nc.scalar.activation(mid[:, :], bcf[:, :], ACT.Copy).then_inc(s_sp, 1)

            def gates(n, par):
                for h in range(2):
                    act.wait_ge(s_z, ONE + 2 * n + h + 1)
                    if h == 0 and not early(n):
                        act.wait_ge(s_ym, ONE + n - 1)
                    nc.scalar.activation(zs[:, par, h:T:2, :], misc[h][:, :].rearrange("c (q m) -> c q m", m=C),
                                         ACT.Silu).then_inc(s_ze, 1)

            def decay(n, h, states=range(HALF)):
                if 0 in states:
                    act.wait_ge(s_dt, ONE + n + 1)
                    if not is_first(n):
                        act.wait_ge(s_st, ONE + 2 * STEPS * n - 2 * STEPS + STEPS * (h + 1))
                for i in states:
                    nc.scalar.activation(dA[:, h, i, :], dt[:, C:TOK], ACT.Exp,
                                         scale=negA[:, HALF * h + i:HALF * h + i + 1]).then_inc(s_a, 1)

            def evac(n):
                act.wait_ge(s_o, ONE + n + 1)
                act.wait_ge(s_os, ONE + 16 * n)
                nc.scalar.activation(xo[:, :, :].rearrange("c g (t k) -> c t g k", t=T),
                                     misc[1][:, :].rearrange("c (t g k) -> c t g k", t=T, g=G), ACT.Copy
                                     ).then_inc(s_oe, 1)

            turned(0)
            front(0, 0)
            decay(0, 0)
            gates(0, 0)

            def body(n, par):
                first, more = is_first(n), before_end(n, 1)
                act.preload_act_table_set("natural_log_exp_and_others")
                decay(n, 1, range(3))
                if more:
                    turned(n + 1)
                decay(n, 1, range(3, HALF))
                copy = (lambda q: None) if first else (lambda q: copy_c(n - 1, 1, q))
                if more:
                    front(n + 1, 1 - par, copy)
                else:
                    for q in range(len(POOLED)):
                        copy(q)
                copy_c(n, 0, 0)
                if more:
                    decay(n + 1, 0, range(2))
                copy_c(n, 0, 1)
                if not first:
                    evac(n - 1)
                for q in range(2, 4):
                    if more:
                        decay(n + 1, 0, range(2 * q - 2, 2 * q))
                    copy_c(n, 0, q)
                copy_c(n, 0, 4)
                if more:
                    decay(n + 1, 0, range(6, 8))
                    gates(n + 1, 1 - par)

            chunks(act, body)
            for q in range(len(POOLED)):
                copy_c(NCH - 1, 1, q)
            evac(NCH - 1)

        @block.vector
        def _(dve):
            dve.wait_ge(s_w, ONE + 16 * N_W)
            nc.vector.memset(wze[:, :, :], 0.0).then_inc(s_p1, 1)
            dve.wait_ge(s_p1, ONE + 1)
            for i in range(5):
                nc.vector.tensor_tensor(out=wtap[:, i], in0=wtap[:, i], in1=wx[:, :], op=ALU.mult)
            nc.vector.tensor_copy(wze[0:64, 0], wz[0:64, :])
            nc.vector.tensor_copy(wze[64:128, 1], wz[64:128, :])
            nc.vector.tensor_scalar(out=diag_d[:, :], in0=ident[:, :], scalar1=v("D"), scalar2=None, op0=ALU.mult)
            nc.vector.tensor_tensor(out=wdt[:, :], in0=wdt[:, :], in1=dtw[:, :], op=ALU.mult).then_inc(s_p1, 1)

            def front(n):
                dve.wait_ge(s_el, ONE + 3 * n + 3)
                nc.vector.scalar_tensor_tensor(out=dt[:, :], in0=pre[:, :], scalar=0.0, in1=sp_[:, :], op0=ALU.max,
                                               op1=ALU.add).then_inc(s_dt, 1)

            def gate(n, par):
                dve.wait_ge(s_y, ONE + NS * n + NS)
                dve.wait_ge(s_ze, ONE + 2 * n + 2)
                nc.vector.tensor_tensor(out=ym[:, :], in0=acc[:, :], in1=zs[:, par].rearrange("c t m -> c (t m)"),
                                        op=ALU.mult).then_inc(s_ym, 1)

            ADDED = (0, 2, 1, 4, 3, 5, 6, 7)

            def states_in(n, h, i):
                dve.wait_ge(s_rep, ONE + base_b(n, h) + i + 1)
                if not is_first(n):
                    dve.wait_ge(s_y, ONE + NS * n - NS + HALF * h + ADDED.index(i) + 1)
                nc.vector.tensor_tensor(out=hh[:, h, i, :], in0=rep[i % 2][:, :], in1=uu[:, :], op=ALU.mult
                                        ).then_inc(s_use[i % 2], 1)

            def states_out(n, h, i):
                dve.wait_ge(s_rep, ONE + base_c(n, h) + i + 1)
                nc.vector.tensor_tensor(out=hh[:, h, i, :], in0=rep[0][:, :], in1=hh[:, h, i, :], op=ALU.mult
                                        ).then_inc(s_use[0], 1)

            BETWEEN = ((0, 1), (2, 4), (4, 8))

            def recur(n, h, between):
                dve.wait_ge(s_a, ONE + NS * n + HALF * (h + 1))
                for x in s_use:
                    dve.wait_ge(x, ONE + half_b(n, h) + HALF // 2)
                for j in range(STEPS):
                    t = j // 2 + 1
                    if j > 0:
                        dve.wait_ge(s_st, ONE + 2 * STEPS * n + STEPS * h + j)
                    now = hh[:, h, :, C * t:C * (t + 1)]
                    if j % 2 == 0:
                        nc.vector.tensor_tensor(out=tmp[:, :, :], in0=dA[:, h, :, C * (t - 1):C * t],
                                                in1=hh[:, h, :, C * (t - 1):C * t], op=ALU.mult).then_inc(s_st, 1)
                    else:
                        nc.vector.tensor_tensor(out=now, in0=tmp[:, :, :], in1=now, op=ALU.add).then_inc(s_st, 1)
                    for f in between.get(j, ()):
                        f()
                dve.wait_ge(s_st, ONE + 2 * STEPS * n + STEPS * (h + 1))

            front(0)

            def body(n, par):
                dve.wait_ge(s_u, ONE + n + 1)
                for i in range(HALF):
                    states_in(n, 0, i)
                recur(n, 0, {} if is_first(n) else
                      {j: [lambda i=i: states_out(n - 1, 1, i)] for i, j in BETWEEN})
                for i in range(HALF):
                    states_in(n, 1, i)
                between = {j: [lambda i=i: states_out(n, 0, i)] for i, j in BETWEEN}
                if not is_first(n):
                    between[0] = [lambda: gate(n - 1, 1 - par)]
                if before_end(n, 1):
                    between[2] = [lambda: front(n + 1)]
                recur(n, 1, between)

            chunks(dve, body)
            for i, j in BETWEEN:
                states_out(NCH - 1, 1, i)
            gate(NCH - 1, (NCH - 1) % 2)

        @block.tensor
        def _(pe):
            pe.wait_ge(s_w, ONE + 16 * N_W)
            pe.wait_ge(s_p1, ONE + 2)
            pe.wait_ge(s_p2, ONE + 2)

            def turn(n):
                pe.wait_ge(s_yr, ONE + n + 1)
                if not is_first(n):
                    pe.wait_ge(s_ze, ONE + 2 * n - 1)
                pe.sem_inc(s_gate, 1)
                for q in range(4):
                    m = nc.tensor.transpose(misc[0][:, C * q:C * (q + 1)],
                                            yr[:, 2 * q:2 * q + 2].rearrange("c b g k -> c (b g k)"),
                                            ident[:, :])
                m.then_inc(s_t, 1)

            def pairs(out, w, shift, start, stop):
                m = 4 - shift
                return nc.tensor.matmul(out[:, C * shift:], w, yT[:, 0:m, :].rearrange("c q m -> c (q m)"),
                                        start=start, stop=stop)

            def conv_even(n, k):
                if k == 0:
                    pe.wait_ge(s_te, ONE + n + 1)
                    pe.wait_ge(s_ze, ONE + 2 * n)
                m = pairs(misc[1], wtap[:, 4 - k], k, k == 0, k == 2)
                if k == 2:
                    m.then_inc(s_x, 1)

            def conv_odd(n, k):
                m = pairs(misc[0], wtap[:, 1 - k], k, k == 0, k == 1)
                if k == 1:
                    m.then_inc(s_x, 1)

            def steps(n, par, h):
                pe.wait_ge(s_xe, ONE + 2 * n + 2)
                nc.tensor.matmul(misc[1 - h][:, :], wdt[:, :],
                                 xc[:, par, 4 * h:4 * h + 4, :].rearrange("c t m -> c (t m)"),
                                 start=True, stop=True).then_inc(s_d, 1)

            def bc(n, par, h):
                pe.wait_ge(s_pre, ONE + 2 * n + h + 1)
                nc.tensor.matmul(misc[1 - h][:, :], wbc[:, :],
                                 xc[:, par, 4 * h:4 * h + 4, :].rearrange("c t m -> c (t m)"),
                                 start=True, stop=True).then_inc(s_bc, 1)

            def gates(n, h, projected):
                if h == 1 and projected:
                    pe.wait_ge(s_oe, ONE + n - 1)
                else:
                    pe.wait_ge(s_bce, ONE + 2 * n + 2)
                pairs(misc[h], wze[:, h], 0, True, True).then_inc(s_z, 1)

            def repeat(n, par, c, h, i):
                if not c and h == 0 and i == 0:
                    pe.wait_ge(s_bcs, ONE + 192 * n + 192)
                if not (is_first(n) and c == 0 and h == 0 and i < 2):
                    pe.wait_ge(s_use[i % 2], ONE + (half_c if c else half_b)(n, h) + i // 2)
                for j in range(2):
                    m = nc.tensor.matmul(rep[i % 2][:, HT * j:HT * (j + 1)], pick[:, i],
                                         bcs[:, par, 2 * c + h, HT * j:HT * (j + 1)], start=True, stop=True)
                m.then_inc(s_rep, 1)

            def skip(n, par, j):
                if j == 0:
                    pe.wait_ge(s_ym, ONE + n)
                m = nc.tensor.matmul(acc[:, HT * j:HT * (j + 1)], diag_d[:, :],
                                     xc[:, par, 4 * j:4 * j + 4, :].rearrange("c t m -> c (t m)"),
                                     start=True, stop=False)
                if j == 1:
                    m.then_inc(s_yd, 1)

            def add(n, h, i):
                if i in POOLED:
                    pe.wait_ge(s_pm, ONE + products(n, h, POOLED.index(i)) + 1)
                else:
                    pe.wait_ge(s_use[0], ONE + half_c(n, h) + i // 2 + 1)
                for j in range(2):
                    m = nc.tensor.matmul(acc[:, HT * j:HT * (j + 1)], ident[:, :], hh[:, h, i, HT * j:HT * (j + 1)],
                                         start=False, stop=(h == 1 and i == HALF - 1))
                m.then_inc(s_y, 1)

            AFTER_C = ((), (), (0,), (), (2, 1), (), (4, 3), ())
            AFTER_B = {1: 5, 3: 6, 5: 7}

            def late(n, h, i):
                if i in AFTER_B:
                    add(n, h, AFTER_B[i])

            def project(n, tokens):
                pe.wait_ge(s_ym, ONE + n + 1)
                for t in tokens:
                    m = nc.tensor.matmul(misc[1][:, G * K * t:G * K * (t + 1)], ym[:, C * t:C * (t + 1)], wout[:, :],
                                         start=True, stop=True)
                    if t == T - 1:
                        m.then_inc(s_o, 1)

            turn(0)
            for k in range(3):
                conv_even(0, k)
            for k in range(2):
                conv_odd(0, k)
            for h in range(2):
                steps(0, 0, h)
            for h in range(2):
                bc(0, 0, h)
            for h in range(2):
                gates(0, h, False)

            def body(n, par):
                first, more = is_first(n), before_end(n, 1)
                other = 1 - par
                for i in range(HALF):
                    repeat(n, par, 0, 0, i)
                    if not first:
                        late(n - 1, 0, i)
                    if more:
                        if i == 6:
                            turn(n + 1)
                        if i == 7:
                            conv_even(n + 1, 0)
                for i in range(HALF):
                    if not first:
                        repeat(n - 1, other, 1, 1, i)
                    if more:
                        for k in range(2) if i < 2 else ():
                            if i == 0:
                                conv_even(n + 1, 1 + k)
                            else:
                                conv_odd(n + 1, k)
                        if 2 <= i < 4:
                            steps(n + 1, other, i - 2)
                        if i in (5, 7):
                            bc(n + 1, other, i // 2 - 2)
                    if not first:
                        for k in AFTER_C[i]:
                            add(n - 1, 1, k)
                for i in range(HALF):
                    repeat(n, par, 0, 1, i)
                    if not first:
                        late(n - 1, 1, i)
                for i in range(HALF):
                    repeat(n, par, 1, 0, i)
                    if i < 2:
                        skip(n, par, i)
                    for k in AFTER_C[i]:
                        add(n, 0, k)
                    if i == 3 and not first:
                        pe.wait_ge(s_bce if more else s_ze, ONE + 2 * n + (3 if more else 2))
                        project(n - 1, range(T))
                    if more and i == 5:
                        gates(n + 1, 0, False)
                    if more and i == 7:
                        gates(n + 1, 1, not first)

            chunks(pe, body)
            last = NCH - 1
            for i in AFTER_B:
                late(last, 0, i)
            for i in range(HALF):
                repeat(last, last % 2, 1, 1, i)
                for k in AFTER_C[i]:
                    add(last, 1, k)
            for i in AFTER_B:
                late(last, 1, i)
            pe.wait_ge(s_oe, ONE + last)
            project(last, range(T))


def normalise(nc, d, x3_dram, xr_dram, out):
    ctx = ExitStack()
    with ctx:
        def sb(name, shape, dt=FP32):
            return ctx.enter_context(nc.sbuf_tensor("c_" + name, shape, dt))

        sems = []

        def sem(name):
            sems.append(ctx.enter_context(nc.semaphore("c_" + name)))
            return sems[-1]

        red = [ctx.enter_context(nc.psum_tensor(f"c_red{i}", [C, 2], FP32)) for i in range(2)]
        S = 2
        vec = sb("vec", [C, NV])
        group = sb("group", [C, C])
        xr = sb("xr", [C, S, PIX])
        x3 = sb("x3", [C, S, PIX])
        res = sb("res", [C, S, PIX])
        stats = sb("stats", [C, S, 7, 6])
        mv = sb("mv", [C, S, 2])
        msq = sb("msq", [C, S, 2])
        var = sb("var", [C, S, 1])
        sc = sb("sc", [C, S, 1])
        rs = sb("rs", [C, S, 1])
        shift = sb("shift", [C, S, 1])
        eps = sb("eps", [C, 1])

        s_gate = sem("gate")
        s_w = sem("w")
        s_x = [sem("x0"), sem("x1")]
        s_st = sem("st")
        s_red = sem("red")
        s_m = sem("m")
        s_ln = sem("ln")
        s_sc = sem("sc")
        s_act = sem("act")
        s_res = sem("res")
        s_out = [sem("out0"), sem("out1")]

        def v(name):
            return vec[:, _V[name][0]:_V[name][0] + 1]

        N_W, LOADS, STATS = 2, 6, 9
        FREE = S
        block = ctx.enter_context(nc.Block())

        def images(eng, body):
            with eng.Fori(0, NB) as q:
                for g in range(G):
                    body(q * G + g, q, g, g % 2)

        @block.sync
        def _(sp):
            sp.dma_start(vec[:, :], d["vecs"]).then_inc(s_w, 16)
            sp.dma_start(group[:, :], d["group"]).then_inc(s_w, 16)

            def body(b, q, g, u):
                sp.wait_ge(s_res, ONE + FREE + b - 1)
                chunk = xr_dram[bass.ds(q * CHUNKS, CHUNKS), :, g, :].rearrange("j c p -> c j p")
                sp.dma_start(xr[0:64, u, 0:PIX - WPIX].rearrange("c (j p) -> c j p", p=CPX),
                             chunk[0:64, 0:CHUNKS - 1, :]).then_inc(s_x[u], 16)
                sp.dma_start(xr[0:64, u, PIX - WPIX:PIX], chunk[64:128, 0, 0:WPIX]).then_inc(s_x[u], 16)
                sp.dma_start(xr[64:128, u, 0:WPIX], chunk[64:128, 0, WPIX:CPX]).then_inc(s_x[u], 16)
                sp.dma_start(xr[64:128, u, WPIX:PIX].rearrange("c (j p) -> c j p", p=CPX), chunk[64:128, 1:CHUNKS, :]
                             ).then_inc(s_x[u], 16)
                for two in range(2):
                    sp.dma_start(x3[64 * two:64 * two + 64, u, :],
                                 x3_dram[bass.ds(b, 1)].rearrange("a (r two) p -> two r (a p)", two=2)[two]
                                 ).then_inc(s_x[u], 16)

            images(sp, body)

        @block.gpsimd
        def _(pool):
            for x in sems:
                pool.sem_inc(x, ONE)
            pool.sem_inc(s_res, FREE)
            for x in s_out:
                pool.sem_inc(x, 32)

        @block.tensor
        def _(pe):
            pe.wait_ge(s_w, ONE + 16 * N_W)

            def body(b, q, g, u):
                pe.wait_ge(s_st, ONE + STATS * (b + 1))
                nc.tensor.matmul(red[u][:, :], group[:, :], mv[:, u], start=True, stop=True).then_inc(s_red, 1)

            images(pe, body)

        @block.scalar
        def _(act):
            act.wait_ge(s_w, ONE + 16 * N_W)

            def store(b, u):
                act.wait_ge(s_res, ONE + FREE + b + 1)
                for two in range(2):
                    act.dma_start(out[bass.ds(b, 1)].rearrange("a (r two) p -> two r (a p)", two=2)[two],
                                  res[64 * two:64 * two + 64, u, :]).then_inc(s_out[u], 16)

            def body(b, q, g, u):
                act.preload_act_table_set("natural_log_exp_and_others")
                act.wait_ge(s_m, ONE + 2 * b + 2)
                nc.scalar.activation(rs[:, u], var[:, u], ACT.Ln, bias=eps[:, 0:1], scale=-1.0).then_inc(s_ln, 1)
                act.wait_ge(s_ln, ONE + 2 * b + 1)
                nc.scalar.activation(rs[:, u], rs[:, u], ACT.Exp, scale=-0.5).then_inc(s_ln, 1)
                act.wait_ge(s_sc, ONE + 3 * b + 3)
                act.wait_ge(s_out[u], ONE + 32 * (2 * q + g // 2 + 1))
                nc.scalar.activation(res[:, u, :], xr[:, u, :], ACT.Silu, bias=shift[:, u], scale=sc[:, u]
                                     ).then_inc(s_act, 1)
                store(b, u)

            images(act, body)
            for x in s_out:
                act.wait_ge(x, ONE + 32 + 32 * IMGS // 2)

        @block.vector
        def _(dve):
            dve.wait_ge(s_w, ONE + 16 * N_W)
            nc.vector.memset(eps[:, :], EPS_GN)

            def body(b, q, g, u):
                dve.wait_ge(s_x[u], ONE + 16 * LOADS * (2 * q + g // 2 + 1))
                for j in range(7):
                    nc.vector.bn_stats(out=stats[:, u, j, :], in_=xr[:, u, STRIP * j:STRIP * (j + 1)]
                                       ).then_inc(s_st, 1)
                dve.wait_ge(s_st, ONE + STATS * b + 7)
                dve.sem_inc(s_gate, 1)
                nc.vector.bn_aggr(out=mv[:, u], in_=stats[:, u].rearrange("c j k -> c (j k)")).then_inc(s_st, 1)
                dve.wait_ge(s_st, ONE + STATS * b + 8)
                nc.vector.scalar_tensor_tensor(out=mv[:, u, 1:2], in0=mv[:, u, 0:1], scalar=mv[:, u, 0:1],
                                               in1=mv[:, u, 1:2], op0=ALU.mult, op1=ALU.add).then_inc(s_st, 1)
                dve.wait_ge(s_red, ONE + b + 1)
                nc.vector.tensor_copy(msq[:, u], red[u][:, :]).then_inc(s_m, 1)
                dve.wait_ge(s_m, ONE + 2 * b + 1)
                nc.vector.scalar_tensor_tensor(out=var[:, u], in0=msq[:, u, 0:1], scalar=msq[:, u, 0:1],
                                               in1=msq[:, u, 1:2], op0=ALU.mult, op1=ALU.subtract,
                                               ).then_inc(s_m, 1)
                dve.wait_ge(s_ln, ONE + 2 * b + 2)
                nc.vector.tensor_tensor(out=sc[:, u], in0=rs[:, u], in1=v("gn_w"), op=ALU.mult).then_inc(s_sc, 1)
                dve.wait_ge(s_sc, ONE + 3 * b + 1)
                nc.vector.tensor_tensor(out=shift[:, u], in0=msq[:, u, 0:1], in1=sc[:, u], op=ALU.mult
                                        ).then_inc(s_sc, 1)
                dve.wait_ge(s_sc, ONE + 3 * b + 2)
                nc.vector.tensor_tensor(out=shift[:, u], in0=v("gn_b"), in1=shift[:, u], op=ALU.subtract
                                        ).then_inc(s_sc, 1)
                dve.wait_ge(s_act, ONE + b + 1)
                nc.vector.tensor_tensor(out=res[:, u, :], in0=res[:, u, :], in1=x3[:, u, :], op=ALU.add
                                        ).then_inc(s_res, 1)

            images(dve, body)


TAP_PAIRS = ((0, 1), (2, 3), (None, 0), (1, 2), (3, None))


def program(nc, d, out):
    x3_dram = nc.dram_tensor("x3", (IMGS, C, PIX), FP32).ap()
    ys_dram = nc.dram_tensor("ys", (NB, CHUNKS, C, G, CPX), FP32).ap()
    xr_dram = nc.dram_tensor("xr", (NB * CHUNKS, C, G, CPX), FP32).ap()
    layer0(nc, d, x3_dram, ys_dram)
    sequences(nc, d, ys_dram.rearrange("q j c g p -> (q j) c g p"), xr_dram)
    normalise(nc, d, x3_dram, xr_dram, out.rearrange("b c h w -> b c (h w)"))


def kernel(**inputs):
    import numpy as np
    import concourse.bacc as bacc
    from concourse.bass_utils import run_bass_kernel_spmd as run

    a = {n: np.asarray(x) for n, x in inputs.items()}
    f32 = np.float32
    even_odd = np.r_[0:C:2, 1:C:2]
    L0, L1 = "L0_conv_", "L1_conv_"

    cols = {
        "pos_w": a[L0 + "pos_w"].reshape(C, 9), "pos_b": a[L0 + "pos_b"].reshape(C, 1),
        "g1": a[L0 + "ln1_g"].reshape(C, 1), "b1": a[L0 + "ln1_b"].reshape(C, 1),
        "qkv_b": a[L0 + "qkv_b"].reshape(3, C).T,
        "lepe_w": a[L0 + "lepe_w"].reshape(C, 25), "lepe_b": a[L0 + "lepe_b"].reshape(C, 1),
        "wo_b": a[L0 + "wo_b"].reshape(C, 1), "g2": a[L0 + "ln2_g"].reshape(C, 1), "b2": a[L0 + "ln2_b"].reshape(C, 1),
        "mb1": a[L0 + "mlp_b1"].reshape(MLP, C).T, "mb2": a[L0 + "mlp_b2"].reshape(C, 1),
        "conv_b": a[L1 + "conv_b"][even_odd].reshape(C, 1),
        "gn_w": a[L1 + "gn_w"][even_odd].reshape(C, 1), "gn_b": a[L1 + "gn_b"][even_odd].reshape(C, 1),
        "c1b": np.tile(a[L1 + "conv1d_b"], G).reshape(C, 1), "dtb": np.tile(a[L1 + "dt_proj_b"], G).reshape(C, 1),
        "D": np.tile(a[L1 + "D"], G).reshape(C, 1), "alog": np.tile(a[L1 + "A_log"], (G, 1)),
        "headmask": np.where(np.arange(C)[:, None] // HD == np.arange(HEADS)[None, :], SCALE, 0.0).astype(f32),
        "rowmask": (np.arange(C)[:, None] // WPIX == np.arange(2)[None, :]).astype(f32),
    }
    vecs = np.concatenate([cols[n] for n in _V], axis=1)
    w_in = a[L1 + "in_proj_w"]
    wx, wz = np.zeros((2, G, K, G, DI), f32), np.zeros((2, G, K, G, DI), f32)
    taps = np.zeros((5, 2, G, K, G, DI), f32)
    x_proj = a[L1 + "x_proj_w"]
    xp_dt, dt_w = np.zeros((G, DI, G, DI), f32), np.zeros((G, DI, G, DI), f32)
    xp_bc = np.zeros((G, DI, 4, G, HALF), f32)
    w_out = np.zeros((G, DI, G, K), f32)
    pick = np.zeros((3, G, HALF, HALF, G, DI), f32)
    cw = a[L1 + "conv1d_w"][:, 0, :]
    for g in range(G):
        for blk in range(2):
            wx[blk, g, :, g, :] = w_in[0:DI].T
            wz[blk, g, :, g, :] = w_in[DI:2 * DI].T
        for m, pair in enumerate(TAP_PAIRS):
            for blk in range(2):
                if pair[blk] is not None:
                    taps[m, blk, g, :, g, :] = cw[:, pair[blk]][None, :]
        xp_dt[g, :, g, :] = x_proj[0][:, None]
        dt_w[g, :, g, :] = a[L1 + "dt_proj_w"][:, 0][None, :]
        for m in range(4):
            at = 1 + NS * (m // 2) + HALF * (m % 2)
            xp_bc[g, :, m, g, :] = x_proj[at:at + HALF].T
        w_out[g, :, g, :] = a[L1 + "out_proj_w"].T
        for n in range(HALF):
            pick[:, g, n, n, g, :] = 1.0
    eye = np.eye(C, dtype=f32)
    rows = np.arange(C) % 64 // 16
    data = {
        "x": a["x"], "vecs": vecs, "ident": eye,
        "centre": (eye - f32(1.0 / C)).astype(f32), "mean": np.full((C, C), 1.0 / C, f32),
        "fold": np.concatenate([np.eye(WPIX, dtype=f32)] * 2, axis=0),
        "qkv_w": a[L0 + "qkv_w"], "wo_w": a[L0 + "wo_w"], "mlp_w1": a[L0 + "mlp_w1"], "mlp_w2": a[L0 + "mlp_w2"],
        "conv_w": np.transpose(a[L1 + "conv_w"], (1, 2, 3, 0)).reshape(C, 9, C)[:, :, even_odd],
        "wx": wx.reshape(C, C), "wz": wz.reshape(C, C), "taps": np.transpose(taps.reshape(5, C, C), (1, 0, 2)),
        "xp_dt": xp_dt.reshape(C, C), "dt_w": dt_w.reshape(C, C), "xp_bc": xp_bc.reshape(C, C),
        "w_out": w_out.reshape(C, G * K), "pick": pick.reshape(3 * G * HALF, HALF * C),
        "group": ((rows[:, None] == rows[None, :]) / 32.0).astype(f32),
    }
    nc = bacc.Bacc("TRN2", target_bir_lowering=False, num_devices=1)
    d, arrays = {}, {}
    for name, x in data.items():
        x = np.ascontiguousarray(x)
        arrays[f"in_{name}"] = x
        d[name] = nc.dram_tensor(f"in_{name}", x.shape, mybir.dt.from_np(x.dtype), kind="ExternalInput").ap()
    out = nc.dram_tensor("out", (IMGS, C, H, W), FP32, kind="ExternalOutput").ap()
    program(nc, d, out)
    return run(nc, [arrays], core_ids=[0]).results[0]["out"]
```
